# Optimizing a Trainium2 kernel written in Bass

```python
import numpy as np
import jax
import jax.numpy as jnp

def _softmax(x, axis=-1):
    return jax.nn.softmax(x, axis=axis)

def _gelu(x):
    return jax.nn.gelu(x, approximate=True)

def _silu(x):
    return jax.nn.silu(x)

def _sigmoid(x):
    return jax.nn.sigmoid(x)

def _layernorm(x, axis=-1, eps=1e-05):
    m = jnp.mean(x, axis=axis, keepdims=True)
    v = jnp.var(x, axis=axis, keepdims=True)
    return (x - m) / jnp.sqrt(v + eps)

def _scatter_add(tgt, idx, src, axis=0):
    return tgt.at[idx].add(src)

def _segment_sum(src, seg, n):
    return jax.ops.segment_sum(src, seg, n)
kernel_name = 'mk_vit_tower_d1_tok_img512_r4_1a7c7f'

def setup_inputs(seed: int=0):
    np.random.seed(seed)
    _w = jnp.asarray

    def _rec_inputs():
        import jax
        import jax.numpy as jnp
        _rk = jax.random.key(seed)
        x = -0.000392918 + 0.999932 * jax.random.normal(jax.random.fold_in(_rk, 1), (32, 1, 128, 128), jnp.float32)
        return x
    x = _rec_inputs()

    def _L0_tok_setup():
        import math
        import jax, jax.numpy as jnp
        import numpy as np
        PW = PH = 16
        EMB = 128
        HID = 128
        B, H, W = (64, 128, 128)
        L = H // PW * (W // PH)
        SIGMA_ZERO = 0.1

        def _f_noise(x):
            return jnp.sign(x) * jnp.sqrt(jnp.abs(x))

        def _noisy_linear(x, w, b, sw, sb, eps_in, eps_out):
            ei = _f_noise(eps_in)
            eo = _f_noise(eps_out)
            w_n = w + sw * (eo[:, None] * ei[None, :])
            b_n = b + sb * eo
            return x @ w_n.T + b_n

        def _unfold_patches(x):
            b = x.shape[0]
            p = x.reshape(b, H // PW, PW, W // PH, PH)
            p = p.transpose(0, 1, 3, 2, 4)
            return p.reshape(b, L, PW * PH)

        def _pos_encoding(x):
            pos = jnp.arange(L, dtype=jnp.float32)[:, None]
            div = jnp.exp(jnp.arange(0, EMB, 2, dtype=jnp.float32) * (-math.log(10000.0) / EMB))
            ang = pos * div
            pe = jnp.stack([jnp.sin(ang), jnp.cos(ang)], axis=-1).reshape(L, EMB)
            return x + pe[None, :, :]
        key = jax.random.key(seed)
        ks = jax.random.split(key, 12)
        in_f = PW * PH
        sig = SIGMA_ZERO / math.sqrt(in_f)
        bnd1 = 1.0 / math.sqrt(in_f)
        bnd3 = 1.0 / math.sqrt(HID)
        u = lambda k, shape, bnd: jax.random.uniform(k, shape, jnp.float32, -bnd, bnd)
        return {'inputs': jax.random.normal(ks[0], (B, 1, H, W), jnp.float32), 'W1_w': u(ks[1], (HID, in_f), bnd1), 'W1_b': u(ks[2], (HID,), bnd1), 'W1_sw': jnp.full((HID, in_f), sig, jnp.float32), 'W1_sb': jnp.full((HID,), sig, jnp.float32), 'W2_w': u(ks[3], (HID, in_f), bnd1), 'W2_b': u(ks[4], (HID,), bnd1), 'W2_sw': jnp.full((HID, in_f), sig, jnp.float32), 'W2_sb': jnp.full((HID,), sig, jnp.float32), 'W3_w': u(ks[5], (EMB, HID), bnd3), 'W3_b': u(ks[6], (EMB,), bnd3), 'eps_in1': jax.random.normal(ks[7], (in_f,), jnp.float32), 'eps_out1': jax.random.normal(ks[8], (HID,), jnp.float32), 'eps_in2': jax.random.normal(ks[9], (in_f,), jnp.float32), 'eps_out2': jax.random.normal(ks[10], (HID,), jnp.float32)}
    _L0_tok_all = _L0_tok_setup()
    _L0_tok_in = {k: v for k, v in _L0_tok_all.items() if k in ('W1_w', 'W1_b', 'W1_sw', 'W1_sb', 'W2_w', 'W2_b', 'W2_sw', 'W2_sb', 'W3_w', 'W3_b', 'eps_in1', 'eps_out1', 'eps_in2', 'eps_out2')}
    del _L0_tok_all

    def _L0_attn_setup():
        import jax, jax.numpy as jnp
        import numpy as np
        INNER_DIM = 64
        HEAD_NUM = 8
        D_MODEL = 128
        key = jax.random.key(seed)
        k1, k2, k3 = jax.random.split(key, 3)
        x = jax.random.normal(k1, (4, 512, D_MODEL), dtype=jnp.float32)
        kernel = jax.random.uniform(k2, (3 * HEAD_NUM, D_MODEL, INNER_DIM), dtype=jnp.float32, minval=-0.05, maxval=0.05)
        head_kernel = jax.random.uniform(k3, (INNER_DIM * HEAD_NUM, D_MODEL), dtype=jnp.float32, minval=-0.05, maxval=0.05)
        return {'x': x, 'kernel': kernel, 'head_kernel': head_kernel}
    _L0_attn_all = _L0_attn_setup()
    _L0_attn_in = {k: v for k, v in _L0_attn_all.items() if k in ('kernel', 'head_kernel')}
    del _L0_attn_all

    def _L0_ffn_setup():
        import jax, jax.numpy as jnp
        import numpy as np
        D = 128
        E = 8
        K = 2
        EXP = 4
        LN_EPS = 1e-05
        key = jax.random.key(seed)
        ks = jax.random.split(key, 8)
        B, T = (8, 512)
        Dh = D * EXP
        x = jax.random.normal(ks[0], (B, T, D), dtype=jnp.float32)
        ln_g = jnp.ones((D,), dtype=jnp.float32)
        ln_b = jnp.zeros((D,), dtype=jnp.float32)
        lim_r = np.sqrt(6.0 / (D + E)).astype(np.float32)
        w_r = jax.random.uniform(ks[1], (E, D), dtype=jnp.float32, minval=-lim_r, maxval=lim_r)
        b_r = jnp.zeros((E,), dtype=jnp.float32)
        lim1 = np.sqrt(6.0 / (D + Dh)).astype(np.float32)
        W1 = jax.random.uniform(ks[2], (E, D, Dh), dtype=jnp.float32, minval=-lim1, maxval=lim1)
        b1 = jnp.zeros((E, Dh), dtype=jnp.float32)
        W2 = jax.random.uniform(ks[3], (E, Dh, D), dtype=jnp.float32, minval=-lim1, maxval=lim1)
        b2 = jnp.zeros((E, D), dtype=jnp.float32)
        return {'x': x, 'ln_g': ln_g, 'ln_b': ln_b, 'w_r': w_r, 'b_r': b_r, 'W1': W1, 'b1': b1, 'W2': W2, 'b2': b2}
    _L0_ffn_all = _L0_ffn_setup()
    _L0_ffn_in = {k: v for k, v in _L0_ffn_all.items() if k in ('ln_g', 'ln_b', 'w_r', 'b_r', 'W1', 'b1', 'W2', 'b2')}
    del _L0_ffn_all
    return {'x': x, 'L0_tok_W1_w': _L0_tok_in['W1_w'], 'L0_tok_W1_b': _L0_tok_in['W1_b'], 'L0_tok_W1_sw': _L0_tok_in['W1_sw'], 'L0_tok_W1_sb': _L0_tok_in['W1_sb'], 'L0_tok_W2_w': _L0_tok_in['W2_w'], 'L0_tok_W2_b': _L0_tok_in['W2_b'], 'L0_tok_W2_sw': _L0_tok_in['W2_sw'], 'L0_tok_W2_sb': _L0_tok_in['W2_sb'], 'L0_tok_W3_w': _L0_tok_in['W3_w'], 'L0_tok_W3_b': _L0_tok_in['W3_b'], 'L0_tok_eps_in1': _L0_tok_in['eps_in1'], 'L0_tok_eps_out1': _L0_tok_in['eps_out1'], 'L0_tok_eps_in2': _L0_tok_in['eps_in2'], 'L0_tok_eps_out2': _L0_tok_in['eps_out2'], 'L0_attn_kernel': _L0_attn_in['kernel'], 'L0_attn_head_kernel': _L0_attn_in['head_kernel'], 'L0_ffn_ln_g': _L0_ffn_in['ln_g'], 'L0_ffn_ln_b': _L0_ffn_in['ln_b'], 'L0_ffn_w_r': _L0_ffn_in['w_r'], 'L0_ffn_b_r': _L0_ffn_in['b_r'], 'L0_ffn_W1': _L0_ffn_in['W1'], 'L0_ffn_b1': _L0_ffn_in['b1'], 'L0_ffn_W2': _L0_ffn_in['W2'], 'L0_ffn_b2': _L0_ffn_in['b2']}

def reference(x, L0_tok_W1_w, L0_tok_W1_b, L0_tok_W1_sw, L0_tok_W1_sb, L0_tok_W2_w, L0_tok_W2_b, L0_tok_W2_sw, L0_tok_W2_sb, L0_tok_W3_w, L0_tok_W3_b, L0_tok_eps_in1, L0_tok_eps_out1, L0_tok_eps_in2, L0_tok_eps_out2, L0_attn_kernel, L0_attn_head_kernel, L0_ffn_ln_g, L0_ffn_ln_b, L0_ffn_w_r, L0_ffn_b_r, L0_ffn_W1, L0_ffn_b1, L0_ffn_W2, L0_ffn_b2):
    import jax
    import jax.numpy as jnp

    def _L0_tok_ref(inputs, W1_w, W1_b, W1_sw, W1_sb, W2_w, W2_b, W2_sw, W2_sb, W3_w, W3_b, eps_in1, eps_out1, eps_in2, eps_out2):
        import math
        import jax, jax.numpy as jnp
        import numpy as np
        PW = PH = 16
        EMB = 128
        HID = 128
        B, H, W = (64, 128, 128)
        L = H // PW * (W // PH)
        SIGMA_ZERO = 0.1

        def _f_noise(x):
            return jnp.sign(x) * jnp.sqrt(jnp.abs(x))

        def _noisy_linear(x, w, b, sw, sb, eps_in, eps_out):
            ei = _f_noise(eps_in)
            eo = _f_noise(eps_out)
            w_n = w + sw * (eo[:, None] * ei[None, :])
            b_n = b + sb * eo
            return x @ w_n.T + b_n

        def _unfold_patches(x):
            b = x.shape[0]
            p = x.reshape(b, H // PW, PW, W // PH, PH)
            p = p.transpose(0, 1, 3, 2, 4)
            return p.reshape(b, L, PW * PH)

        def _pos_encoding(x):
            pos = jnp.arange(L, dtype=jnp.float32)[:, None]
            div = jnp.exp(jnp.arange(0, EMB, 2, dtype=jnp.float32) * (-math.log(10000.0) / EMB))
            ang = pos * div
            pe = jnp.stack([jnp.sin(ang), jnp.cos(ang)], axis=-1).reshape(L, EMB)
            return x + pe[None, :, :]
        x = _unfold_patches(inputs)
        g = _noisy_linear(x, W1_w, W1_b, W1_sw, W1_sb, eps_in1, eps_out1)
        x_gate = g * jnp.tanh(jax.nn.softplus(g))
        x_inner = _noisy_linear(x, W2_w, W2_b, W2_sw, W2_sb, eps_in2, eps_out2)
        x = x_gate * x_inner
        x = x @ W3_w.T + W3_b
        return _pos_encoding(x)

    def _L0_attn_ref(x, kernel, head_kernel):
        import jax, jax.numpy as jnp
        import numpy as np
        INNER_DIM = 64
        HEAD_NUM = 8
        D_MODEL = 128
        H, K = (HEAD_NUM, INNER_DIM)
        w = kernel.reshape(H, 3, kernel.shape[1], K)
        wq, wk, wv = (w[:, 0], w[:, 1], w[:, 2])
        q = jnp.einsum('bsd,hdk->bhsk', x, wq)
        k = jnp.einsum('bsd,hdk->bhsk', x, wk)
        v = jnp.einsum('bsd,hdk->bhsk', x, wv)
        scores = jnp.einsum('bhsk,bhtk->bhst', q, k) / jnp.sqrt(jnp.asarray(K, x.dtype))
        probs = jax.nn.softmax(scores, axis=-1)
        o = jnp.einsum('bhst,bhtk->bhsk', probs, v)
        B, _, S, _ = o.shape
        concated = jnp.transpose(o, (0, 2, 1, 3)).reshape(B, S, H * K)
        return jnp.einsum('bse,ed->bsd', concated, head_kernel)

    def _L0_ffn_ref(x, ln_g, ln_b, w_r, b_r, W1, b1, W2, b2):
        import jax, jax.numpy as jnp
        import numpy as np
        D = 128
        E = 8
        K = 2
        EXP = 4
        LN_EPS = 1e-05
        B, T, d = x.shape
        mu = jnp.mean(x, axis=-1, keepdims=True)
        var = jnp.mean(jnp.square(x - mu), axis=-1, keepdims=True)
        h = (x - mu) * jax.lax.rsqrt(var + LN_EPS) * ln_g + ln_b
        logits = jnp.einsum('btd,ed->bte', h, w_r) + b_r
        topk_vals, topk_idx = jax.lax.top_k(logits, K)
        gates = jax.nn.softmax(topk_vals, axis=-1)
        hf = h.reshape(B * T, d)
        hid = jax.nn.gelu(jnp.einsum('nd,edf->nef', hf, W1) + b1, approximate=False)
        expert_stack = jnp.einsum('nef,efd->ned', hid, W2) + b2
        idx_flat = topk_idx.reshape(B * T, K)
        gates_flat = gates.reshape(B * T, K)
        gathered = jnp.take_along_axis(expert_stack, idx_flat[:, :, None], axis=1)
        mixed = jnp.sum(gathered * gates_flat[:, :, None], axis=1).reshape(B, T, d)
        return x + mixed
    h = _L0_tok_ref(x, L0_tok_W1_w, L0_tok_W1_b, L0_tok_W1_sw, L0_tok_W1_sb, L0_tok_W2_w, L0_tok_W2_b, L0_tok_W2_sw, L0_tok_W2_sb, L0_tok_W3_w, L0_tok_W3_b, L0_tok_eps_in1, L0_tok_eps_out1, L0_tok_eps_in2, L0_tok_eps_out2)
    h = h + _L0_attn_ref(_layernorm(h, axis=-1), L0_attn_kernel, L0_attn_head_kernel)
    h = h + _L0_ffn_ref(_layernorm(h, axis=-1), L0_ffn_ln_g, L0_ffn_ln_b, L0_ffn_w_r, L0_ffn_b_r, L0_ffn_W1, L0_ffn_b1, L0_ffn_W2, L0_ffn_b2)
    return h

_drawn_inputs = setup_inputs


def setup_inputs(seed=0):
    import zlib

    import numpy as np

    out = dict(_drawn_inputs(seed))
    spreads = {'L0_tok_W1_sw': (0.0062500000931322575, 0.6),
     'L0_tok_W1_sb': (0.0062500000931322575, 0.6),
     'L0_tok_W2_sw': (0.0062500000931322575, 0.6),
     'L0_tok_W2_sb': (0.0062500000931322575, 0.6),
     'L0_ffn_ln_g': (1.0, 0.2),
     'L0_ffn_ln_b': (0.0, 0.1),
     'L0_ffn_b_r': (0.0, 0.303),
     'L0_ffn_b1': (0.0, 0.1),
     'L0_ffn_b2': (0.0, 0.1)}
    factors = {'L0_tok_W1_b': 3.312, 'L0_tok_W2_b': 3.449}
    for name, (base, spread) in spreads.items():
        noise = np.random.default_rng([zlib.crc32(name.encode()), seed]).standard_normal(out[name].shape)
        drawn = base * np.exp(spread * noise) if base else spread * noise
        out[name] = jnp.asarray(drawn.astype(out[name].dtype))
    for name, factor in factors.items():
        out[name] = (out[name] * factor).astype(out[name].dtype)
    return out
```

```python
from contextlib import ExitStack

import concourse.bass as bass
from concourse import mybir

F32 = mybir.dt.float32
BF16 = mybir.dt.bfloat16
I32 = mybir.dt.int32
U32 = mybir.dt.uint32
ALU = mybir.AluOpType
ACT = mybir.ActivationFunctionType
AX_X = mybir.AxisListType.X

P = 128
IMAGES, SIDE, PATCH = 32, 128, 16
L = (SIDE // PATCH) ** 2
D = 128
PIX = PATCH * PATCH
NTOK = IMAGES * L
HEADS, HD = 8, 64
PAIRS = HEADS // 2
EXPERTS, HID = 8, 512
FC = HID // P
GROUP = 256
GROUPS = NTOK // GROUP
TILES = GROUP // P
IPG = GROUP // L
IPT = P // L
BANK = 512
EPS = 1e-5
ROWLEN = D + 1
EXPERT_TILE = 256
REGION = NTOK + EXPERT_TILE
TAIL_ROWS = EXPERTS * EXPERT_TILE

C_IDENT = 0
C_UPPER = C_IDENT + P
C_POS = C_UPPER + P
C_IOTA = C_POS + D
C_EBASE = C_IOTA + TILES * EXPERTS
C_DEST = C_EBASE + TILES * EXPERTS
C_STEP = C_DEST + 2 * TILES
C_LOWER = C_STEP + EXPERTS
C_TAIL = C_LOWER + EXPERTS * EXPERTS
C_END = C_TAIL + EXPERTS * 2

V_ROUTER = 0
V_B1 = V_ROUTER + EXPERTS
V_TOK = V_B1 + EXPERTS * FC
V_ROWS = V_TOK + 6


def constants():
    import math
    import numpy as np

    c = np.zeros((P, C_END), np.float32)
    p = np.arange(P)
    c[:, C_IDENT:C_IDENT + P] = np.eye(P)
    c[:, C_UPPER:C_UPPER + P] = p[:, None] < p[None, :]
    pos = np.arange(L, dtype=np.float32)[:, None]
    div = np.exp(np.arange(0, D, 2, dtype=np.float32) * np.float32(-math.log(10000.0) / D))
    angle = (pos * div).astype(np.float32)
    table = np.stack([np.sin(angle), np.cos(angle)], axis=-1).reshape(L, D)
    c[:, C_POS:C_POS + D] = np.concatenate([table] * IPT)
    c[:, C_IOTA:C_EBASE] = np.tile(np.arange(EXPERTS), TILES)
    c[:, C_EBASE:C_DEST] = np.tile(np.arange(EXPERTS) * REGION, TILES)
    for k in range(2):
        for i in range(TILES):
            c[:, C_DEST + k * TILES + i] = p + i * P + k * NTOK
    c[:, C_STEP:C_LOWER] = np.arange(EXPERTS) * EXPERT_TILE
    c[:, C_LOWER:C_TAIL] = (np.arange(EXPERTS)[None, :] < np.arange(EXPERTS)[:, None]).reshape(-1)
    for e in range(EXPERTS):
        for r in range(2):
            c[:, C_TAIL + 2 * e + r] = 2 * NTOK + e * EXPERT_TILE + 2 * p + r
    return c


def vit_tower(nc, x, W1_w, W1_b, W1_sw, W1_sb, W2_w, W2_b, W2_sw, W2_sb, W3_w, W3_b,
              eps_in1, eps_out1, eps_in2, eps_out2, attn_kernel, head_kernel, ln_g, ln_b,
              w_r, b_r, E_W1, E_b1, E_W2, E_b2, consts, out):
    rows_dram = nc.dram_tensor("expert_rows", [EXPERTS * REGION, ROWLEN], F32, kind="Internal").ap()
    mixed_dram = nc.dram_tensor("chosen_rows", [2 * NTOK + TAIL_ROWS, D], F32, kind="Internal").ap()

    ctx = ExitStack()
    with ctx:
        def sb(name, shape, dt=F32):
            return ctx.enter_context(nc.sbuf_tensor(name, shape, dt))

        def sem(name):
            return ctx.enter_context(nc.semaphore(name))

        cst = sb("cst", [P, C_END])
        ident = cst[:, C_IDENT:C_IDENT + P]
        upper = sb("upper", [P, P], BF16)
        ones = sb("ones", [P, P], BF16)
        vrows = sb("vrows", [V_ROWS, P])
        vcols = sb("vcols", [P, V_ROWS])
        bias_tok = sb("bias_tok", [P, 2])
        bias_t = sb("bias_t", [P, 2])
        w_tok = sb("w_tok", [P, 2, PIX])
        sw_tok = sb("sw_tok", [P, 2, PIX])
        noise_in = sb("noise_in", [P, 2, PIX])
        noise_abs = sb("noise_abs", [P, 2, PIX])
        noise_sgn = sb("noise_sgn", [P, 2, PIX])
        eo_abs = sb("eo_abs", [P, 2])
        eo_sgn = sb("eo_sgn", [P, 2])
        eo = sb("eo", [P, 2])
        w_tokT = sb("w_tokT", [P, 2, 2, P])
        w3 = sb("w3", [P, P])
        w3T = sb("w3T", [P, P])
        pos_b3 = sb("pos_b3", [P, D])
        b3_row = sb("b3_row", [P, D])
        ak = sb("ak", [P, 3, HEADS, HD])
        wqT = sb("wqT", [P, PAIRS, D])
        wkT = sb("wkT", [P, PAIRS, D])
        qkT = sb("qkT", [P, HEADS, D])
        wo = sb("wo", [P, PAIRS, D])
        g_row = sb("g_row", [P, D])
        b_row = sb("b_row", [P, D])
        br_row = sb("br_row", [P, EXPERTS])
        ew1 = sb("ew1", [P, EXPERTS, HID])
        ew2 = sb("ew2", [P, EXPERTS, FC, D])
        b2_row = sb("b2_row", [P, EXPERTS, D])
        tail = sb("tail", [P, EXPERTS, 2, ROWLEN])

        xrow = sb("xrow", [P, 2, PATCH * SIDE])
        xpatch = sb("xpatch", [P, 2, SIDE // PATCH, PIX])
        xT = sb("xT", [P, 2, NTOK])
        gpre = sb("gpre", [P, GROUP])
        gclip = sb("gclip", [P, GROUP])
        gexp = sb("gexp", [P, GROUP])
        gnum = sb("gnum", [P, GROUP])
        gden = sb("gden", [P, GROUP])
        gmul = sb("gmul", [P, GROUP])
        mT = sb("mT", [P, GROUP])
        h_all = sb("h_all", [P, GROUPS, TILES, D])
        st1 = sb("st1", [P, TILES, 6])
        mv1 = sb("mv1", [P, TILES, 2])
        ve1 = sb("ve1", [P, TILES])
        ln1 = sb("ln1", [P, TILES])
        r1 = sb("r1", [P, TILES])
        n1 = sb("n1", [P, TILES])
        rstd1 = sb("rstd1", [P, TILES])
        xn = sb("xn", [P, TILES, D])
        xnT = sb("xnT", [P, GROUP])
        zs = sb("zs", [P, IPG, HEADS, L])
        vs = sb("vs", [P, TILES, IPT, PAIRS, HD])
        smax = sb("smax", [P, TILES, HEADS])
        sx = sb("sx", [P, TILES, HEADS, L])
        ssum = sb("ssum", [P, TILES, HEADS])
        srec = sb("srec", [P, TILES, HEADS])
        prob = sb("prob", [P, TILES, HEADS, L])
        probT = sb("probT", [P, TILES, PAIRS, P])
        oT = sb("oT", [P, TILES, PAIRS, P])
        st2 = sb("st2", [P, TILES, 6])
        mv2 = sb("mv2", [P, TILES, 2])
        ve2 = sb("ve2", [P, 2, TILES])
        ln2 = sb("ln2", [P, 2, TILES])
        r2 = sb("r2", [P, 2, TILES])
        n2 = sb("n2", [P, 2, TILES])
        rstd2 = sb("rstd2", [P, 2, TILES])
        y = sb("y", [P, TILES, D])
        hh = sb("hh", [P, TILES, D])
        hg = sb("hg", [P, TILES, D])
        dest = sb("dest", [P, 2, TILES])
        send = [sb(f"send{k}", [P, TILES, ROWLEN]) for k in range(2)]
        hfT = sb("hfT", [P, TILES, P])
        lg = sb("lg", [P, TILES, EXPERTS])
        top = sb("top", [P, TILES, 8])
        topi = sb("topi", [P, TILES, 8], U32)
        topf = sb("topf", [P, TILES, 2])
        diff = sb("diff", [P, TILES])
        ediff = sb("ediff", [P, TILES])
        eone = sb("eone", [P, TILES])
        onehot = sb("onehot", [P, 2, TILES, EXPERTS])
        picks = sb("picks", [P, TILES, EXPERTS], BF16)
        run = sb("run", [P, TILES + 1, EXPERTS], BF16)
        slot8 = sb("slot8", [P, TILES, EXPERTS])
        slotk = sb("slotk", [P, 2, TILES, EXPERTS])
        slotf = sb("slotf", [P, 2, TILES])
        slot = sb("slot", [P, 2 * TILES], U32)
        gates = sb("gates", [P, GROUPS, 2, TILES])

        cnt = sb("cnt", [P, EXPERTS])
        over = sb("over", [P, EXPERTS, EXPERTS])
        steps = sb("steps", [P, EXPERTS])
        before = sb("before", [P, EXPERTS, EXPERTS])
        start_f = sb("start_f", [P, EXPERTS])
        table = sb("table", [P, 3 * EXPERTS], I32)
        xe = [sb(f"xe{h}", [P, ROWLEN]) for h in range(2)]
        xeT = sb("xeT", [P, EXPERT_TILE])
        hid = sb("hid", [P, FC, EXPERT_TILE])
        idx_next = sb("idx_next", [P, 2], U32)
        idx_now = sb("idx_now", [P, 2], U32)
        ye = [sb(f"ye{h}", [P, D]) for h in range(2)]
        first = sb("first", [P, NTOK // P, D])
        second = sb("second", [P, NTOK // P, D])

        ps = ctx.enter_context(nc.psum_tensor("ps", [P, 8, BANK], F32))
        S_BANK, V_BANK, PT_BANK, O_BANK, Z_BANK, N_BANK = 0, 2, 3, 4, 5, 7
        HID_BANKS = (0, 1, 5, 6)

        names = """cst_in vec_in tok_in noise_w_in w3_in b3_in x_in0 x_in1 ak_in wo_in rows_in ew_in
            vcols_p qk_p qkT_ready wtok_p xpatch_a xpatch_v xT_p xT_a xT_v w_noise w_chain bf_ready
            noise_a posb tail_ready run0 qkT_p qkTs w3T_ready vcols_ready wtokT_ready
            embed_p mish_step exp_ready mT_ready w3_p ln1_step ln1_ln ln1_guess xn_ready xnT_p xnT_ready
            z_p z_act z_dve s_p v_p vs_ready soft_max soft_sub soft_sum soft_rec e_ready prob_ready pt_p probT_ready pv_p
            o_ready wo_p h1_ready hy_ready ln2_step ln2_ln ln2_guess send_step send_ready hft_p hfT_ready
            lg_p route_step route_exp rank_p slot_ready scattered
            count_p count_step start_ready tail_out xe_in0 xe_in1 xe_free xet_p xeT_ready hid_p
            hid_ready y_p ye_ready idx_step idx_ready y_out ye_free y_step fin_in0 fin_in1 fin_in2 fin_in3 mix_step out_done passed""".split()
        s = {n: sem(n) for n in names}

        def wait(eng, name, g, per=1, k=0):
            if isinstance(g, int) and g < 0:
                return
            eng.wait_ge(s[name], g * per + k + 1)

        MISH, LN1, LN2, ROUTE = 7, 9, 11, 19

        def counts(eng, e):
            if e == 0:
                eng.wait_ge(s["count_step"], 8)
            c = eng.value_load(table[0:1, EXPERTS + e:EXPERTS + e + 1], min_val=1, max_val=EXPERTS)
            t = eng.value_load(table[0:1, 2 * EXPERTS + e:2 * EXPERTS + e + 1], min_val=0, max_val=3 * EXPERTS)
            return c, t

        def apart(eng):
            eng.sem_inc(s["passed"])

        def patches_to(n):
            half, k, jq = n // 4, n // 2 % 2, n % 2
            v = xT[:, k, half * (NTOK // 2):(half + 1) * (NTOK // 2)].rearrange("p (b j) -> p j b", j=8)
            return v[:, 4 * jq:4 * jq + 4, :]

        def z_src(q):
            return ps[:, Z_BANK + q % 2, :].rearrange("p (h b t) -> p h b t", h=2, b=IPG)

        def z_dst(q):
            return zs[:, :, 2 * q:2 * q + 2, :].rearrange("p b h t -> p h b t")

        block = ctx.enter_context(nc.Block())

        @block.sync
        def _(sp):
            xr = x.rearrange("a c (i r) w -> (a c i) (r w)", r=PATCH)
            sp.dma_start(xrow[:, 0, :], xr[0:P, :]).then_inc(s["x_in0"], 16)
            sp.dma_start(xrow[:, 1, :], xr[P:2 * P, :]).then_inc(s["x_in1"], 16)
            av = attn_kernel.rearrange("(h s) d k -> s d h k", s=3)
            for q in range(3):
                sp.dma_start(ak[:, q, :, :], av[q]).then_inc(s["ak_in"], 16)
            sp.dma_start(wo[:], head_kernel.rearrange("(p e) d -> e p d", e=P)).then_inc(s["wo_in"], 16)
            sp.dma_start(g_row[:], ln_g.partition_broadcast(P)).then_inc(s["rows_in"], 16)
            sp.dma_start(b_row[:], ln_b.partition_broadcast(P)).then_inc(s["rows_in"], 16)
            sp.dma_start(br_row[:], b_r.partition_broadcast(P)).then_inc(s["rows_in"], 16)
            sp.dma_start(ew1[:], E_W1.rearrange("e d f -> d e f")).then_inc(s["ew_in"], 16)
            sp.dma_start(ew2[:], E_W2.rearrange("e (c f) d -> f e c d", f=P)).then_inc(s["ew_in"], 16)
            sp.dma_start(b2_row[:], E_b2.rearrange("e d -> (e d)").partition_broadcast(P)
                         .rearrange("p (e d) -> p e d", e=EXPERTS)).then_inc(s["ew_in"], 16)

            sp.wait_ge(s["count_step"], 8)
            sp.wait_ge(s["tail_ready"], 2)
            for e in range(EXPERTS):
                n = sp.value_load(table[0:1, e:e + 1], min_val=0, max_val=NTOK)
                dst = rows_dram[bass.ds(n + e * REGION, EXPERT_TILE), :]
                sp.dma_start(dst.rearrange("(p r) c -> p r c", r=2), tail[:, e, :, :]).then_inc(s["tail_out"], 16)

            def load_step(row):
                for h in range(2):
                    sp.dma_start(xe[h][:], rows_dram[bass.ds(row + h * P, P), :]).then_inc(s[f"xe_in{h}"], 16)

            sp.wait_ge(s["scattered"], 16 * GROUPS * 2 * TILES)
            sp.wait_ge(s["tail_out"], 16 * EXPERTS)
            for e in range(EXPERTS):
                c, t = counts(sp, e)
                with sp.Fori(0, c) as i:
                    sp.wait_ge(s["xe_free"], t + i + 1)
                    load_step(i * EXPERT_TILE + e * REGION)
            sp.wait_ge(s["xe_free"], t + c + 1)
            load_step(0)

            sp.wait_ge(s["y_out"], (t + c) * 32)
            ncol = 4
            mv_ = mixed_dram[0:2 * NTOK, :].rearrange("(k t p) d -> k p t d", k=2, p=P)
            for q in range(NTOK // P // ncol):
                cols = slice(ncol * q, ncol * q + ncol)
                sp.dma_start(first[:, cols, :], mv_[0][:, cols, :]).then_inc(s[f"fin_in{q}"], 16)
                sp.dma_start(second[:, cols, :], mv_[1][:, cols, :]).then_inc(s[f"fin_in{q}"], 16)
            ov = out.rearrange("a l d -> (a l) d").rearrange("(t p) d -> p t d", p=P)
            for q in range(NTOK // P // ncol):
                cols = slice(ncol * q, ncol * q + ncol)
                sp.wait_ge(s["mix_step"], 8 * (q + 1))
                sp.dma_start(ov[:, cols, :], first[:, cols, :]).then_inc(s["out_done"], 16)
            sp.wait_ge(s["out_done"], 16 * (NTOK // P // ncol))

        @block.gpsimd
        def _(pool):
            pool.memset(ones[:], 1.0).then_inc(s["bf_ready"], 1)
            pool.memset(run[:], 0.0).then_inc(s["run0"], 1)
            pool.memset(tail[:], 0.0).then_inc(s["tail_ready"], 1)
            pool.wait_ge(s["cst_in"], 16)
            pool.wait_ge(s["tail_ready"], 1)
            pool.tensor_copy(tail[:, :, :, D], cst[:, C_TAIL:C_END].rearrange("p (e r) -> p e r", r=2))\
                .then_inc(s["tail_ready"], 1)
            pool.tensor_copy(dest[:].rearrange("p k i -> p (k i)"), cst[:, C_DEST:C_STEP])\
                .then_inc(s["send_step"], 1)
            pool.wait_ge(s["rows_in"], 48)

            def probabilities(g, i):
                wait(pool, "e_ready", g, TILES, i)
                wait(pool, "soft_rec", g, TILES, i)
                wait(pool, "pt_p", g - 1, TILES, i)
                pool.tensor_tensor(prob[:, i, :, :], sx[:, i, :, :],
                                   srec[:, i, :].unsqueeze(2).broadcast_to([P, HEADS, L]), ALU.mult)\
                    .then_inc(s["prob_ready"], 1)

            def rows_to_send(g):
                wait(pool, "ln2_step", g, LN2, 10)
                pool.tensor_tensor(hg[:], hh[:], g_row[:].unsqueeze(1).broadcast_to([P, TILES, D]), ALU.mult)\
                    .then_inc(s["send_step"], 1)
                if not (isinstance(g, int) and g == 0):
                    pool.wait_ge(s["scattered"], g * (32 * TILES))
                wait(pool, "hft_p", g - 1)
                pool.wait_ge(s["send_step"], g * 4 + 1)
                apart(pool)
                for k in range(2):
                    pool.tensor_copy(send[k][:, :, D], dest[:, k, :]).then_inc(s["send_step"], 1)
                pool.wait_ge(s["send_step"], g * 4 + 2)
                pool.tensor_tensor(send[0][:, :, 0:D], hg[:], b_row[:].unsqueeze(1).broadcast_to([P, TILES, D]),
                                   ALU.add).then_inc(s["send_ready"], 1)
                pool.wait_ge(s["send_step"], g * 4 + 4)
                apart(pool)
                pool.tensor_scalar(dest[:], dest[:], float(GROUP), None, ALU.add).then_inc(s["send_step"], 1)

            def scatter(g):
                wait(pool, "slot_ready", g)
                wait(pool, "send_ready", g, 2, 1)
                pool.wait_ge(s["send_step"], g * 4 + 5)
                apart(pool)
                for k in range(2):
                    for i in range(TILES):
                        n = k * TILES + i
                        pool.indirect_dma_start(rows_dram, bass.IndirectOffsetOnAxis(ap=slot[:, n:n + 1], axis=0),
                                                send[k][:, i, :], None).then_inc(s["scattered"], 16)

            def body(g, last=False):
                for i in range(TILES):
                    if i == 1 and not (isinstance(g, int) and g == 0):
                        rows_to_send(g - 1)
                    probabilities(g, i)
                if not (isinstance(g, int) and g == 0):
                    scatter(g - 1)

            body(0)
            body(1)
            with pool.Fori(2, GROUPS - 1) as g:
                body(g)
            body(GROUPS - 1)
            rows_to_send(GROUPS - 1)
            scatter(GROUPS - 1)

            pool.nop().then_inc(s["ye_free"], 1)
            for e in range(EXPERTS):
                c, t = counts(pool, e)
                with pool.Fori(0, c) as i:
                    pool.wait_ge(s["idx_ready"], t + i + 1)
                    for h in range(2):
                        pool.wait_ge(s["ye_ready"], (t + i) * 2 + h + 3)
                        apart(pool)
                        pool.indirect_dma_start(
                            mixed_dram, bass.IndirectOffsetOnAxis(ap=idx_now[:, h:h + 1], axis=0),
                            ye[h][:], None).then_inc(s["y_out"], 16)
                    pool.wait_ge(s["y_out"], (t + i) * 32 + 32)
                    pool.sem_inc(s["ye_free"])

        @block.scalar
        def _(act):
            act.dma_start(cst[:], consts).then_inc(s["cst_in"], 16)
            act.dma_start(vrows[V_ROUTER:V_B1, :], w_r).then_inc(s["vec_in"], 16)
            act.dma_start(vrows[V_B1:V_TOK, :], E_b1.rearrange("e (c f) -> (e c) f", f=P)).then_inc(s["vec_in"], 16)
            for n, v in enumerate((W1_b, W1_sb, eps_out1, W2_b, W2_sb, eps_out2)):
                act.dma_start(vrows[V_TOK + n:V_TOK + n + 1, :], v.unsqueeze(0)).then_inc(s["vec_in"], 16)
            act.dma_start(noise_in[:, 0, :], eps_in1.partition_broadcast(P)).then_inc(s["tok_in"], 16)
            act.dma_start(noise_in[:, 1, :], eps_in2.partition_broadcast(P)).then_inc(s["tok_in"], 16)
            for n, (w, sw) in enumerate(((W1_w, W1_sw), (W2_w, W2_sw))):
                act.dma_start(w_tok[:, n, :], w).then_inc(s["noise_w_in"], 16)
                act.dma_start(sw_tok[:, n, :], sw).then_inc(s["noise_w_in"], 16)
            act.dma_start(w3[:], W3_w).then_inc(s["w3_in"], 16)
            act.dma_start(b3_row[:], W3_b.partition_broadcast(P)).then_inc(s["b3_in"], 16)

            act.wait_ge(s["tok_in"], 32)
            act.activation(noise_abs[:], noise_in[:], ACT.Abs).then_inc(s["noise_a"], 1)
            act.activation(noise_sgn[:], noise_in[:], ACT.Sign).then_inc(s["noise_a"], 1)
            act.wait_ge(s["vcols_ready"], 1)
            eo_cols = vcols[:, V_TOK + 2:V_TOK + 6:3]
            act.activation(eo_abs[:], eo_cols, ACT.Abs).then_inc(s["noise_a"], 1)
            act.activation(eo_sgn[:], eo_cols, ACT.Sign).then_inc(s["noise_a"], 1)
            act.wait_ge(s["noise_a"], 4)
            act.activation(noise_abs[:], noise_abs[:], ACT.Sqrt).then_inc(s["noise_a"], 1)
            act.activation(eo_abs[:], eo_abs[:], ACT.Sqrt).then_inc(s["noise_a"], 1)
            for h in range(2):
                act.wait_ge(s[f"x_in{h}"], 16)
                src = xrow[:, h, :].rearrange("p (r j c) -> p j r c", r=PATCH, c=PATCH)
                act.activation(xpatch[:, h, 5:8, :].rearrange("p j (r c) -> p j r c", r=PATCH), src[:, 5:8],
                               ACT.Copy).then_inc(s["xpatch_a"], 1)
            act.wait_ge(s["qk_p"], 2)
            act.activation(wkT[:], ps[:, 1, :].rearrange("p (a d) -> p a d", d=D), ACT.Copy).then_inc(s["qkT_ready"], 1)
            act.wait_ge(s["qkT_p"], 1)
            for par in range(2):
                act.activation(qkT[:, par::2, :], ps[:, 2 + par, :].rearrange("p (a d) -> p a d", d=D), ACT.Copy,
                               scale=HD ** -0.5).then_inc(s["qkTs"], 1)
            for n in range(0, 8, 2):
                act.wait_ge(s["xT_p"], n + 1)
                act.activation(patches_to(n), ps[:, n, :].rearrange("p (j b) -> p j b", j=4), ACT.Copy)\
                    .then_inc(s["xT_a"], 1)

            def embed(g):
                wait(act, "mish_step", g, MISH, 1)
                act.activation(gexp[:], gclip[:], ACT.Exp).then_inc(s["exp_ready"], 1)

            def norm1(g):
                wait(act, "ln1_step", g, LN1, 5)
                act.activation(ln1[:], ve1[:], ACT.Ln).then_inc(s["ln1_ln"], 1)
                wait(act, "ln1_ln", g)
                act.activation(r1[:], ln1[:], ACT.Exp, scale=-0.5).then_inc(s["ln1_guess"], 1)

            def norm1_out(g):
                wait(act, "xnT_p", g)
                act.activation(xnT[:], ps[:, N_BANK, GROUP:2 * GROUP], ACT.Copy).then_inc(s["xnT_ready"], 1)

            def z_out(g, q):
                wait(act, "z_p", g, 4, q)
                act.activation(z_dst(q), z_src(q), ACT.Copy).then_inc(s["z_act"], 1)

            def values(g, i):
                wait(act, "v_p", g, TILES, i)
                wait(act, "pv_p", g - 1, TILES, i)
                act.activation(vs[:, i].rearrange("p b a k -> p (b a k)"), ps[:, V_BANK, :], ACT.Copy)\
                    .then_inc(s["vs_ready"], 1)

            def expo(g, i):
                wait(act, "soft_sub", g, TILES, i)
                act.activation(sx[:, i].rearrange("p h t -> p (h t)"), sx[:, i].rearrange("p h t -> p (h t)"),
                               ACT.Exp).then_inc(s["e_ready"], 1)

            def probs_out(g, i):
                wait(act, "pt_p", g, TILES, i)
                wait(act, "pv_p", g - 1, TILES, i)
                act.activation(probT[:, i].rearrange("p a b -> p (a b)"), ps[:, PT_BANK, :], ACT.Copy)\
                    .then_inc(s["probT_ready"], 1)

            def o_out(g, i):
                wait(act, "pv_p", g, TILES, i)
                wait(act, "wo_p", g - 1)
                act.activation(oT[:, i].rearrange("p a b -> p (a b)"), ps[:, O_BANK, :], ACT.Copy)\
                    .then_inc(s["o_ready"], 1)

            def norm2(g):
                wait(act, "ln2_step", g, LN2, 5)
                act.activation(ln2[:], ve2[:], ACT.Ln).then_inc(s["ln2_ln"], 1)
                wait(act, "ln2_ln", g)
                act.activation(r2[:], ln2[:], ACT.Exp, scale=-0.5).then_inc(s["ln2_guess"], 1)

            def send_copy(g):
                wait(act, "send_ready", g, 2, 0)
                act.activation(send[1][:, :, 0:D], send[0][:, :, 0:D], ACT.Copy).then_inc(s["send_ready"], 1)

            def hfT_out(g):
                wait(act, "hft_p", g)
                act.activation(hfT[:].rearrange("p i t -> p (i t)"), ps[:, V_BANK, GROUP:2 * GROUP], ACT.Copy)\
                    .then_inc(s["hfT_ready"], 1)

            def route(g):
                wait(act, "route_step", g, ROUTE, 3)
                act.activation(ediff[:], diff[:], ACT.Exp).then_inc(s["route_exp"], 1)

            def embed_all(g):
                embed(g)
                norm1(g)
                norm1_out(g)
                z_out(g, 0)
                z_out(g, 2)

            def body(g, nxt=True, prev=True):
                values(g, 0)
                expo(g, 0)
                if prev:
                    norm2(g - 1)
                values(g, 1)
                expo(g, 1)
                if nxt:
                    embed(g + 1)
                if prev:
                    send_copy(g - 1)
                    hfT_out(g - 1)
                probs_out(g, 0)
                if nxt:
                    norm1(g + 1)
                o_out(g, 0)
                if prev:
                    route(g - 1)
                probs_out(g, 1)
                if nxt:
                    norm1_out(g + 1)
                o_out(g, 1)
                if nxt:
                    z_out(g + 1, 0)
                    z_out(g + 1, 2)

            embed_all(0)
            body(0, prev=False)
            body(1)
            with act.Fori(2, GROUPS - 1) as g:
                body(g)
            body(GROUPS - 1, nxt=False)
            norm2(GROUPS - 1)
            send_copy(GROUPS - 1)
            hfT_out(GROUPS - 1)
            route(GROUPS - 1)

            for e in range(EXPERTS):
                c, t = counts(act, e)
                with act.Fori(0, c) as i:
                    for f in range(FC):
                        act.wait_ge(s["hid_p"], (t + i) * FC + f + 1)
                        act.activation(hid[:, f, :], ps[:, HID_BANKS[f], 0:EXPERT_TILE], ACT.Gelu,
                                       bias=vcols[:, V_B1 + e * FC + f:V_B1 + e * FC + f + 1])\
                            .then_inc(s["hid_ready"], 1)

        @block.vector
        def _(dve):
            dve.wait_ge(s["cst_in"], 16)
            dve.tensor_copy(upper[:], cst[:, C_UPPER:C_UPPER + P]).then_inc(s["bf_ready"], 1)
            dve.wait_ge(s["b3_in"], 16)
            dve.tensor_tensor(pos_b3[:], cst[:, C_POS:C_POS + D], b3_row[:], ALU.add).then_inc(s["posb"], 1)
            dve.wait_ge(s["vcols_p"], 1)
            dve.tensor_copy(vcols[:], ps[:, 4, 0:V_ROWS]).then_inc(s["vcols_ready"], 1)
            dve.wait_ge(s["vcols_p"], 2)
            dve.tensor_copy(w3T[:], ps[:, 5, 0:P]).then_inc(s["w3T_ready"], 1)
            dve.wait_ge(s["noise_a"], 6)
            dve.tensor_tensor(noise_in[:], noise_abs[:], noise_sgn[:], ALU.mult).then_inc(s["w_chain"], 1)
            dve.tensor_tensor(eo[:], eo_abs[:], eo_sgn[:], ALU.mult).then_inc(s["w_chain"], 1)
            dve.wait_ge(s["w_chain"], 2)
            dve.wait_ge(s["noise_w_in"], 64)
            dve.wait_ge(s["vcols_ready"], 1)
            for n in range(2):
                dve.tensor_scalar(noise_in[:, n, :], noise_in[:, n, :], eo[:, n:n + 1], None, ALU.mult)\
                    .then_inc(s["w_chain"], 1)
            dve.tensor_tensor(bias_t[:], vcols[:, V_TOK + 1:V_TOK + 5:3], eo[:], ALU.mult).then_inc(s["w_chain"], 1)
            dve.wait_ge(s["w_chain"], 5)
            dve.tensor_tensor(noise_in[:], noise_in[:], sw_tok[:], ALU.mult).then_inc(s["w_chain"], 1)
            dve.tensor_tensor(bias_tok[:], bias_t[:], vcols[:, V_TOK:V_TOK + 4:3], ALU.add).then_inc(s["w_chain"], 1)
            dve.wait_ge(s["w_chain"], 7)
            dve.tensor_tensor(w_tok[:], w_tok[:], noise_in[:], ALU.add).then_inc(s["w_noise"], 1)
            for h in range(2):
                dve.wait_ge(s[f"x_in{h}"], 16)
                src = xrow[:, h, :].rearrange("p (r j c) -> p j r c", r=PATCH, c=PATCH)
                dve.tensor_copy(xpatch[:, h, 0:5, :].rearrange("p j (r c) -> p j r c", r=PATCH), src[:, 0:5])\
                    .then_inc(s["xpatch_v"], 1)
            dve.wait_ge(s["qk_p"], 1)
            dve.tensor_copy(wqT[:], ps[:, 0, :].rearrange("p (a d) -> p a d", d=D)).then_inc(s["qkT_ready"], 1)
            dve.wait_ge(s["wtok_p"], 1)
            dve.tensor_copy(w_tokT[:].rearrange("p n k h -> p (n k h)"), ps[:, 6, :]).then_inc(s["wtokT_ready"], 1)
            for n in range(1, 8, 2):
                dve.wait_ge(s["xT_p"], n + 1)
                dve.tensor_copy(patches_to(n), ps[:, n, :].rearrange("p (j b) -> p j b", j=4)).then_inc(s["xT_v"], 1)
            dve.wait_ge(s["run0"], 1)

            def newton(name, g, per, k, ve, r, n, to):
                dve.scalar_tensor_tensor(n, r, -0.5, r, ALU.mult, ALU.mult).then_inc(s[name], 1)
                wait(dve, name, g, per, k)
                dve.tensor_tensor(n, n, ve, ALU.mult).then_inc(s[name], 1)
                wait(dve, name, g, per, k + 1)
                dve.scalar_tensor_tensor(to, n, 1.5, r, ALU.add, ALU.mult).then_inc(s[name], 1)
                wait(dve, name, g, per, k + 2)

            def embed_a(g):
                wait(dve, "embed_p", g)
                wait(dve, "mish_step", g - 1, MISH, 4)
                dve.tensor_scalar(gpre[:], ps[:, Z_BANK, 0:GROUP], bias_tok[:, 0:1], None, ALU.add)\
                    .then_inc(s["mish_step"], 1)
                wait(dve, "mish_step", g, MISH, 0)
                dve.tensor_scalar(gclip[:], gpre[:], 20.0, None, ALU.min).then_inc(s["mish_step"], 1)

            def embed_b(g):
                wait(dve, "exp_ready", g)
                dve.scalar_tensor_tensor(gnum[:], gexp[:], 2.0, gexp[:], ALU.add, ALU.mult).then_inc(s["mish_step"], 1)
                wait(dve, "mish_step", g, MISH, 2)
                dve.tensor_scalar(gden[:], gnum[:], 2.0, None, ALU.add).then_inc(s["mish_step"], 1)
                dve.tensor_tensor(gmul[:], gnum[:], gpre[:], ALU.mult).then_inc(s["mish_step"], 1)
                wait(dve, "mish_step", g, MISH, 4)
                dve.reciprocal(gden[:], gden[:]).then_inc(s["mish_step"], 1)
                wait(dve, "mish_step", g, MISH, 5)
                dve.tensor_tensor(gmul[:], gmul[:], gden[:], ALU.mult).then_inc(s["mish_step"], 1)
                wait(dve, "mish_step", g, MISH, 6)
                wait(dve, "w3_p", g - 1)
                dve.scalar_tensor_tensor(mT[:], ps[:, Z_BANK, GROUP:2 * GROUP], bias_tok[:, 1:2], gmul[:],
                                         ALU.add, ALU.mult).then_inc(s["mT_ready"], 1)

            def token_norm(g):
                wait(dve, "w3_p", g)
                if isinstance(g, int) and g == 0:
                    dve.wait_ge(s["posb"], 1)
                h0 = h_at(g)
                dve.tensor_tensor(h0, ps[:, N_BANK, 0:GROUP].rearrange("p (i d) -> p i d", i=TILES),
                                  pos_b3[:].unsqueeze(1).broadcast_to([P, TILES, D]), ALU.add)\
                    .then_inc(s["ln1_step"], 1)
                wait(dve, "ln1_step", g, LN1, 0)
                for i in range(TILES):
                    dve.bn_stats(st1[:, i, :], h_tile(g, i)).then_inc(s["ln1_step"], 1)
                for i in range(TILES):
                    wait(dve, "ln1_step", g, LN1, 1 + i)
                    apart(dve)
                    dve.bn_aggr(mv1[:, i, :], st1[:, i, :]).then_inc(s["ln1_step"], 1)
                wait(dve, "ln1_step", g, LN1, 4)
                dve.tensor_scalar(ve1[:], mv1[:, :, 1], EPS, None, ALU.add).then_inc(s["ln1_step"], 1)

            def token_norm_out(g):
                wait(dve, "ln1_guess", g)
                newton("ln1_step", g, LN1, 6, ve1[:], r1[:], n1[:], rstd1[:])
                wait(dve, "xnT_p", g - 1)
                for i in range(TILES):
                    ins = dve.tensor_scalar(xn[:, i, :], h_tile(g, i), mv1[:, i, 0:1], rstd1[:, i:i + 1],
                                            ALU.subtract, ALU.mult)
                    ins.then_inc(s["xn_ready"], 1)

            def z_out(g, q):
                wait(dve, "z_p", g, 4, q)
                dve.tensor_copy(z_dst(q), z_src(q)).then_inc(s["z_dve"], 1)

            def soft_a(g, i):
                wait(dve, "s_p", g, TILES, i)
                sc = ps[:, S_BANK + i, :].rearrange("p (h t) -> p h t", h=HEADS)
                dve.tensor_reduce(smax[:, i, :], sc, AX_X, ALU.max).then_inc(s["soft_max"], 1)
                wait(dve, "soft_max", g, TILES, i)
                wait(dve, "prob_ready", g - 1, TILES, i)
                dve.tensor_tensor(sx[:, i], sc, smax[:, i, :].unsqueeze(2).broadcast_to([P, HEADS, L]),
                                  ALU.subtract).then_inc(s["soft_sub"], 1)

            def soft_b(g, i):
                wait(dve, "e_ready", g, TILES, i)
                dve.tensor_reduce(ssum[:, i, :], sx[:, i], AX_X, ALU.add).then_inc(s["soft_sum"], 1)
                wait(dve, "soft_sum", g, TILES, i)
                dve.reciprocal(srec[:, i, :], ssum[:, i, :]).then_inc(s["soft_rec"], 1)

            def residual(g):
                wait(dve, "wo_p", g)
                h = h_at(g)
                dve.tensor_tensor(h, ps[:, V_BANK, 0:GROUP].rearrange("p (i d) -> p i d", i=TILES), h, ALU.add)\
                    .then_inc(s["h1_ready"], 1)

            def norm2_a(g):
                wait(dve, "h1_ready", g)
                for i in range(TILES):
                    dve.bn_stats(st2[:, i, :], h_tile(g, i)).then_inc(s["ln2_step"], 1)
                for i in range(TILES):
                    wait(dve, "ln2_step", g, LN2, i)
                    apart(dve)
                    dve.bn_aggr(mv2[:, i, :], st2[:, i, :]).then_inc(s["ln2_step"], 1)
                wait(dve, "ln2_step", g, LN2, 3)
                dve.tensor_scalar(ve2[:, 0, :], mv2[:, :, 1], EPS, None, ALU.add).then_inc(s["ln2_step"], 1)
                wait(dve, "ln2_step", g, LN2, 4)
                dve.scalar_tensor_tensor(ve2[:, 1, :], ve2[:, 0, :], EPS, mv2[:, :, 1], ALU.mult, ALU.add)\
                    .then_inc(s["ln2_step"], 1)

            def norm2_b(g):
                wait(dve, "ln2_guess", g)
                newton("ln2_step", g, LN2, 6, ve2[:], r2[:], n2[:], rstd2[:])
                wait(dve, "send_step", g - 1, 4, 1)
                for i in range(TILES):
                    ins = dve.tensor_scalar(hh[:, i, :], h_tile(g, i), mv2[:, i, 0:1], rstd2[:, 1, i:i + 1],
                                            ALU.subtract, ALU.mult)
                    ins.then_inc(s["ln2_step"], 1)
                for i in range(TILES):
                    dve.tensor_scalar(y[:, i, :], h_tile(g, i), mv2[:, i, 0:1], rstd2[:, 0, i:i + 1],
                                      ALU.subtract, ALU.mult).then_inc(s["y_step"], 1)
                wait(dve, "y_step", g, TILES, 1)
                dve.tensor_tensor(h_at(g), h_at(g), y[:], ALU.add).then_inc(s["hy_ready"], 1)

            def route_a(g):
                def done(k):
                    wait(dve, "route_step", g, ROUTE, k)

                wait(dve, "lg_p", g)
                dve.tensor_tensor(lg[:], ps[:, V_BANK, 0:TILES * EXPERTS].rearrange("p (i e) -> p i e", i=TILES),
                                  br_row[:].unsqueeze(1).broadcast_to([P, TILES, EXPERTS]), ALU.add)\
                    .then_inc(s["route_step"], 1)
                done(0)
                apart(dve)
                for i in range(TILES):
                    dve.max(top[:, i, :], lg[:, i, :]).then_inc(s["route_step"], 1)
                done(2)
                dve.tensor_tensor(diff[:], top[:, :, 1], top[:, :, 0], ALU.subtract).then_inc(s["route_step"], 1)
                for i in range(TILES):
                    dve.max_index(topi[:, i, :], top[:, i, :], lg[:, i, :]).then_inc(s["route_step"], 1)
                done(5)
                dve.tensor_copy(topf[:], topi[:, :, 0:2]).then_inc(s["route_step"], 1)
                done(6)
                iota = cst[:, C_IOTA:C_EBASE].rearrange("p (i e) -> p i e", i=TILES)
                for k in range(2):
                    dve.tensor_tensor(onehot[:, k], iota, topf[:, :, k].unsqueeze(2).broadcast_to([P, TILES, EXPERTS]),
                                      ALU.is_equal).then_inc(s["route_step"], 1)
                wait(dve, "rank_p", g - 1)
                dve.tensor_copy(run[:, 0, :], run[:, TILES, :]).then_inc(s["route_step"], 1)
                done(8)
                dve.tensor_tensor(picks[:], onehot[:, 0], onehot[:, 1], ALU.add).then_inc(s["route_step"], 1)
                for i in range(TILES):
                    done(10 + i)
                    dve.tensor_tensor(run[:, i + 1, :], run[:, i, :], picks[:, i, :], ALU.add)\
                        .then_inc(s["route_step"], 1)

            def route_b(g):
                def done(k):
                    wait(dve, "route_step", g, ROUTE, k)

                wait(dve, "route_exp", g)
                dve.tensor_scalar(eone[:], ediff[:], 1.0, None, ALU.add).then_inc(s["route_step"], 1)
                done(13)
                dve.reciprocal(gate_at(g, 0), eone[:]).then_inc(s["route_step"], 1)
                wait(dve, "rank_p", g)
                dve.tensor_tensor(slot8[:], ps[:, V_BANK, 32:32 + TILES * EXPERTS].rearrange("p (i e) -> p i e", i=TILES),
                                  cst[:, C_EBASE:C_DEST].rearrange("p (i e) -> p i e", i=TILES), ALU.add)\
                    .then_inc(s["route_step"], 1)
                done(14)
                dve.tensor_tensor(gate_at(g, 1), gate_at(g, 0), ediff[:], ALU.mult).then_inc(s["route_step"], 1)
                done(15)
                dve.tensor_tensor(slotk[:], onehot[:], slot8[:].unsqueeze(1).broadcast_to([P, 2, TILES, EXPERTS]),
                                  ALU.mult).then_inc(s["route_step"], 1)
                done(17)
                dve.tensor_reduce(slotf[:], slotk[:], AX_X, ALU.add).then_inc(s["route_step"], 1)
                done(18)
                if not (isinstance(g, int) and g == 0):
                    dve.wait_ge(s["scattered"], g * (32 * TILES))
                dve.tensor_copy(slot[:], slotf[:].rearrange("p k i -> p (k i)")).then_inc(s["slot_ready"], 1)

            def h_at(g):
                return h_all[:, g, :, :] if isinstance(g, int) else \
                    h_all[:].rearrange("p g i d -> p (g i) d")[:, bass.ds(g * TILES, TILES), :]

            def h_tile(g, i):
                return h_all[:, g, i, :] if isinstance(g, int) else \
                    h_all[:].rearrange("p g i d -> p (g i d)")[:, bass.ds(g * (TILES * D) + i * D, D)]

            def gate_at(g, k):
                return gates[:, g, k, :] if isinstance(g, int) else \
                    gates[:].rearrange("p g k i -> p (g k i)")[:, bass.ds(g * (2 * TILES) + k * TILES, TILES)]

            def body(g, nxt=True, prev=True):
                soft_a(g, 0)
                if prev:
                    norm2_a(g - 1)
                soft_a(g, 1)
                soft_b(g, 0)
                if nxt:
                    embed_a(g + 1)
                if prev:
                    norm2_b(g - 1)
                soft_b(g, 1)
                if nxt:
                    embed_b(g + 1)
                if prev:
                    route_a(g - 1)
                if nxt:
                    token_norm(g + 1)
                if prev:
                    route_b(g - 1)
                if nxt:
                    token_norm_out(g + 1)
                    z_out(g + 1, 1)
                    z_out(g + 1, 3)
                residual(g)

            embed_a(0)
            embed_b(0)
            token_norm(0)
            token_norm_out(0)
            z_out(0, 1)
            z_out(0, 3)
            body(0, prev=False)
            body(1)
            with dve.Fori(2, GROUPS - 1) as g:
                body(g)
            body(GROUPS - 1, nxt=False)
            norm2_a(GROUPS - 1)
            norm2_b(GROUPS - 1)
            route_a(GROUPS - 1)
            route_b(GROUPS - 1)

            def step_done(k):
                dve.wait_ge(s["count_step"], k)

            dve.wait_ge(s["count_p"], 1)
            dve.tensor_copy(cnt[:], ps[:, V_BANK, 64:64 + EXPERTS]).then_inc(s["count_step"], 1)
            step_done(1)
            dve.tensor_copy(table[:, 0:EXPERTS], cnt[:]).then_inc(s["count_step"], 1)
            dve.tensor_tensor(over[:], cnt[:].unsqueeze(2).broadcast_to([P, EXPERTS, EXPERTS]),
                              cst[:, C_STEP:C_LOWER].unsqueeze(1).broadcast_to([P, EXPERTS, EXPERTS]), ALU.is_gt)\
                .then_inc(s["count_step"], 1)
            step_done(3)
            dve.tensor_reduce(steps[:], over[:], AX_X, ALU.add).then_inc(s["count_step"], 1)
            step_done(4)
            dve.tensor_scalar(steps[:], steps[:], 1.0, None, ALU.max).then_inc(s["count_step"], 1)
            step_done(5)
            dve.tensor_tensor(before[:], steps[:].unsqueeze(1).broadcast_to([P, EXPERTS, EXPERTS]),
                              cst[:, C_LOWER:C_TAIL].rearrange("p (a b) -> p a b", a=EXPERTS), ALU.mult)\
                .then_inc(s["count_step"], 1)
            dve.tensor_copy(table[:, EXPERTS:2 * EXPERTS], steps[:]).then_inc(s["count_step"], 1)
            step_done(7)
            dve.tensor_reduce(start_f[:], before[:], AX_X, ALU.add).then_inc(s["start_ready"], 1)
            dve.wait_ge(s["start_ready"], 1)
            dve.tensor_copy(table[:, 2 * EXPERTS:], start_f[:]).then_inc(s["count_step"], 1)

            dve.nop().then_inc(s["xe_free"], 1)
            dve.nop().then_inc(s["ye_ready"], 2)

            def take(j):
                dve.wait_ge(s["xet_p"], j + 1)
                dve.tensor_copy(xeT[:], ps[:, 2, 0:EXPERT_TILE]).then_inc(s["xeT_ready"], 1)
                for h in range(2):
                    dve.wait_ge(s[f"xe_in{h}"], (j + 1) * 16)
                dve.tensor_copy(idx_next[:, 0:1], xe[0][:, D:D + 1]).then_inc(s["idx_step"], 1)
                dve.tensor_copy(idx_next[:, 1:2], xe[1][:, D:D + 1]).then_inc(s["xe_free"], 1)

            take(0)
            for e in range(EXPERTS):
                c, t = counts(dve, e)
                with dve.Fori(0, c) as i:
                    dve.wait_ge(s["ye_free"], t + i + 1)
                    dve.wait_ge(s["idx_step"], t + i + 1)
                    dve.wait_ge(s["xe_free"], t + i + 2)
                    dve.tensor_copy(idx_now[:], idx_next[:]).then_inc(s["idx_ready"], 1)
                    dve.wait_ge(s["idx_ready"], t + i + 1)
                    dve.wait_ge(s["hid_p"], (t + i) * FC + FC)
                    take(t + i + 1)
                    for h in range(2):
                        dve.wait_ge(s["y_p"], (t + i) * 2 + h + 1)
                        dve.tensor_tensor(ye[h][:], ps[:, 3 + h, 0:D], b2_row[:, e, :], ALU.add)\
                            .then_inc(s["ye_ready"], 1)

            dve.wait_ge(s["hy_ready"], GROUPS)
            dve.wait_ge(s["route_step"], GROUPS * ROUTE)
            hy = h_all[:].rearrange("p g i d -> p (g i) d")
            for t in range(NTOK // P):
                g, i = t // TILES, t % TILES
                dve.wait_ge(s[f"fin_in{t // 4}"], 32)
                dve.scalar_tensor_tensor(first[:, t, :], first[:, t, :], gates[:, g, 0, i:i + 1], hy[:, t, :],
                                         ALU.mult, ALU.add).then_inc(s["mix_step"], 1)
                if t % 4 == 3:
                    for u in range(t - 3, t + 1):
                        g, i = u // TILES, u % TILES
                        dve.wait_ge(s["mix_step"], 8 * (t // 4) + u % 4 + 1)
                        dve.scalar_tensor_tensor(first[:, u, :], second[:, u, :], gates[:, g, 1, i:i + 1],
                                                 first[:, u, :], ALU.mult, ALU.add).then_inc(s["mix_step"], 1)

        @block.tensor
        def _(pe):
            pe.wait_ge(s["cst_in"], 16)
            pe.wait_ge(s["vec_in"], 16 * 8)
            pe.transpose(ps[:, 4, 0:V_ROWS], vrows[:], ident[0:V_ROWS, 0:V_ROWS]).then_inc(s["vcols_p"], 1)
            pe.wait_ge(s["w3_in"], 16)
            pe.transpose(ps[:, 5, 0:P], w3[:], ident).then_inc(s["vcols_p"], 1)
            pe.wait_ge(s["ak_in"], 48)
            for q in range(2):
                for a in range(PAIRS):
                    last = pe.transpose(ps[:, q, a * D:(a + 1) * D],
                                        ak[:, q, 2 * a:2 * a + 2, :].rearrange("p h k -> p (h k)"), ident)
                last.then_inc(s["qk_p"], 1)
            pe.wait_ge(s["qkT_ready"], 2)
            for h in range(HEADS):
                a, par = h // 2, h % 2
                r = slice(par * HD, par * HD + HD)
                last = pe.matmul(ps[:, 2 + par, a * D:(a + 1) * D], wkT[r, a, :], wqT[r, a, :], start=True, stop=True)
            last.then_inc(s["qkT_p"], 1)
            pe.wait_ge(s["w_noise"], 1)
            for n in range(2):
                for k in range(2):
                    last = pe.transpose(ps[:, 6, (2 * n + k) * P:(2 * n + k + 1) * P],
                                        w_tok[:, n, k * P:(k + 1) * P], ident)
            last.then_inc(s["wtok_p"], 1)
            for n in range(8):
                half, k, jq = n // 4, n // 2 % 2, n % 2
                pe.wait_ge(s["xpatch_v"], half + 1)
                pe.wait_ge(s["xpatch_a"], half + 1)
                if n == 2:
                    pe.wait_ge(s["qkTs"], 2)
                if n == 4:
                    pe.wait_ge(s["vcols_ready"], 1)
                if n == 5:
                    pe.wait_ge(s["w3T_ready"], 1)
                if n == 6:
                    pe.wait_ge(s["wtokT_ready"], 1)
                for j in range(4):
                    last = pe.transpose(ps[:, n, j * P:(j + 1) * P],
                                        xpatch[:, half, 4 * jq + j, k * P:(k + 1) * P], ident)
                last.then_inc(s["xT_p"], 1)

            def embed(g):
                if isinstance(g, int) and g == 0:
                    pe.wait_ge(s["xT_a"], 4)
                    pe.wait_ge(s["xT_v"], 4)
                    pe.wait_ge(s["wtokT_ready"], 1)
                wait(pe, "z_act", g - 1, 2, 1)
                for n in range(2):
                    for k in range(2):
                        last = pe.matmul(ps[:, Z_BANK, n * GROUP:(n + 1) * GROUP], w_tokT[:, n, k, :], xT_at(g, k),
                                         start=(k == 0), stop=(k == 1))
                last.then_inc(s["embed_p"], 1)

            def xT_at(g, k):
                return xT[:, k, g * GROUP:(g + 1) * GROUP] if isinstance(g, int) else \
                    xT[:].rearrange("p k t -> p (k t)")[:, bass.ds(g * GROUP + k * NTOK, GROUP)]

            def project(g):
                wait(pe, "mT_ready", g)
                wait(pe, "xnT_ready", g - 1)
                for i in range(TILES):
                    last = pe.matmul(ps[:, N_BANK, i * D:(i + 1) * D], mT[:, i * P:(i + 1) * P], w3T[:],
                                     start=True, stop=True)
                last.then_inc(s["w3_p"], 1)

            def turn_norm(g):
                for i in range(TILES):
                    wait(pe, "xn_ready", g, TILES, i)
                    last = pe.transpose(ps[:, N_BANK, GROUP + i * P:GROUP + (i + 1) * P], xn[:, i, :], ident)
                last.then_inc(s["xnT_p"], 1)

            def z(g):
                wait(pe, "xnT_ready", g)
                for q in range(4):
                    if q == 1:
                        wait(pe, "z_dve", g - 1, 2, 1)
                    if q == 2:
                        wait(pe, "z_act", g, 2, 0)
                    if q == 3:
                        wait(pe, "z_dve", g, 2, 0)
                    for hh_ in range(2):
                        last = pe.matmul(ps[:, Z_BANK + q % 2, hh_ * GROUP:(hh_ + 1) * GROUP], qkT[:, 2 * q + hh_, :],
                                         xnT[:], start=True, stop=True)
                    last.then_inc(s["z_p"], 1)

            def scores(g, i):
                wait(pe, "z_act", g, 2, 1)
                wait(pe, "z_dve", g, 2, 1)
                wait(pe, "soft_sub", g - 1, TILES, i)
                for b in range(IPT):
                    n = i * IPT + b
                    last = pe.matmul(ps[b * L:(b + 1) * L, S_BANK + i, :], xnT[:, n * L:(n + 1) * L],
                                     zs[:, n].rearrange("p h t -> p (h t)"), start=True, stop=True)
                last.then_inc(s["s_p"], 1)

            def values(g, i):
                if i == 0:
                    wait(pe, "h1_ready", g - 1)
                else:
                    wait(pe, "vs_ready", g, TILES, 0)
                for b in range(IPT):
                    n = i * IPT + b
                    for par in range(2):
                        last = pe.matmul(ps[par * HD:(par + 1) * HD, V_BANK, b * GROUP:(b + 1) * GROUP],
                                         xnT[:, n * L:(n + 1) * L], ak[:, 2, par::2, :], start=True, stop=True)
                last.then_inc(s["v_p"], 1)

            def turn_probs(g, i):
                wait(pe, "prob_ready", g, TILES, i)
                if i == 0:
                    wait(pe, "probT_ready", g - 1, TILES, 1)
                else:
                    wait(pe, "probT_ready", g, TILES, 0)
                for a in range(PAIRS):
                    last = pe.transpose(ps[:, PT_BANK, a * P:(a + 1) * P],
                                        prob[:, i, 2 * a:2 * a + 2, :].rearrange("p h t -> p (h t)"), ident)
                last.then_inc(s["pt_p"], 1)

            def attend(g, i):
                wait(pe, "probT_ready", g, TILES, i)
                wait(pe, "vs_ready", g, TILES, i)
                if i == 0:
                    wait(pe, "o_ready", g - 1, TILES, 1)
                else:
                    wait(pe, "o_ready", g, TILES, 0)
                apart(pe)
                for a in range(PAIRS):
                    for b in range(IPT):
                        for par in range(2):
                            r = slice(par * HD, par * HD + HD)
                            last = pe.matmul(ps[r, O_BANK, a * P + b * L:a * P + (b + 1) * L], vs[r, i, b, a, :],
                                             probT[r, i, a, b * L:(b + 1) * L], start=True, stop=True)
                last.then_inc(s["pv_p"], 1)

            def out_project(g):
                if isinstance(g, int) and g == 0:
                    pe.wait_ge(s["wo_in"], 16)
                    wait(pe, "vs_ready", g, TILES, 1)
                else:
                    wait(pe, "route_step", g - 1, ROUTE, 15)
                for i in range(TILES):
                    wait(pe, "o_ready", g, TILES, i)
                    for a in range(PAIRS):
                        last = pe.matmul(ps[:, V_BANK, i * D:(i + 1) * D], oT[:, i, a, :], wo[:, a, :],
                                         start=(a == 0), stop=(a == PAIRS - 1))
                last.then_inc(s["wo_p"], 1)

            def turn_rows(g, last_group=False):
                wait(pe, "send_ready", g, 2, 0)
                if not last_group:
                    wait(pe, "vs_ready", g + 1, TILES, 1)
                wait(pe, "hfT_ready", g - 1)
                for i in range(TILES):
                    last = pe.transpose(ps[:, V_BANK, GROUP + i * P:GROUP + (i + 1) * P], send[0][:, i, 0:D], ident)
                last.then_inc(s["hft_p"], 1)

            def logits(g):
                wait(pe, "hfT_ready", g)
                for i in range(TILES):
                    last = pe.matmul(ps[:, V_BANK, i * EXPERTS:(i + 1) * EXPERTS], hfT[:, i, :],
                                     vcols[:, V_ROUTER:V_ROUTER + EXPERTS], start=True, stop=True)
                last.then_inc(s["lg_p"], 1)

            def ranks(g):
                wait(pe, "route_step", g, ROUTE, 12)
                if isinstance(g, int) and g == 0:
                    pe.wait_ge(s["bf_ready"], 2)
                o = ps[:, V_BANK, 32:32 + TILES * EXPERTS]
                pe.matmul(o, upper[:], picks[:].rearrange("p i e -> p (i e)"), start=True, stop=False)
                pe.matmul(o, ones[:], run[:, 0:TILES, :].rearrange("p i e -> p (i e)"), start=False, stop=True)\
                    .then_inc(s["rank_p"], 1)

            def body(g, nxt=True, prev=True):
                for i in range(TILES):
                    scores(g, i)
                    values(g, i)
                if nxt:
                    embed(g + 1)
                if prev:
                    turn_rows(g - 1)
                    logits(g - 1)
                turn_probs(g, 0)
                attend(g, 0)
                if nxt:
                    project(g + 1)
                turn_probs(g, 1)
                if prev:
                    ranks(g - 1)
                attend(g, 1)
                if nxt:
                    turn_norm(g + 1)
                    z(g + 1)
                out_project(g)

            embed(0)
            project(0)
            turn_norm(0)
            z(0)
            body(0, prev=False)
            body(1)
            with pe.Fori(2, GROUPS - 1) as g:
                body(g)
            body(GROUPS - 1, nxt=False)
            g = GROUPS - 1
            wait(pe, "h1_ready", g)
            turn_rows(g, last_group=True)
            logits(g)
            ranks(g)
            wait(pe, "route_step", g, ROUTE, 15)
            pe.matmul(ps[:, V_BANK, 64:64 + EXPERTS], ones[:], run[:, TILES, :], start=True, stop=True)\
                .then_inc(s["count_p"], 1)

            pe.wait_ge(s["ew_in"], 48)
            pe.wait_ge(s["count_step"], 8)

            def turn(j):
                for h in range(2):
                    pe.wait_ge(s[f"xe_in{h}"], (j + 1) * 16)
                    last = pe.transpose(ps[:, 2, h * P:(h + 1) * P], xe[h][:, 0:D], ident)
                    if h == 0:
                        continue
                    last.then_inc(s["xet_p"], 1)

            turn(0)
            for e in range(EXPERTS):
                c, t = counts(pe, e)
                with pe.Fori(0, c) as i:
                    j = t + i
                    pe.wait_ge(s["xeT_ready"], j + 1)
                    for f in range(FC):
                        pe.matmul(ps[:, HID_BANKS[f], 0:EXPERT_TILE],
                                  ew1[:, e, f * P:(f + 1) * P], xeT[:], start=True, stop=True)\
                            .then_inc(s["hid_p"], 1)
                    turn(j + 1)
                    for f in range(FC):
                        pe.wait_ge(s["hid_ready"], j * FC + f + 1)
                        if f == 0:
                            pe.wait_ge(s["ye_ready"], j * 2 + 2)
                        for h in range(2):
                            last = pe.matmul(ps[:, 3 + h, 0:D], hid[:, f, h * P:(h + 1) * P], ew2[:, e, f, :],
                                             start=(f == 0), stop=(f == FC - 1))
                            if f == FC - 1:
                                last.then_inc(s["y_p"], 1)


_INS = ['x'] + ['L0_tok_' + n for n in ('W1_w', 'W1_b', 'W1_sw', 'W1_sb', 'W2_w', 'W2_b', 'W2_sw', 'W2_sb', 'W3_w',
                                        'W3_b', 'eps_in1', 'eps_out1', 'eps_in2', 'eps_out2')] \
    + ['L0_attn_kernel', 'L0_attn_head_kernel'] \
    + ['L0_ffn_' + n for n in ('ln_g', 'ln_b', 'w_r', 'b_r', 'W1', 'b1', 'W2', 'b2')]


def kernel(**inputs):
    import numpy as _np
    import concourse.bacc as _bacc
    from concourse import mybir as _mybir
    from concourse.bass_utils import run_bass_kernel_spmd as _run

    nc = _bacc.Bacc("TRN2", target_bir_lowering=False, num_devices=1)
    arrays, args = {}, []
    for name in _INS:
        a = _np.ascontiguousarray(inputs[name])
        arrays[f"in_{name}_dram"] = a
        args.append(nc.dram_tensor(f"in_{name}_dram", a.shape, _mybir.dt.from_np(a.dtype), kind="ExternalInput").ap())
    arrays["constants_dram"] = constants()
    args.append(nc.dram_tensor("constants_dram", (P, C_END), F32, kind="ExternalInput").ap())
    args.append(nc.dram_tensor("out_0_dram", (IMAGES, L, D), F32, kind="ExternalOutput").ap())
    vit_tower(nc, *args)
    r = _run(nc, [arrays], core_ids=[0])
    return r.results[0]["out_0_dram"]
```

```python
from contextlib import ExitStack

import concourse.bass as bass
from concourse import mybir

F32 = mybir.dt.float32
BF16 = mybir.dt.bfloat16
I32 = mybir.dt.int32
U32 = mybir.dt.uint32
ALU = mybir.AluOpType
ACT = mybir.ActivationFunctionType
AX_X = mybir.AxisListType.X

P = 128
IMAGES, SIDE, PATCH = 32, 128, 16
L = (SIDE // PATCH) ** 2
D = 128
PIX = PATCH * PATCH
NTOK = IMAGES * L
HEADS, HD = 8, 64
PAIRS = HEADS // 2
EXPERTS, HID = 8, 512
FC = HID // P
GROUP = 256
GROUPS = NTOK // GROUP
TILES = GROUP // P
IPG = GROUP // L
IPT = P // L
BANK = 512
EPS = 1e-5
ROWLEN = D + 1
EXPERT_TILE = 256
TAIL = GROUP + EXPERT_TILE
REGION = NTOK + TAIL
TAIL_ROWS = EXPERTS * TAIL

C_IDENT = 0
C_UPPER = C_IDENT + P
C_POS = C_UPPER + P
C_IOTA = C_POS + D
C_EBASE = C_IOTA + TILES * EXPERTS
C_DEST = C_EBASE + TILES * EXPERTS
C_STEP = C_DEST + 2 * TILES
C_LOWER = C_STEP + EXPERTS
C_TAIL = C_LOWER + EXPERTS * EXPERTS
TAIL_R = TAIL // P
C_END = C_TAIL + EXPERTS * TAIL_R

T_W = 0
T_SW = T_W + 2 * 2 * P
T_EI = T_SW + 2 * 2 * P
T_VEC = T_EI + 4
T_W3 = T_VEC + 6
T_ROUTER = T_W3 + P
T_B1 = T_ROUTER + EXPERTS
T_END = T_B1 + EXPERTS * FC

R_EO = 0
R_B3 = R_EO + 2 * P
R_G = R_B3 + D
R_B = R_G + D
R_BR = R_B + D
R_B2 = R_BR + EXPERTS
R_END = R_B2 + EXPERTS * D


def constants():
    import math
    import numpy as np

    c = np.zeros((P, C_END), np.float32)
    p = np.arange(P)
    c[:, C_IDENT:C_IDENT + P] = np.eye(P)
    c[:, C_UPPER:C_UPPER + P] = p[:, None] < p[None, :]
    pos = np.arange(L, dtype=np.float32)[:, None]
    div = np.exp(np.arange(0, D, 2, dtype=np.float32) * np.float32(-math.log(10000.0) / D))
    angle = (pos * div).astype(np.float32)
    table = np.stack([np.sin(angle), np.cos(angle)], axis=-1).reshape(L, D)
    c[:, C_POS:C_POS + D] = np.concatenate([table] * IPT)
    c[:, C_IOTA:C_EBASE] = np.tile(np.arange(EXPERTS), TILES)
    c[:, C_EBASE:C_DEST] = np.tile(np.arange(EXPERTS) * REGION, TILES)
    for k in range(2):
        for i in range(TILES):
            c[:, C_DEST + k * TILES + i] = p + i * P + k * NTOK
    c[:, C_STEP:C_LOWER] = np.arange(EXPERTS) * EXPERT_TILE
    c[:, C_LOWER:C_TAIL] = (np.arange(EXPERTS)[None, :] < np.arange(EXPERTS)[:, None]).reshape(-1)
    for e in range(EXPERTS):
        for r in range(TAIL_R):
            c[:, C_TAIL + TAIL_R * e + r] = 2 * NTOK + e * TAIL + TAIL_R * p + r
    return c


def vit_tower(nc, patches, small, rows, attn, E_W1, E_W2, consts, out):
    rows_dram = nc.dram_tensor("expert_rows", [EXPERTS * REGION, ROWLEN], F32, kind="Internal").ap()
    mixed_dram = nc.dram_tensor("chosen_rows", [2 * NTOK + TAIL_ROWS, D], F32, kind="Internal").ap()

    ctx = ExitStack()
    with ctx:
        def sb(name, shape, dt=F32):
            return ctx.enter_context(nc.sbuf_tensor(name, shape, dt))

        def sem(name):
            return ctx.enter_context(nc.semaphore(name))

        cst = sb("cst", [P, C_END])
        ident = cst[:, C_IDENT:C_IDENT + P]
        upper = sb("upper", [P, P], BF16)
        ones = sb("ones", [P, P], BF16)
        sm = sb("sm", [P, T_END])
        row = sb("row", [P, R_END])
        w_tokT = sm[:, T_W:T_SW].rearrange("p (n k h) -> p n k h", n=2, k=2)
        sw_tokT = sm[:, T_SW:T_EI].rearrange("p (n k h) -> p n k h", n=2, k=2)
        w3T = sm[:, T_W3:T_ROUTER]
        wrT = sm[:, T_ROUTER:T_B1]
        g_row, b_row, br_row = row[:, R_G:R_B], row[:, R_B:R_BR], row[:, R_BR:R_B2]
        b2_row = row[:, R_B2:R_END].rearrange("p (e d) -> p e d", e=EXPERTS)
        ei_abs = sb("ei_abs", [P, 4])
        ei_sgn = sb("ei_sgn", [P, 4])
        ei = sb("ei", [P, 4])
        eo_abs = sb("eo_abs", [P, 2, P])
        eo_sgn = sb("eo_sgn", [P, 2, P])
        eo = sb("eo", [P, 2, P])
        ec_abs = sb("ec_abs", [P, 2])
        ec_sgn = sb("ec_sgn", [P, 2])
        ec = sb("ec", [P, 2])
        noise = sb("noise", [P, 2, 2, P])
        bias_t = sb("bias_t", [P, 2])
        bias_tok = sb("bias_tok", [P, 2])
        pos_b3 = sb("pos_b3", [P, D])
        at = sb("at", [P, 4, PAIRS, D])
        wqT, wkT, wo = at[:, 0], at[:, 1], at[:, 3]
        wv = at[:, 2].rearrange("p a (q k) -> p (a q k)", q=2).rearrange("p (r n) -> p r n", r=2)
        qkT = sb("qkT", [P, HEADS, D])
        ew1 = sb("ew1", [P, EXPERTS, HID])
        ew2 = sb("ew2", [P, EXPERTS, FC, D])
        tail = sb("tail", [P, EXPERTS, TAIL_R, ROWLEN])

        xT = sb("xT", [P, 2, NTOK])
        gpre = sb("gpre", [P, GROUP])
        gclip = sb("gclip", [P, GROUP])
        gexp = sb("gexp", [P, GROUP])
        gnum = sb("gnum", [P, GROUP])
        gden = sb("gden", [P, GROUP])
        glog = sb("glog", [P, GROUP])
        grec = sb("grec", [P, GROUP])
        gleft = sb("gleft", [P, GROUP])
        gfac = sb("gfac", [P, GROUP])
        up = sb("up", [P, GROUP])
        gu = sb("gu", [P, GROUP])
        gnu = sb("gnu", [P, GROUP])
        mT = sb("mT", [P, GROUP])
        h_all = sb("h_all", [P, GROUPS, TILES, D])
        st1 = sb("st1", [P, TILES, 6])
        mv1 = sb("mv1", [P, TILES, 2])
        ve1 = sb("ve1", [P, TILES])
        ln1 = sb("ln1", [P, TILES])
        r1 = sb("r1", [P, TILES])
        n1 = sb("n1", [P, TILES])
        rstd1 = sb("rstd1", [P, TILES])
        xn = sb("xn", [P, TILES, D])
        xnT = sb("xnT", [P, GROUP])
        zs = sb("zs", [P, IPG, HEADS, L])
        vs = sb("vs", [P, TILES, IPT, PAIRS, HD])
        smax = sb("smax", [P, TILES, HEADS])
        sx = sb("sx", [P, TILES, HEADS, L])
        ssum = sb("ssum", [P, TILES, HEADS])
        srec = sb("srec", [P, TILES, HEADS])
        prob = sb("prob", [P, TILES, HEADS, L])
        probT = sb("probT", [P, TILES, PAIRS, P])
        oT = sb("oT", [P, TILES, PAIRS, P])
        st2 = sb("st2", [P, TILES, 6])
        mv2 = sb("mv2", [P, TILES, 2])
        ve2 = sb("ve2", [P, 2, TILES])
        ln2 = sb("ln2", [P, 2, TILES])
        r2 = sb("r2", [P, 2, TILES])
        n2 = sb("n2", [P, 2, TILES])
        rstd2 = sb("rstd2", [P, 2, TILES])
        shift2 = sb("shift2", [P, 2, TILES])
        grow2 = sb("grow2", [P, TILES])
        hh = sb("hh", [P, TILES, D])
        hg = sb("hg", [P, TILES, D])
        dest = sb("dest", [P, 2, TILES])
        send = [sb(f"send{k}", [P, TILES, ROWLEN]) for k in range(2)]
        hfT = sb("hfT", [P, TILES, P])
        lg = sb("lg", [P, TILES, EXPERTS])
        top = sb("top", [P, TILES, 8])
        topi = sb("topi", [P, TILES, 8], U32)
        topf = sb("topf", [P, TILES, 2])
        diff = sb("diff", [P, TILES])
        ediff = sb("ediff", [P, TILES])
        eone = sb("eone", [P, TILES])
        onehot = sb("onehot", [P, 2, TILES, EXPERTS])
        picks = sb("picks", [P, TILES, EXPERTS], BF16)
        run = sb("run", [P, TILES + 1, EXPERTS], BF16)
        slot8 = sb("slot8", [P, TILES, EXPERTS])
        slotk = sb("slotk", [P, 2, TILES, EXPERTS])
        slotf = sb("slotf", [P, 2, TILES])
        slot = sb("slot", [P, 2 * TILES], U32)
        gates = sb("gates", [P, GROUPS, 2, TILES])

        cnt = sb("cnt", [P, EXPERTS])
        over = sb("over", [P, EXPERTS, EXPERTS])
        steps = sb("steps", [P, EXPERTS])
        before = sb("before", [P, EXPERTS, EXPERTS])
        start_f = sb("start_f", [P, EXPERTS])
        table = sb("table", [P, 3 * EXPERTS], I32)
        fill = sb("fill", [P, EXPERTS], I32)
        ring = sb("ring", [P, 2, 2, ROWLEN])
        xe = [sb(f"xe{h}", [P, ROWLEN]) for h in range(2)]
        xeT = sb("xeT", [P, EXPERT_TILE])
        hid = sb("hid", [P, FC, EXPERT_TILE])
        idx_next = sb("idx_next", [P, 2], U32)
        idx_now = [sb(f"idx_now{h}", [P, 1], U32) for h in range(2)]
        ye = [sb(f"ye{h}", [P, D]) for h in range(2)]
        first = sb("first", [P, NTOK // P, D])
        second = sb("second", [P, NTOK // P, D])

        ps = ctx.enter_context(nc.psum_tensor("ps", [P, 8, BANK], F32))
        S_BANK, V_BANK, PT_BANK, O_BANK, Z_BANK, N_BANK = 0, 2, 3, 4, 5, 7
        VALUES_BANKS = (V_BANK, O_BANK)
        ROUTER_BANK, ROWS_BANK = PT_BANK, S_BANK + 1
        HID_BANKS = (0, 1, 5, 6)

        names = """cst_in small_in rows_in attn_in x_in0 x_in1 x_in2 ew_in noise_a noise_step w_noise
            bias_ready posb bf_ready run0 tail_ready qkT_p qkTs
            embed_p gpre_ready up_ready clip_ready exp_ready num_ready den_ready log_ready rec_ready fac_step
            gu_ready gnu_ready mT_ready w3_p ln1_step ln1_ln ln1_guess xn_ready xnT_p xnT_ready
            z_p z_out s_p v_p vs_ready soft_max soft_sub soft_sum soft_rec e_ready prob_ready pt_p probT_ready pv_p
            o_ready wo_p h1_ready hh_ready hy_ready ln2_step ln2_ln ln2_guess send_step send_ready hft_p hfT_ready
            lg_p route_step route_exp rank_p slot_ready scattered
            count_p count_step start_ready tail_out fill_p fill_step xe_in ring_free xe_ready xet_p xeT_ready hid_p
            hid_ready y_p ye_ready idx_step idx_ready0 idx_ready1 y_out0 y_out1 ye_free0 ye_free1 fin_in0 fin_in1 fin_in2 fin_in3 mix_step out_done passed""".split()
        s = {n: sem(n) for n in names}

        def wait(eng, name, g, per=1, k=0):
            if isinstance(g, int) and g < 0:
                return
            eng.wait_ge(s[name], g * per + k + 1)

        LN1, LN2, ROUTE = 9, 11, 19

        def counts(eng, e):
            if e == 0:
                eng.wait_ge(s["count_step"], 8)
            c = eng.value_load(table[0:1, EXPERTS + e:EXPERTS + e + 1], min_val=1, max_val=EXPERTS)
            t = eng.value_load(table[0:1, 2 * EXPERTS + e:2 * EXPERTS + e + 1], min_val=0, max_val=3 * EXPERTS)
            return c, t

        def apart(eng):
            eng.sem_inc(s["passed"])

        def g_is_last(g):
            return isinstance(g, int) and g == GROUPS - 1

        FIRST_STEP, LOOP_FROM, LOOP_TO, LAST_STEP = -3, 2, GROUPS - 3, GROUPS

        def has(g):
            return not isinstance(g, int) or 0 <= g < GROUPS

        def all_steps(eng, step):
            for g in range(FIRST_STEP, LOOP_FROM):
                step(g)
            with eng.Fori(LOOP_FROM, LOOP_TO) as g:
                step(g)
            for g in range(LOOP_TO, LAST_STEP + 1):
                step(g)

        def h_at(g):
            return h_all[:, g, :, :] if isinstance(g, int) else \
                h_all[:].rearrange("p g i d -> p (g i) d")[:, bass.ds(g * TILES, TILES), :]

        def h_tile(g, i):
            return h_all[:, g, i, :] if isinstance(g, int) else \
                h_all[:].rearrange("p g i d -> p (g i d)")[:, bass.ds(g * (TILES * D) + i * D, D)]

        def ring_at(j):
            return ring[:].rearrange("p j h c -> p (j h) c")[:, bass.ds((j % 2) * 2, 2), :]

        def z_src(q):
            return ps[:, Z_BANK + (q + 1) % 2, :].rearrange("p (h b t) -> p h b t", h=2, b=IPG)

        def z_dst(q):
            return zs[:, :, 2 * q:2 * q + 2, :].rearrange("p b h t -> p h b t")

        block = ctx.enter_context(nc.Block())

        @block.sync
        def _(sp):
            sp.dma_start(sm[:], small).then_inc(s["small_in"], 16)
            sp.dma_start(row[:], rows.partition_broadcast(P)).then_inc(s["rows_in"], 16)
            sp.dma_start(at[:].rearrange("p a b c -> p (a b c)"), attn).then_inc(s["attn_in"], 16)
            sp.wait_ge(s["x_in2"], 16)
            sp.dma_start(ew1[:].rearrange("p e f -> p (e f)"), E_W1).then_inc(s["ew_in"], 16)
            sp.dma_start(ew2[:].rearrange("p e c d -> p (e c d)"), E_W2).then_inc(s["ew_in"], 16)

            sp.wait_ge(s["fill_step"], 1)
            sp.wait_ge(s["tail_ready"], 2)
            for e in range(EXPERTS):
                n = sp.value_load(fill[0:1, e:e + 1], min_val=0, max_val=NTOK)
                dst = rows_dram[bass.ds(n + e * REGION, TAIL), :]
                sp.dma_start(dst.rearrange("(p r) c -> p r c", r=TAIL_R), tail[:, e, :, :])\
                    .then_inc(s["tail_out"], 16)

            def load_step(j, at_row):
                sp.wait_ge(s["ring_free"], j + 1)
                apart(sp)
                sp.dma_start(ring_at(j), rows_dram[bass.ds(at_row, EXPERT_TILE), :].rearrange("(h p) c -> p h c", p=P))\
                    .then_inc(s["xe_in"], 16)
                sp.wait_ge(s["xe_in"], (j + 1) * 16)
                apart(sp)

            sp.wait_ge(s["scattered"], 16 * GROUPS * 2 * TILES)
            for e in range(EXPERTS):
                c, t = counts(sp, e)
                with sp.Fori(0, c) as i:
                    load_step(t + i, i * EXPERT_TILE + e * REGION)
            load_step(t + c, 0)

            for h in range(2):
                sp.wait_ge(s[f"y_out{h}"], (t + c) * 16)
            ncol = 4
            mv_ = mixed_dram[0:2 * NTOK, :].rearrange("(k t p) d -> k p t d", k=2, p=P)
            for q in range(NTOK // P // ncol):
                cols = slice(ncol * q, ncol * q + ncol)
                sp.dma_start(first[:, cols, :], mv_[0][:, cols, :]).then_inc(s[f"fin_in{q}"], 16)
                sp.dma_start(second[:, cols, :], mv_[1][:, cols, :]).then_inc(s[f"fin_in{q}"], 16)
            ov = out.rearrange("a l d -> (a l) d").rearrange("(t p) d -> p t d", p=P)
            for q in range(NTOK // P // ncol):
                cols = slice(ncol * q, ncol * q + ncol)
                sp.wait_ge(s["mix_step"], 8 * (q + 1))
                sp.dma_start(ov[:, cols, :], first[:, cols, :]).then_inc(s["out_done"], 16)
            sp.wait_ge(s["out_done"], 16 * (NTOK // P // ncol))

        @block.gpsimd
        def _(pool):
            pool.memset(ones[:], 1.0).then_inc(s["bf_ready"], 1)
            pool.memset(run[:], 0.0).then_inc(s["run0"], 1)
            pool.memset(tail[:], 0.0).then_inc(s["tail_ready"], 1)
            pool.wait_ge(s["cst_in"], 16)
            pool.wait_ge(s["tail_ready"], 1)
            pool.tensor_copy(tail[:, :, :, D], cst[:, C_TAIL:C_END].rearrange("p (e r) -> p e r", e=EXPERTS))\
                .then_inc(s["tail_ready"], 1)
            pool.tensor_copy(dest[:].rearrange("p k i -> p (k i)"), cst[:, C_DEST:C_STEP])\
                .then_inc(s["send_step"], 1)
            pool.wait_ge(s["rows_in"], 16)

            def probabilities(g, i):
                wait(pool, "e_ready", g, TILES, i)
                wait(pool, "soft_rec", g, TILES, i)
                wait(pool, "pt_p", g - 1, TILES, i)
                pool.tensor_tensor(prob[:, i, :, :], sx[:, i, :, :],
                                   srec[:, i, :].unsqueeze(2).broadcast_to([P, HEADS, L]), ALU.mult)\
                    .then_inc(s["prob_ready"], 1)

            def rows_to_send(g):
                wait(pool, "hh_ready", g, TILES, 1)
                pool.tensor_tensor(hg[:], hh[:], g_row.unsqueeze(1).broadcast_to([P, TILES, D]), ALU.mult)\
                    .then_inc(s["send_step"], 1)
                if not (isinstance(g, int) and g == 0):
                    pool.wait_ge(s["scattered"], g * (32 * TILES))
                wait(pool, "hft_p", g - 1)
                pool.wait_ge(s["send_step"], g * 4 + 1)
                apart(pool)
                for k in range(2):
                    pool.tensor_copy(send[k][:, :, D], dest[:, k, :]).then_inc(s["send_step"], 1)
                pool.wait_ge(s["send_step"], g * 4 + 2)
                pool.tensor_tensor(send[0][:, :, 0:D], hg[:], b_row.unsqueeze(1).broadcast_to([P, TILES, D]),
                                   ALU.add).then_inc(s["send_ready"], 1)
                pool.wait_ge(s["send_step"], g * 4 + 4)
                apart(pool)
                pool.tensor_scalar(dest[:], dest[:], float(GROUP), None, ALU.add).then_inc(s["send_step"], 1)

            def scatter(g):
                wait(pool, "slot_ready", g)
                wait(pool, "send_ready", g, 2, 1)
                pool.wait_ge(s["send_step"], g * 4 + 5)
                apart(pool)
                if isinstance(g, int) and g == GROUPS - 1:
                    pool.wait_ge(s["tail_out"], 16 * EXPERTS)
                for k in range(2):
                    for i in range(TILES):
                        n = k * TILES + i
                        pool.indirect_dma_start(rows_dram, bass.IndirectOffsetOnAxis(ap=slot[:, n:n + 1], axis=0),
                                                send[k][:, i, :], None).then_inc(s["scattered"], 16)

            def gate_times_up(g):
                wait(pool, "up_ready", g)
                wait(pool, "gnu_ready", g - 1)
                pool.tensor_tensor(gu[:], gpre[:], up[:], ALU.mult).then_inc(s["gu_ready"], 1)

            def times_numerator(g):
                wait(pool, "num_ready", g)
                wait(pool, "gu_ready", g)
                pool.tensor_tensor(gnu[:], gnum[:], gu[:], ALU.mult).then_inc(s["gnu_ready"], 1)

            def step(g):
                if has(g):
                    probabilities(g, 0)
                if has(g + 3):
                    gate_times_up(g + 3)
                if has(g):
                    probabilities(g, 1)
                if has(g - 1):
                    rows_to_send(g - 1)
                if has(g + 3):
                    times_numerator(g + 3)
                if has(g - 1):
                    scatter(g - 1)

            all_steps(pool, step)

            for h in range(2):
                pool.nop().then_inc(s[f"ye_free{h}"], 1)
            for e in range(EXPERTS):
                c, t = counts(pool, e)
                with pool.Fori(0, c) as i:
                    for h in range(2):
                        pool.wait_ge(s[f"idx_ready{h}"], t + i + 1)
                        pool.wait_ge(s["ye_ready"], (t + i) * 2 + h + 3)
                        apart(pool)
                        pool.indirect_dma_start(
                            mixed_dram, bass.IndirectOffsetOnAxis(ap=idx_now[h][:, 0:1], axis=0),
                            ye[h][:], None).then_inc(s[f"y_out{h}"], 16)
                    for h in range(2):
                        pool.wait_ge(s[f"y_out{h}"], (t + i) * 16 + 16)
                        pool.sem_inc(s[f"ye_free{h}"])

        @block.scalar
        def _(act):
            act.dma_start(cst[:], consts).then_inc(s["cst_in"], 16)
            for n, (a, b) in enumerate(((0, GROUP), (GROUP, 4 * GROUP), (4 * GROUP, NTOK))):
                act.dma_start(xT[:, :, a:b], patches[:, :, a:b]).then_inc(s[f"x_in{n}"], 16)

            act.preload_act_table(ACT.Sqrt)
            act.wait_ge(s["small_in"], 16)
            ei_in = sm[:, T_EI:T_VEC]
            ec_in = sm[:, T_VEC + 4:T_VEC + 6]
            act.activation(ei_abs[:], ei_in, ACT.Abs).then_inc(s["noise_a"], 1)
            act.activation(ei_sgn[:], ei_in, ACT.Sign).then_inc(s["noise_a"], 1)
            act.activation(ec_abs[:], ec_in, ACT.Abs).then_inc(s["noise_a"], 1)
            act.activation(ec_sgn[:], ec_in, ACT.Sign).then_inc(s["noise_a"], 1)
            act.wait_ge(s["noise_a"], 4)
            act.activation(ei_abs[:], ei_abs[:], ACT.Sqrt).then_inc(s["noise_a"], 1)
            act.activation(ec_abs[:], ec_abs[:], ACT.Sqrt).then_inc(s["noise_a"], 1)
            act.wait_ge(s["rows_in"], 16)
            eo_in = row[:, R_EO:R_B3].rearrange("p (n h) -> p n h", n=2)
            act.activation(eo_abs[:], eo_in, ACT.Abs).then_inc(s["noise_a"], 1)
            act.activation(eo_sgn[:], eo_in, ACT.Sign).then_inc(s["noise_a"], 1)
            act.wait_ge(s["noise_a"], 8)
            act.activation(eo_abs[:], eo_abs[:], ACT.Sqrt).then_inc(s["noise_a"], 1)
            act.preload_act_table_set("natural_log_exp_and_others")
            act.wait_ge(s["qkT_p"], 1)
            for par in range(2):
                act.activation(qkT[:, par::2, :], ps[:, 2 + par, :].rearrange("p (a d) -> p a d", d=D), ACT.Copy,
                               scale=HD ** -0.5).then_inc(s["qkTs"], 1)

            def linears_out(g):
                wait(act, "embed_p", g)
                wait(act, "gu_ready", g - 1)
                act.activation(gpre[:], ps[:, Z_BANK, 0:GROUP], ACT.Identity, bias=bias_tok[:, 0:1])\
                    .then_inc(s["gpre_ready"], 1)
                act.activation(up[:], ps[:, Z_BANK, GROUP:2 * GROUP], ACT.Identity, bias=bias_tok[:, 1:2])\
                    .then_inc(s["up_ready"], 1)

            def gate_exp(g):
                wait(act, "clip_ready", g)
                act.activation(gexp[:], gclip[:], ACT.Exp).then_inc(s["exp_ready"], 1)

            def gate_guess(g):
                wait(act, "den_ready", g)
                act.activation(glog[:], gden[:], ACT.Ln).then_inc(s["log_ready"], 1)
                wait(act, "log_ready", g)
                act.activation(grec[:], glog[:], ACT.Exp, scale=-1.0).then_inc(s["rec_ready"], 1)

            def norm1(g):
                wait(act, "ln1_step", g, LN1, 5)
                act.activation(ln1[:], ve1[:], ACT.Ln).then_inc(s["ln1_ln"], 1)
                wait(act, "ln1_ln", g)
                act.activation(r1[:], ln1[:], ACT.Exp, scale=-0.5).then_inc(s["ln1_guess"], 1)

            def norm1_out(g):
                wait(act, "xnT_p", g)
                wait(act, "v_p", g - 1, TILES, 1)
                act.activation(xnT[:], ps[:, N_BANK, GROUP:2 * GROUP], ACT.Copy).then_inc(s["xnT_ready"], 1)

            def z_out(g, q):
                wait(act, "z_p", g, 4, q)
                act.activation(z_dst(q), z_src(q), ACT.Copy).then_inc(s["z_out"], 1)

            def values(g, i):
                wait(act, "v_p", g, TILES, i)
                wait(act, "pv_p", g - 1, TILES, i)
                act.activation(vs[:, i].rearrange("p b a k -> p (b a k)"), ps[:, VALUES_BANKS[i], :], ACT.Copy)\
                    .then_inc(s["vs_ready"], 1)

            def expo(g, i):
                wait(act, "soft_sub", g, TILES, i)
                act.activation(sx[:, i].rearrange("p h t -> p (h t)"), sx[:, i].rearrange("p h t -> p (h t)"),
                               ACT.Exp).then_inc(s["e_ready"], 1)

            def probs_out(g, i):
                wait(act, "pt_p", g, TILES, i)
                wait(act, "pv_p", g - 1, TILES, i)
                act.activation(probT[:, i].rearrange("p a b -> p (a b)"), ps[:, PT_BANK, :], ACT.Copy)\
                    .then_inc(s["probT_ready"], 1)

            def o_out(g, i):
                wait(act, "pv_p", g, TILES, i)
                wait(act, "wo_p", g - 1)
                act.activation(oT[:, i].rearrange("p a b -> p (a b)"), ps[:, O_BANK, :], ACT.Copy)\
                    .then_inc(s["o_ready"], 1)

            def norm2(g):
                wait(act, "ln2_step", g, LN2, 5)
                act.activation(ln2[:], ve2[:], ACT.Ln).then_inc(s["ln2_ln"], 1)
                wait(act, "ln2_ln", g)
                act.activation(r2[:], ln2[:], ACT.Exp, scale=-0.5).then_inc(s["ln2_guess"], 1)

            def norm2_out(g):
                wait(act, "ln2_step", g, LN2, 10)
                wait(act, "send_step", g - 1, 4, 1)
                apart(act)
                for i in range(TILES):
                    act.activation(hh[:, i, :], h_tile(g, i), ACT.Identity, scale=rstd2[:, 1, i:i + 1],
                                   bias=shift2[:, 1, i:i + 1]).then_inc(s["hh_ready"], 1)

            def add_norm2(g):
                wait(act, "hh_ready", g, TILES, 1)
                apart(act)
                for i in range(TILES):
                    act.activation(h_tile(g, i), h_tile(g, i), ACT.Identity, scale=grow2[:, i:i + 1],
                                   bias=shift2[:, 0, i:i + 1]).then_inc(s["hy_ready"], 1)

            def send_copy(g):
                wait(act, "send_ready", g, 2, 0)
                act.activation(send[1][:, :, 0:D], send[0][:, :, 0:D], ACT.Copy).then_inc(s["send_ready"], 1)

            def hfT_out(g):
                wait(act, "hft_p", g)
                act.activation(hfT[:].rearrange("p i t -> p (i t)"), ps[:, ROWS_BANK, 0:GROUP], ACT.Copy)\
                    .then_inc(s["hfT_ready"], 1)

            def route(g):
                wait(act, "route_step", g, ROUTE, 3)
                act.activation(ediff[:], diff[:], ACT.Exp).then_inc(s["route_exp"], 1)

            def step(g):
                if has(g):
                    expo(g, 0)
                    values(g, 0)
                if has(g + 1):
                    norm1_out(g + 1)
                if has(g):
                    expo(g, 1)
                    values(g, 1)
                if has(g + 3):
                    linears_out(g + 3)
                if has(g - 1):
                    norm2(g - 1)
                if has(g):
                    probs_out(g, 0)
                if has(g + 3):
                    gate_exp(g + 3)
                if has(g + 1):
                    z_out(g + 1, 0)
                    z_out(g + 1, 1)
                if has(g - 1):
                    norm2_out(g - 1)
                if has(g + 2):
                    norm1(g + 2)
                if has(g):
                    o_out(g, 0)
                if has(g + 3):
                    gate_guess(g + 3)
                if has(g + 1):
                    z_out(g + 1, 2)
                if has(g):
                    probs_out(g, 1)
                if has(g - 1):
                    send_copy(g - 1)
                if has(g + 1):
                    z_out(g + 1, 3)
                if has(g - 1):
                    hfT_out(g - 1)
                    add_norm2(g - 1)
                if has(g):
                    o_out(g, 1)
                if has(g - 1):
                    route(g - 1)

            act.wait_ge(s["bias_ready"], 1)
            all_steps(act, step)

            act.preload_act_table(ACT.Gelu)
            for e in range(EXPERTS):
                c, t = counts(act, e)
                with act.Fori(0, c) as i:
                    for f in range(FC):
                        act.wait_ge(s["hid_p"], (t + i) * FC + f + 1)
                        act.activation(hid[:, f, :], ps[:, HID_BANKS[f], 0:EXPERT_TILE], ACT.Gelu,
                                       bias=sm[:, T_B1 + e * FC + f:T_B1 + e * FC + f + 1])\
                            .then_inc(s["hid_ready"], 1)

        @block.vector
        def _(dve):
            dve.wait_ge(s["cst_in"], 16)
            dve.tensor_copy(upper[:], cst[:, C_UPPER:C_UPPER + P]).then_inc(s["bf_ready"], 1)
            dve.wait_ge(s["noise_a"], 6)
            dve.tensor_tensor(ei[:], ei_abs[:], ei_sgn[:], ALU.mult).then_inc(s["noise_step"], 1)
            dve.tensor_tensor(ec[:], ec_abs[:], ec_sgn[:], ALU.mult).then_inc(s["noise_step"], 1)
            dve.wait_ge(s["noise_step"], 2)
            dve.tensor_tensor(bias_t[:], sm[:, T_VEC + 2:T_VEC + 4], ec[:], ALU.mult).then_inc(s["noise_step"], 1)
            dve.wait_ge(s["rows_in"], 16)
            dve.tensor_tensor(pos_b3[:], cst[:, C_POS:C_POS + D], row[:, R_B3:R_G], ALU.add).then_inc(s["posb"], 1)
            dve.wait_ge(s["noise_step"], 3)
            dve.tensor_tensor(bias_tok[:], bias_t[:], sm[:, T_VEC:T_VEC + 2], ALU.add).then_inc(s["bias_ready"], 1)
            dve.wait_ge(s["noise_a"], 9)
            dve.tensor_tensor(eo[:], eo_abs[:], eo_sgn[:], ALU.mult).then_inc(s["noise_step"], 1)
            dve.wait_ge(s["noise_step"], 4)
            for n in range(2):
                for k in range(2):
                    dve.tensor_scalar(noise[:, n, k, :], eo[:, n, :], ei[:, 2 * n + k:2 * n + k + 1], None, ALU.mult)\
                        .then_inc(s["noise_step"], 1)
            dve.wait_ge(s["noise_step"], 8)
            dve.tensor_tensor(noise[:], noise[:], sw_tokT, ALU.mult).then_inc(s["noise_step"], 1)
            dve.wait_ge(s["noise_step"], 9)
            dve.tensor_tensor(w_tokT, w_tokT, noise[:], ALU.add).then_inc(s["w_noise"], 1)
            dve.wait_ge(s["run0"], 1)

            def newton(name, g, per, k, ve, r, n, to):
                dve.scalar_tensor_tensor(n, r, -0.5, r, ALU.mult, ALU.mult).then_inc(s[name], 1)
                wait(dve, name, g, per, k)
                dve.tensor_tensor(n, n, ve, ALU.mult).then_inc(s[name], 1)
                wait(dve, name, g, per, k + 1)
                dve.scalar_tensor_tensor(to, n, 1.5, r, ALU.add, ALU.mult).then_inc(s[name], 1)
                wait(dve, name, g, per, k + 2)

            def gate_clip(g):
                wait(dve, "gpre_ready", g)
                dve.tensor_scalar(gclip[:], gpre[:], 20.0, None, ALU.min).then_inc(s["clip_ready"], 1)

            def gate_fraction(g):
                wait(dve, "exp_ready", g)
                dve.scalar_tensor_tensor(gnum[:], gexp[:], 2.0, gexp[:], ALU.add, ALU.mult).then_inc(s["num_ready"], 1)
                wait(dve, "num_ready", g)
                dve.tensor_scalar(gden[:], gnum[:], 2.0, None, ALU.add).then_inc(s["den_ready"], 1)

            def gated(g):
                wait(dve, "rec_ready", g)
                dve.scalar_tensor_tensor(gleft[:], gden[:], -1.0, grec[:], ALU.mult, ALU.mult)\
                    .then_inc(s["fac_step"], 1)
                wait(dve, "fac_step", g, 2, 0)
                dve.scalar_tensor_tensor(gfac[:], gleft[:], 2.0, grec[:], ALU.add, ALU.mult)\
                    .then_inc(s["fac_step"], 1)
                wait(dve, "fac_step", g, 2, 1)
                wait(dve, "gnu_ready", g)
                wait(dve, "w3_p", g - 1)
                dve.tensor_tensor(mT[:], gfac[:], gnu[:], ALU.mult).then_inc(s["mT_ready"], 1)

            def token_norm(g):
                wait(dve, "w3_p", g)
                if isinstance(g, int) and g == 0:
                    dve.wait_ge(s["posb"], 1)
                h0 = h_at(g)
                dve.tensor_tensor(h0, ps[:, N_BANK, 0:GROUP].rearrange("p (i d) -> p i d", i=TILES),
                                  pos_b3[:].unsqueeze(1).broadcast_to([P, TILES, D]), ALU.add)\
                    .then_inc(s["ln1_step"], 1)
                wait(dve, "ln1_step", g, LN1, 0)
                for i in range(TILES):
                    dve.bn_stats(st1[:, i, :], h_tile(g, i)).then_inc(s["ln1_step"], 1)
                for i in range(TILES):
                    wait(dve, "ln1_step", g, LN1, 1 + i)
                    apart(dve)
                    dve.bn_aggr(mv1[:, i, :], st1[:, i, :]).then_inc(s["ln1_step"], 1)
                wait(dve, "ln1_step", g, LN1, 4)
                dve.tensor_scalar(ve1[:], mv1[:, :, 1], EPS, None, ALU.add).then_inc(s["ln1_step"], 1)

            def token_norm_out(g):
                wait(dve, "ln1_guess", g)
                newton("ln1_step", g, LN1, 6, ve1[:], r1[:], n1[:], rstd1[:])
                wait(dve, "xnT_p", g - 1)
                for i in range(TILES):
                    ins = dve.tensor_scalar(xn[:, i, :], h_tile(g, i), mv1[:, i, 0:1], rstd1[:, i:i + 1],
                                            ALU.subtract, ALU.mult)
                    ins.then_inc(s["xn_ready"], 1)

            def soft_a(g, i):
                wait(dve, "s_p", g, TILES, i)
                sc = ps[:, S_BANK + i, :].rearrange("p (h t) -> p h t", h=HEADS)
                dve.tensor_reduce(smax[:, i, :], sc, AX_X, ALU.max).then_inc(s["soft_max"], 1)
                wait(dve, "soft_max", g, TILES, i)
                wait(dve, "prob_ready", g - 1, TILES, i)
                dve.tensor_tensor(sx[:, i], sc, smax[:, i, :].unsqueeze(2).broadcast_to([P, HEADS, L]),
                                  ALU.subtract).then_inc(s["soft_sub"], 1)

            def soft_b(g, i):
                wait(dve, "e_ready", g, TILES, i)
                dve.tensor_reduce(ssum[:, i, :], sx[:, i], AX_X, ALU.add).then_inc(s["soft_sum"], 1)
                wait(dve, "soft_sum", g, TILES, i)
                dve.reciprocal(srec[:, i, :], ssum[:, i, :]).then_inc(s["soft_rec"], 1)

            def residual(g):
                wait(dve, "wo_p", g)
                h = h_at(g)
                dve.tensor_tensor(h, ps[:, V_BANK, 0:GROUP].rearrange("p (i d) -> p i d", i=TILES), h, ALU.add)\
                    .then_inc(s["h1_ready"], 1)

            def norm2_a(g):
                wait(dve, "h1_ready", g)
                for i in range(TILES):
                    dve.bn_stats(st2[:, i, :], h_tile(g, i)).then_inc(s["ln2_step"], 1)
                for i in range(TILES):
                    wait(dve, "ln2_step", g, LN2, i)
                    apart(dve)
                    dve.bn_aggr(mv2[:, i, :], st2[:, i, :]).then_inc(s["ln2_step"], 1)
                wait(dve, "ln2_step", g, LN2, 3)
                dve.tensor_scalar(ve2[:, 0, :], mv2[:, :, 1], EPS, None, ALU.add).then_inc(s["ln2_step"], 1)
                wait(dve, "ln2_step", g, LN2, 4)
                dve.scalar_tensor_tensor(ve2[:, 1, :], ve2[:, 0, :], EPS, mv2[:, :, 1], ALU.mult, ALU.add)\
                    .then_inc(s["ln2_step"], 1)

            def norm2_b(g):
                wait(dve, "ln2_guess", g)
                wait(dve, "hy_ready", g - 1, TILES, 1)
                newton("ln2_step", g, LN2, 6, ve2[:], r2[:], n2[:], rstd2[:])
                dve.scalar_tensor_tensor(shift2[:], rstd2[:], -1.0, mv2[:, :, 0].unsqueeze(1).broadcast_to([P, 2, TILES]),
                                         ALU.mult, ALU.mult).then_inc(s["ln2_step"], 1)
                dve.tensor_scalar(grow2[:], rstd2[:, 0, :], 1.0, None, ALU.add).then_inc(s["ln2_step"], 1)

            def route_a(g):
                def done(k):
                    wait(dve, "route_step", g, ROUTE, k)

                wait(dve, "lg_p", g)
                dve.tensor_tensor(lg[:], ps[:, ROUTER_BANK, 0:TILES * EXPERTS].rearrange("p (i e) -> p i e", i=TILES),
                                  br_row.unsqueeze(1).broadcast_to([P, TILES, EXPERTS]), ALU.add)\
                    .then_inc(s["route_step"], 1)
                done(0)
                apart(dve)
                for i in range(TILES):
                    dve.max(top[:, i, :], lg[:, i, :]).then_inc(s["route_step"], 1)
                done(2)
                dve.tensor_tensor(diff[:], top[:, :, 1], top[:, :, 0], ALU.subtract).then_inc(s["route_step"], 1)
                for i in range(TILES):
                    dve.max_index(topi[:, i, :], top[:, i, :], lg[:, i, :]).then_inc(s["route_step"], 1)
                done(5)
                dve.tensor_copy(topf[:], topi[:, :, 0:2]).then_inc(s["route_step"], 1)
                done(6)
                iota = cst[:, C_IOTA:C_EBASE].rearrange("p (i e) -> p i e", i=TILES)
                for k in range(2):
                    dve.tensor_tensor(onehot[:, k], iota, topf[:, :, k].unsqueeze(2).broadcast_to([P, TILES, EXPERTS]),
                                      ALU.is_equal).then_inc(s["route_step"], 1)
                wait(dve, "rank_p", g - 1)
                dve.tensor_copy(run[:, 0, :], run[:, TILES, :]).then_inc(s["route_step"], 1)
                done(8)
                dve.tensor_tensor(picks[:], onehot[:, 0], onehot[:, 1], ALU.add).then_inc(s["route_step"], 1)
                for i in range(TILES):
                    done(10 + i)
                    dve.tensor_tensor(run[:, i + 1, :], run[:, i, :], picks[:, i, :], ALU.add)\
                        .then_inc(s["route_step"], 1)

            def route_b(g):
                def done(k):
                    wait(dve, "route_step", g, ROUTE, k)

                wait(dve, "route_exp", g)
                dve.tensor_scalar(eone[:], ediff[:], 1.0, None, ALU.add).then_inc(s["route_step"], 1)
                done(13)
                dve.reciprocal(gate_at(g, 0), eone[:]).then_inc(s["route_step"], 1)
                wait(dve, "rank_p", g)
                dve.tensor_tensor(slot8[:], ps[:, ROUTER_BANK, 32:32 + TILES * EXPERTS].rearrange("p (i e) -> p i e", i=TILES),
                                  cst[:, C_EBASE:C_DEST].rearrange("p (i e) -> p i e", i=TILES), ALU.add)\
                    .then_inc(s["route_step"], 1)
                done(14)
                dve.tensor_tensor(gate_at(g, 1), gate_at(g, 0), ediff[:], ALU.mult).then_inc(s["route_step"], 1)
                done(15)
                dve.tensor_tensor(slotk[:], onehot[:], slot8[:].unsqueeze(1).broadcast_to([P, 2, TILES, EXPERTS]),
                                  ALU.mult).then_inc(s["route_step"], 1)
                done(17)
                dve.tensor_reduce(slotf[:], slotk[:], AX_X, ALU.add).then_inc(s["route_step"], 1)
                done(18)
                if not (isinstance(g, int) and g == 0):
                    dve.wait_ge(s["scattered"], g * (32 * TILES))
                dve.tensor_copy(slot[:], slotf[:].rearrange("p k i -> p (k i)")).then_inc(s["slot_ready"], 1)

            def gate_at(g, k):
                return gates[:, g, k, :] if isinstance(g, int) else \
                    gates[:].rearrange("p g k i -> p (g k i)")[:, bass.ds(g * (2 * TILES) + k * TILES, TILES)]

            def step(g):
                if has(g):
                    soft_a(g, 0)
                    soft_a(g, 1)
                    soft_b(g, 0)
                if has(g - 1):
                    norm2_a(g - 1)
                if has(g):
                    soft_b(g, 1)
                if has(g + 3):
                    gate_clip(g + 3)
                if has(g - 1):
                    norm2_b(g - 1)
                if has(g + 2):
                    token_norm(g + 2)
                if has(g + 3):
                    gate_fraction(g + 3)
                if has(g + 2):
                    token_norm_out(g + 2)
                if has(g + 3):
                    gated(g + 3)
                if has(g - 1):
                    route_a(g - 1)
                if has(g):
                    residual(g)
                if has(g - 1):
                    route_b(g - 1)
                if g_is_last(g):
                    dve.wait_ge(s["fill_p"], 1)
                    dve.tensor_copy(fill[:], ps[:, ROUTER_BANK, 64:64 + EXPERTS]).then_inc(s["fill_step"], 1)

            all_steps(dve, step)

            def step_done(k):
                dve.wait_ge(s["count_step"], k)

            dve.wait_ge(s["count_p"], 1)
            dve.tensor_copy(cnt[:], ps[:, ROUTER_BANK, 64:64 + EXPERTS]).then_inc(s["count_step"], 1)
            step_done(1)
            dve.tensor_copy(table[:, 0:EXPERTS], cnt[:]).then_inc(s["count_step"], 1)
            dve.tensor_tensor(over[:], cnt[:].unsqueeze(2).broadcast_to([P, EXPERTS, EXPERTS]),
                              cst[:, C_STEP:C_LOWER].unsqueeze(1).broadcast_to([P, EXPERTS, EXPERTS]), ALU.is_gt)\
                .then_inc(s["count_step"], 1)
            step_done(3)
            dve.tensor_reduce(steps[:], over[:], AX_X, ALU.add).then_inc(s["count_step"], 1)
            step_done(4)
            dve.tensor_scalar(steps[:], steps[:], 1.0, None, ALU.max).then_inc(s["count_step"], 1)
            step_done(5)
            dve.tensor_tensor(before[:], steps[:].unsqueeze(1).broadcast_to([P, EXPERTS, EXPERTS]),
                              cst[:, C_LOWER:C_TAIL].rearrange("p (a b) -> p a b", a=EXPERTS), ALU.mult)\
                .then_inc(s["count_step"], 1)
            dve.tensor_copy(table[:, EXPERTS:2 * EXPERTS], steps[:]).then_inc(s["count_step"], 1)
            step_done(7)
            dve.tensor_reduce(start_f[:], before[:], AX_X, ALU.add).then_inc(s["start_ready"], 1)
            dve.wait_ge(s["start_ready"], 1)
            dve.tensor_copy(table[:, 2 * EXPERTS:], start_f[:]).then_inc(s["count_step"], 1)

            dve.nop().then_inc(s["ring_free"], 2)
            dve.nop().then_inc(s["ye_ready"], 2)

            def fetch(j):
                dve.wait_ge(s["xe_in"], (j + 1) * 16)
                src = ring_at(j)
                dve.tensor_copy(xe[0][:], src[:, 0, :]).then_inc(s["xe_ready"], 1)
                dve.tensor_copy(xe[1][:], src[:, 1, :]).then_inc(s["ring_free"], 1)

            def turned(j):
                dve.wait_ge(s["xet_p"], j + 1)
                dve.tensor_copy(xeT[:], ps[:, 2, 0:EXPERT_TILE]).then_inc(s["xeT_ready"], 1)

            fetch(0)
            turned(0)
            for e in range(EXPERTS):
                c, t = counts(dve, e)
                with dve.Fori(0, c) as i:
                    j = t + i
                    dve.wait_ge(s["xe_ready"], j + 1)
                    dve.tensor_copy(idx_next[:, 0:1], xe[0][:, D:D + 1]).then_inc(s["idx_step"], 1)
                    dve.wait_ge(s["ring_free"], j + 3)
                    dve.tensor_copy(idx_next[:, 1:2], xe[1][:, D:D + 1]).then_inc(s["idx_step"], 1)
                    dve.wait_ge(s["idx_step"], j * 2 + 2)
                    fetch(j + 1)
                    dve.wait_ge(s["hid_p"], j * FC + FC)
                    turned(j + 1)
                    for h in range(2):
                        dve.wait_ge(s[f"ye_free{h}"], j + 1)
                        dve.tensor_copy(idx_now[h][:], idx_next[:, h:h + 1]).then_inc(s[f"idx_ready{h}"], 1)
                    for h in range(2):
                        dve.wait_ge(s["y_p"], j * 2 + h + 1)
                        dve.tensor_tensor(ye[h][:], ps[:, 3 + h, 0:D], b2_row[:, e, :], ALU.add)\
                            .then_inc(s["ye_ready"], 1)
                    for h in range(2):
                        dve.wait_ge(s[f"idx_ready{h}"], j + 1)

            dve.wait_ge(s["hy_ready"], GROUPS * TILES)
            dve.wait_ge(s["route_step"], GROUPS * ROUTE)
            hy = h_all[:].rearrange("p g i d -> p (g i) d")
            for t in range(NTOK // P):
                g, i = t // TILES, t % TILES
                dve.wait_ge(s[f"fin_in{t // 4}"], 32)
                dve.scalar_tensor_tensor(first[:, t, :], first[:, t, :], gates[:, g, 0, i:i + 1], hy[:, t, :],
                                         ALU.mult, ALU.add).then_inc(s["mix_step"], 1)
                if t % 4 == 3:
                    for u in range(t - 3, t + 1):
                        g, i = u // TILES, u % TILES
                        dve.wait_ge(s["mix_step"], 8 * (t // 4) + u % 4 + 1)
                        dve.scalar_tensor_tensor(first[:, u, :], second[:, u, :], gates[:, g, 1, i:i + 1],
                                                 first[:, u, :], ALU.mult, ALU.add).then_inc(s["mix_step"], 1)

        @block.tensor
        def _(pe):
            pe.wait_ge(s["cst_in"], 16)
            pe.wait_ge(s["attn_in"], 16)
            for h in range(HEADS):
                a, par = h // 2, h % 2
                r = slice(par * HD, par * HD + HD)
                last = pe.matmul(ps[:, 2 + par, a * D:(a + 1) * D], wkT[r, a, :], wqT[r, a, :], start=True, stop=True)
            last.then_inc(s["qkT_p"], 1)

            def embed(g):
                if isinstance(g, int) and g <= 1:
                    pe.wait_ge(s[f"x_in{g}"], 16)
                    pe.wait_ge(s["w_noise"], 1)
                if isinstance(g, int) and g == 4:
                    pe.wait_ge(s["x_in2"], 16)
                if isinstance(g, int) and g <= 2:
                    wait(pe, "up_ready", g - 1)
                else:
                    wait(pe, "z_out", g - 3, 4, 3)
                for n in range(2):
                    for k in range(2):
                        last = pe.matmul(ps[:, Z_BANK, n * GROUP:(n + 1) * GROUP], w_tokT[:, n, k, :], xT_at(g, k),
                                         start=(k == 0), stop=(k == 1))
                last.then_inc(s["embed_p"], 1)

            def xT_at(g, k):
                return xT[:, k, g * GROUP:(g + 1) * GROUP] if isinstance(g, int) else \
                    xT[:].rearrange("p k t -> p (k t)")[:, bass.ds(g * GROUP + k * NTOK, GROUP)]

            def project(g):
                wait(pe, "mT_ready", g)
                wait(pe, "xnT_ready", g - 1)
                for i in range(TILES):
                    last = pe.matmul(ps[:, N_BANK, i * D:(i + 1) * D], mT[:, i * P:(i + 1) * P], w3T,
                                     start=True, stop=True)
                last.then_inc(s["w3_p"], 1)

            def turn_norm(g):
                for i in range(TILES):
                    wait(pe, "xn_ready", g, TILES, i)
                    last = pe.transpose(ps[:, N_BANK, GROUP + i * P:GROUP + (i + 1) * P], xn[:, i, :], ident)
                last.then_inc(s["xnT_p"], 1)

            def z(g, q):
                wait(pe, "xnT_ready", g)
                if isinstance(g, int) and g == 0:
                    pe.wait_ge(s["qkTs"], 2)
                if q == 0:
                    wait(pe, "z_out", g - 1, 4, 2)
                elif q == 1 and has(g + 2):
                    wait(pe, "up_ready", g + 2)
                elif q == 1:
                    wait(pe, "z_out", g - 1, 4, 3)
                else:
                    wait(pe, "z_out", g, 4, q - 2)
                for k in range(2):
                    last = pe.matmul(ps[:, Z_BANK + (q + 1) % 2, k * GROUP:(k + 1) * GROUP], qkT[:, 2 * q + k, :],
                                     xnT[:], start=True, stop=True)
                last.then_inc(s["z_p"], 1)

            def scores(g, i):
                wait(pe, "z_out", g, 4, 3)
                wait(pe, "soft_sub", g - 1, TILES, i)
                if i == 1:
                    wait(pe, "hfT_ready", g - 2)
                for b in range(IPT):
                    n = i * IPT + b
                    last = pe.matmul(ps[b * L:(b + 1) * L, S_BANK + i, :], xnT[:, n * L:(n + 1) * L],
                                     zs[:, n].rearrange("p h t -> p (h t)"), start=True, stop=True)
                last.then_inc(s["s_p"], 1)

            def values(g, i):
                if i == 0:
                    wait(pe, "h1_ready", g - 1)
                else:
                    wait(pe, "o_ready", g - 1, TILES, 1)
                for b in range(IPT):
                    n = i * IPT + b
                    for par in range(2):
                        last = pe.matmul(ps[par * HD:(par + 1) * HD, VALUES_BANKS[i], b * GROUP:(b + 1) * GROUP],
                                         xnT[:, n * L:(n + 1) * L], wv[:, par, :], start=True, stop=True)
                last.then_inc(s["v_p"], 1)

            def turn_probs(g, i):
                wait(pe, "prob_ready", g, TILES, i)
                if i == 0:
                    wait(pe, "probT_ready", g - 1, TILES, 1)
                    wait(pe, "route_step", g - 2, ROUTE, 15)
                else:
                    wait(pe, "probT_ready", g, TILES, 0)
                for a in range(PAIRS):
                    last = pe.transpose(ps[:, PT_BANK, a * P:(a + 1) * P],
                                        prob[:, i, 2 * a:2 * a + 2, :].rearrange("p h t -> p (h t)"), ident)
                last.then_inc(s["pt_p"], 1)

            def attend(g, i):
                wait(pe, "probT_ready", g, TILES, i)
                wait(pe, "vs_ready", g, TILES, 1)
                if i == 1:
                    wait(pe, "o_ready", g, TILES, 0)
                apart(pe)
                for a in range(PAIRS):
                    for b in range(IPT):
                        for par in range(2):
                            r = slice(par * HD, par * HD + HD)
                            last = pe.matmul(ps[r, O_BANK, a * P + b * L:a * P + (b + 1) * L], vs[r, i, b, a, :],
                                             probT[r, i, a, b * L:(b + 1) * L], start=True, stop=True)
                last.then_inc(s["pv_p"], 1)

            def out_project(g):
                for i in range(TILES):
                    wait(pe, "o_ready", g, TILES, i)
                    for a in range(PAIRS):
                        last = pe.matmul(ps[:, V_BANK, i * D:(i + 1) * D], oT[:, i, a, :], wo[:, a, :],
                                         start=(a == 0), stop=(a == PAIRS - 1))
                last.then_inc(s["wo_p"], 1)

            def turn_rows(g):
                wait(pe, "send_ready", g, 2, 0)
                if not g_is_last(g):
                    wait(pe, "soft_sub", g + 1, TILES, 1)
                for i in range(TILES):
                    last = pe.transpose(ps[:, ROWS_BANK, i * P:(i + 1) * P], send[0][:, i, 0:D], ident)
                last.then_inc(s["hft_p"], 1)

            def logits(g):
                wait(pe, "hfT_ready", g)
                if g_is_last(g):
                    pe.wait_ge(s["fill_step"], 1)
                else:
                    wait(pe, "probT_ready", g + 1, TILES, 1)
                for i in range(TILES):
                    last = pe.matmul(ps[:, ROUTER_BANK, i * EXPERTS:(i + 1) * EXPERTS], hfT[:, i, :],
                                     wrT, start=True, stop=True)
                last.then_inc(s["lg_p"], 1)

            def ranks(g):
                wait(pe, "route_step", g, ROUTE, 12)
                if isinstance(g, int) and g == 0:
                    pe.wait_ge(s["bf_ready"], 2)
                o = ps[:, ROUTER_BANK, 32:32 + TILES * EXPERTS]
                pe.matmul(o, upper[:], picks[:].rearrange("p i e -> p (i e)"), start=True, stop=False)
                pe.matmul(o, ones[:], run[:, 0:TILES, :].rearrange("p i e -> p (i e)"), start=False, stop=True)\
                    .then_inc(s["rank_p"], 1)

            def count(g, signal):
                wait(pe, "route_step", g, ROUTE, 15)
                pe.matmul(ps[:, ROUTER_BANK, 64:64 + EXPERTS], ones[:], run[:, TILES, :], start=True, stop=True)\
                    .then_inc(s[signal], 1)

            def step(g):
                if has(g):
                    scores(g, 0)
                    scores(g, 1)
                    values(g, 0)
                    values(g, 1)
                if has(g + 3):
                    embed(g + 3)
                if has(g + 2):
                    project(g + 2)
                if has(g):
                    turn_probs(g, 0)
                if has(g + 1):
                    z(g + 1, 0)
                    z(g + 1, 1)
                if has(g):
                    attend(g, 0)
                if has(g + 1):
                    z(g + 1, 2)
                if has(g):
                    turn_probs(g, 1)
                if has(g + 1):
                    z(g + 1, 3)
                if has(g - 1):
                    turn_rows(g - 1)
                if has(g):
                    attend(g, 1)
                if has(g - 1):
                    logits(g - 1)
                if has(g + 2):
                    turn_norm(g + 2)
                if has(g):
                    out_project(g)
                if has(g - 1):
                    ranks(g - 1)
                if g_is_last(g):
                    count(g - 1, "fill_p")

            all_steps(pe, step)
            count(GROUPS - 1, "count_p")

            pe.wait_ge(s["ew_in"], 32)
            pe.wait_ge(s["count_step"], 8)

            def turn(j):
                pe.wait_ge(s["xe_ready"], j + 1)
                pe.transpose(ps[:, 2, 0:P], xe[0][:, 0:D], ident)
                pe.wait_ge(s["ring_free"], j + 3)
                pe.transpose(ps[:, 2, P:2 * P], xe[1][:, 0:D], ident).then_inc(s["xet_p"], 1)

            turn(0)
            for e in range(EXPERTS):
                c, t = counts(pe, e)
                with pe.Fori(0, c) as i:
                    j = t + i
                    pe.wait_ge(s["xeT_ready"], j + 1)
                    for f in range(FC):
                        pe.matmul(ps[:, HID_BANKS[f], 0:EXPERT_TILE],
                                  ew1[:, e, f * P:(f + 1) * P], xeT[:], start=True, stop=True)\
                            .then_inc(s["hid_p"], 1)
                    turn(j + 1)
                    for f in range(FC):
                        pe.wait_ge(s["hid_ready"], j * FC + f + 1)
                        if f == 0:
                            pe.wait_ge(s["ye_ready"], j * 2 + 2)
                        for h in range(2):
                            last = pe.matmul(ps[:, 3 + h, 0:D], hid[:, f, h * P:(h + 1) * P], ew2[:, e, f, :],
                                             start=(f == 0), stop=(f == FC - 1))
                            if f == FC - 1:
                                last.then_inc(s["y_p"], 1)


def _laid_out(i):
    import numpy as np

    def t(name):
        return np.asarray(i[name])

    def cols(v, n):
        return v.reshape(n, P).T

    tok, ffn = "L0_tok_", "L0_ffn_"
    patches = t("x").reshape(IMAGES, SIDE // PATCH, PATCH, SIDE // PATCH, PATCH).transpose(2, 4, 0, 1, 3)
    patches = patches.reshape(2, P, NTOK).transpose(1, 0, 2)

    def linear(w):
        return t(tok + w).T.reshape(2, P, P).transpose(1, 0, 2).reshape(P, 2 * P)

    small = np.concatenate(
        [linear("W1_w"), linear("W2_w"), linear("W1_sw"), linear("W2_sw"),
         cols(t(tok + "eps_in1"), 2), cols(t(tok + "eps_in2"), 2)]
        + [cols(t(tok + n), 1) for n in ("W1_b", "W2_b", "W1_sb", "W2_sb", "eps_out1", "eps_out2")]
        + [t(tok + "W3_w").T, t(ffn + "w_r").T, cols(t(ffn + "b1").reshape(-1), EXPERTS * FC)], axis=1)
    rows = np.concatenate([t(tok + "eps_out1"), t(tok + "eps_out2"), t(tok + "W3_b"), t(ffn + "ln_g"),
                           t(ffn + "ln_b"), t(ffn + "b_r"), t(ffn + "b2").reshape(-1)])
    k = t("L0_attn_kernel").reshape(PAIRS, 2, 3, D, HD)
    q_and_k = [k[:, :, n].transpose(1, 3, 0, 2).reshape(P, PAIRS * D) for n in range(2)]
    v = k[:, :, 2].transpose(2, 1, 0, 3).reshape(D, HEADS * HD)
    wo = t("L0_attn_head_kernel").reshape(PAIRS, P, D).transpose(1, 0, 2).reshape(P, PAIRS * D)
    attn = np.concatenate(q_and_k + [v, wo], axis=1)
    w1 = t(ffn + "W1").transpose(1, 0, 2).reshape(D, EXPERTS * HID)
    w2 = t(ffn + "W2").reshape(EXPERTS, FC, P, D).transpose(2, 0, 1, 3).reshape(P, EXPERTS * FC * D)
    return {"patches": patches, "small": small, "rows": rows, "attn": attn, "w1": w1, "w2": w2,
            "constants": constants()}


def kernel(**inputs):
    import numpy as _np
    import concourse.bacc as _bacc
    from concourse import mybir as _mybir
    from concourse.bass_utils import run_bass_kernel_spmd as _run

    nc = _bacc.Bacc("TRN2", target_bir_lowering=False, num_devices=1)
    arrays, args = {}, []
    for name, a in _laid_out(inputs).items():
        a = _np.ascontiguousarray(a)
        arrays[f"in_{name}_dram"] = a
        args.append(nc.dram_tensor(f"in_{name}_dram", a.shape, _mybir.dt.from_np(a.dtype), kind="ExternalInput").ap())
    args.append(nc.dram_tensor("out_0_dram", (IMAGES, L, D), F32, kind="ExternalOutput").ap())
    vit_tower(nc, *args)
    r = _run(nc, [arrays], core_ids=[0])
    return r.results[0]["out_0_dram"]
```

```python
from contextlib import ExitStack

import concourse.bass as bass
from concourse import mybir

F32 = mybir.dt.float32
BF16 = mybir.dt.bfloat16
I32 = mybir.dt.int32
U32 = mybir.dt.uint32
ALU = mybir.AluOpType
ACT = mybir.ActivationFunctionType
AX_X = mybir.AxisListType.X

P = 128
IMAGES, SIDE, PATCH = 32, 128, 16
L = (SIDE // PATCH) ** 2
D = 128
NTOK = IMAGES * L
HEADS, HD = 8, 64
PAIRS = HEADS // 2
EXPERTS, HID = 8, 512
FC = HID // P
GROUP = 256
GROUPS = NTOK // GROUP
TILES = GROUP // P
IPG = GROUP // L
IPT = P // L
BANK = 512
EPS = 1e-5
ROWLEN = D + 1
EXPERT_TILE = 256
TAIL = 2 * GROUP + EXPERT_TILE
REGION = NTOK + TAIL
IDLE_ROWS = EXPERTS * REGION
TAIL_ROWS = EXPERTS * TAIL

C_IDENT = 0
C_UPPER = C_IDENT + P
C_POS = C_UPPER + P
C_IOTA = C_POS + D
C_EBASE = C_IOTA + TILES * EXPERTS
C_DEST = C_EBASE + TILES * EXPERTS
C_STEP = C_DEST + 2 * TILES
C_BASE = C_STEP + EXPERTS
C_LOWER = C_BASE + EXPERTS
C_TAIL = C_LOWER + EXPERTS * EXPERTS
TAIL_R = TAIL // P
C_END = C_TAIL + EXPERTS * TAIL_R

T_W = 0
T_SW = T_W + 2 * 2 * P
T_EI = T_SW + 2 * 2 * P
T_VEC = T_EI + 4
T_W3 = T_VEC + 6
T_ROUTER = T_W3 + P
T_B1 = T_ROUTER + EXPERTS
T_END = T_B1 + EXPERTS * FC

R_EO = 0
R_B3 = R_EO + 2 * P
R_G = R_B3 + D
R_B = R_G + D
R_BR = R_B + D
R_B2 = R_BR + EXPERTS
R_END = R_B2 + EXPERTS * D


def constants():
    import math
    import numpy as np

    c = np.zeros((P, C_END), np.float32)
    p = np.arange(P)
    c[:, C_IDENT:C_IDENT + P] = np.eye(P)
    c[:, C_UPPER:C_UPPER + P] = p[:, None] < p[None, :]
    pos = np.arange(L, dtype=np.float32)[:, None]
    div = np.exp(np.arange(0, D, 2, dtype=np.float32) * np.float32(-math.log(10000.0) / D))
    angle = (pos * div).astype(np.float32)
    table = np.stack([np.sin(angle), np.cos(angle)], axis=-1).reshape(L, D)
    c[:, C_POS:C_POS + D] = np.concatenate([table] * IPT)
    c[:, C_IOTA:C_EBASE] = np.tile(np.arange(EXPERTS), TILES)
    c[:, C_EBASE:C_DEST] = np.tile(np.arange(EXPERTS) * REGION, TILES)
    for k in range(2):
        for i in range(TILES):
            c[:, C_DEST + k * TILES + i] = p + i * P + k * NTOK
    c[:, C_STEP:C_BASE] = np.arange(EXPERTS) * EXPERT_TILE
    c[:, C_BASE:C_LOWER] = np.arange(EXPERTS) * REGION - IDLE_ROWS
    c[:, C_LOWER:C_TAIL] = (np.arange(EXPERTS)[None, :] <= np.arange(EXPERTS)[:, None]).reshape(-1)
    for e in range(EXPERTS):
        for r in range(TAIL_R):
            c[:, C_TAIL + TAIL_R * e + r] = 2 * NTOK + e * TAIL + TAIL_R * p + r
    return c


def vit_tower(nc, patches, small, rows, attn, E_W1, E_W2, consts, out):
    rows_dram = nc.dram_tensor("expert_rows", [IDLE_ROWS + EXPERTS * EXPERT_TILE, ROWLEN], F32, kind="Internal").ap()
    mixed_dram = nc.dram_tensor("chosen_rows", [2 * NTOK + TAIL_ROWS, D], F32, kind="Internal").ap()

    ctx = ExitStack()
    with ctx:
        def sb(name, shape, dt=F32):
            return ctx.enter_context(nc.sbuf_tensor(name, shape, dt))

        def sem(name):
            return ctx.enter_context(nc.semaphore(name))

        cst = sb("cst", [P, C_END])
        ident = cst[:, C_IDENT:C_IDENT + P]
        upper = sb("upper", [P, P], BF16)
        ones = sb("ones", [P, P], BF16)
        sm = sb("sm", [P, T_END])
        row = sb("row", [P, R_END])
        w_tokT = sm[:, T_W:T_SW].rearrange("p (n k h) -> p n k h", n=2, k=2)
        sw_tokT = sm[:, T_SW:T_EI].rearrange("p (n k h) -> p n k h", n=2, k=2)
        w3T = sm[:, T_W3:T_ROUTER]
        wrT = sm[:, T_ROUTER:T_B1]
        g_row, b_row, br_row = row[:, R_G:R_B], row[:, R_B:R_BR], row[:, R_BR:R_B2]
        b2_row = row[:, R_B2:R_END].rearrange("p (e d) -> p e d", e=EXPERTS)
        ei_abs = sb("ei_abs", [P, 4])
        ei_sgn = sb("ei_sgn", [P, 4])
        ei = sb("ei", [P, 4])
        eo_abs = sb("eo_abs", [P, 2, P])
        eo_sgn = sb("eo_sgn", [P, 2, P])
        eo = sb("eo", [P, 2, P])
        ec_abs = sb("ec_abs", [P, 2])
        ec_sgn = sb("ec_sgn", [P, 2])
        ec = sb("ec", [P, 2])
        noise = sb("noise", [P, 2, 2, P])
        bias_t = sb("bias_t", [P, 2])
        bias_tok = sb("bias_tok", [P, 2])
        pos_b3 = sb("pos_b3", [P, D])
        at = sb("at", [P, 4, PAIRS, D])
        wqT, wkT, wo = at[:, 0], at[:, 1], at[:, 3]
        wv = at[:, 2].rearrange("p a (q k) -> p (a q k)", q=2).rearrange("p (r n) -> p r n", r=2)
        qkT = sb("qkT", [P, HEADS, D])
        ew1 = sb("ew1", [P, EXPERTS, HID])
        ew2 = sb("ew2", [P, EXPERTS, FC, D])
        tail = sb("tail", [P, EXPERTS, TAIL_R, ROWLEN])

        xT = sb("xT", [P, 2, NTOK])
        gpre = sb("gpre", [P, GROUP])
        gclip = sb("gclip", [P, GROUP])
        gexp = sb("gexp", [P, GROUP])
        gnum = sb("gnum", [P, GROUP])
        gden = sb("gden", [P, GROUP])
        glog = sb("glog", [P, GROUP])
        grec = sb("grec", [P, GROUP])
        gleft = sb("gleft", [P, GROUP])
        gfac = sb("gfac", [P, GROUP])
        up = sb("up", [P, GROUP])
        gu = sb("gu", [P, GROUP])
        gnu = sb("gnu", [P, GROUP])
        mT = sb("mT", [P, GROUP])
        h_all = sb("h_all", [P, GROUPS, TILES, D])
        st1 = sb("st1", [P, TILES, 6])
        mv1 = sb("mv1", [P, TILES, 2])
        ve1 = sb("ve1", [P, TILES])
        ln1 = sb("ln1", [P, TILES])
        r1 = sb("r1", [P, TILES])
        n1 = sb("n1", [P, TILES])
        rstd1 = sb("rstd1", [P, TILES])
        xn = sb("xn", [P, TILES, D])
        xnT = sb("xnT", [P, GROUP])
        zs = sb("zs", [P, IPG, HEADS, L])
        vs = sb("vs", [P, TILES, IPT, PAIRS, HD])
        smax = sb("smax", [P, TILES, HEADS])
        sx = sb("sx", [P, TILES, HEADS, L])
        ssum = sb("ssum", [P, TILES, HEADS])
        srec = sb("srec", [P, TILES, HEADS])
        prob = sb("prob", [P, TILES, HEADS, L])
        probT = sb("probT", [P, TILES, PAIRS, P])
        oT = sb("oT", [P, TILES, PAIRS, P])
        st2 = sb("st2", [P, TILES, 6])
        mv2 = sb("mv2", [P, TILES, 2])
        ve2 = sb("ve2", [P, 2, TILES])
        ln2 = sb("ln2", [P, 2, TILES])
        r2 = sb("r2", [P, 2, TILES])
        n2 = sb("n2", [P, 2, TILES])
        rstd2 = sb("rstd2", [P, 2, TILES])
        shift2 = sb("shift2", [P, 2, TILES])
        grow2 = sb("grow2", [P, TILES])
        hh = sb("hh", [P, TILES, D])
        hg = sb("hg", [P, TILES, D])
        dest = sb("dest", [P, 2, TILES])
        send = [sb(f"send{k}", [P, TILES, ROWLEN]) for k in range(2)]
        hfT = sb("hfT", [P, TILES, P])
        lg = sb("lg", [P, TILES, EXPERTS])
        top = sb("top", [P, TILES, 8])
        topi = sb("topi", [P, TILES, 8], U32)
        topf = sb("topf", [P, TILES, 2])
        diff = sb("diff", [P, NTOK // P])
        ediff = sb("ediff", [P, NTOK // P])
        eone = sb("eone", [P, NTOK // P])
        onehot = sb("onehot", [P, 2, TILES, EXPERTS])
        picks = sb("picks", [P, TILES, EXPERTS], BF16)
        run = sb("run", [P, TILES + 1, EXPERTS], BF16)
        slot8 = sb("slot8", [P, TILES, EXPERTS])
        slotk = sb("slotk", [P, 2, TILES, EXPERTS])
        slotf = sb("slotf", [P, 2, TILES])
        slot = sb("slot", [P, 2 * TILES], U32)
        gates = sb("gates", [P, 2, NTOK // P])

        cnt = sb("cnt", [P, 2, EXPERTS])
        over = sb("over", [P, EXPERTS, EXPERTS])
        steps = sb("steps", [P, 2, EXPERTS])
        before = sb("before", [P, EXPERTS, EXPERTS])
        rel = sb("rel", [P, EXPERTS])
        ends = sb("ends", [P, EXPERTS])
        first_rows_f = sb("first_rows_f", [P, EXPERTS])
        first_rows = sb("first_rows", [P, EXPERTS], I32)
        work_f = sb("work_f", [P, 3, EXPERTS])
        work = sb("work", [P, 3, EXPERTS], I32)
        fill = sb("fill", [P, EXPERTS], I32)
        ring = sb("ring", [P, 2, 2, ROWLEN])
        xe = [sb(f"xe{h}", [P, ROWLEN]) for h in range(2)]
        xeT = sb("xeT", [P, EXPERT_TILE])
        hid = sb("hid", [P, FC, EXPERT_TILE])
        idx_next = sb("idx_next", [P, 2], U32)
        idx_now = [sb(f"idx_now{h}", [P, 1], U32) for h in range(2)]
        ye = [sb(f"ye{h}", [P, D]) for h in range(2)]
        first = sb("first", [P, NTOK // P, D])
        second = sb("second", [P, NTOK // P, D])

        ps = ctx.enter_context(nc.psum_tensor("ps", [P, 8, BANK], F32))
        S_BANK, V_BANK, PT_BANK, O_BANK, Z_BANK, N_BANK = 0, 2, 3, 4, 5, 7
        VALUES_BANKS = (V_BANK, O_BANK)
        ROUTER_BANK, ROWS_BANK = PT_BANK, S_BANK + 1
        HID_BANKS, XET_BANK, Y_BANKS = (0, 1, 5, 6), N_BANK, (3, 4)

        names = """cst_in vec_in small_in w3_in eo_in rows_in attn_in x_in0 x_in1 x_in2 ew_in noise_a noise_step w_noise
            bias_ready posb bf_ready run0 tail_ready qkT_p qkTs
            embed_p gpre_ready up_ready clip_ready exp_ready num_ready den_ready log_ready rec_ready fac_step
            gu_ready gnu_ready mT_ready w3_p ln1_step ln1_ln ln1_guess xn_ready xnT_p xnT_ready
            z_p z_out s_p v_p vs_ready soft_max soft_sub soft_sum soft_rec e_ready prob_ready pt_p probT_ready pv_p
            o_ready wo_p h1_ready hh_ready hy_ready ln2_step ln2_ln ln2_guess send_step send_ready hft_p hfT_ready
            lg_p route_step gate_exp gate_step rank_p slot_ready scattered
            full_step rest_p rest_step rows_ready work_ready tail_out idle_out fill_p fill_step xe_in ring_free xe_ready xet_p xeT_ready hid_p
            hid_ready y_p ye_ready idx_step idx_ready0 idx_ready1 y_out0 y_out1 fin_in0 fin_in1 fin_in2 fin_in3 fin_in4 scaled mix_step mix_step_p out_done passed""".split()
        s = {n: sem(n) for n in names}

        def wait(eng, name, g, per=1, k=0):
            if isinstance(g, int) and g < 0:
                return
            eng.wait_ge(s[name], g * per + k + 1)

        LN1, LN2, ROUTE = 9, 11, 16

        def entry(eng, e, what, lo, hi):
            return eng.value_load(work[0:1, what, e:e + 1], min_val=lo, max_val=hi)

        def end_of(eng, e):
            if e == 0:
                eng.wait_ge(s["work_ready"], 1)
            return entry(eng, e, 0, EXPERTS, 6 * EXPERTS)

        def expert_steps(eng, step, between):
            ends = []

            def load(e):
                if e < EXPERTS:
                    ends.append(end_of(eng, e))

            for e in range(EXPERTS):
                step(e, e, (lambda: load(0)) if e == EXPERTS - 1 else (lambda: None))
                between(e)
            start = EXPERTS
            for e in range(EXPERTS):
                end = ends[e]
                with eng.Fori(start, end) as j:
                    step(e, j, lambda: load(e + 1))
                start = end

        def apart(eng):
            eng.sem_inc(s["passed"])

        def g_is(g, n):
            return isinstance(g, int) and g == n

        def g_is_last(g):
            return g_is(g, GROUPS - 1)

        FIRST_STEP, LOOP_FROM, LOOP_TO, LAST_STEP = -3, 2, GROUPS - 3, GROUPS - 1

        def rows_at(g):
            return V_BANK if g_is_last(g) else ROWS_BANK

        def router_at(g, col, width):
            bank, base = (V_BANK, GROUP) if g_is_last(g) else (ROUTER_BANK, 0)
            return ps[:, bank, base + col:base + col + width]

        def has(g):
            return not isinstance(g, int) or 0 <= g < GROUPS

        def all_steps(eng, step):
            for g in range(FIRST_STEP, LOOP_FROM):
                step(g)
            with eng.Fori(LOOP_FROM, LOOP_TO) as g:
                step(g)
            for g in range(LOOP_TO, LAST_STEP + 1):
                step(g)

        def h_at(g):
            return h_all[:, g, :, :] if isinstance(g, int) else \
                h_all[:].rearrange("p g i d -> p (g i) d")[:, bass.ds(g * TILES, TILES), :]

        def h_tile(g, i):
            return h_all[:, g, i, :] if isinstance(g, int) else \
                h_all[:].rearrange("p g i d -> p (g i d)")[:, bass.ds(g * (TILES * D) + i * D, D)]

        MIX_SPLIT = ((3, 1), (2, 2), (3, 1), (2, 1), (1, 0))
        CHUNKS = len(MIX_SPLIT)
        chunk_from = [sum(sum(c) for c in MIX_SPLIT[:q]) for q in range(CHUNKS + 1)]
        assert chunk_from[-1] == NTOK // P

        def chunk(q):
            return slice(chunk_from[q], chunk_from[q + 1])

        def vector_tiles(q):
            return range(chunk_from[q], chunk_from[q] + MIX_SPLIT[q][0])

        def other_tiles(q):
            return range(chunk_from[q] + MIX_SPLIT[q][0], chunk_from[q + 1])

        def mixed_before(q, part):
            return sum(c[part] for c in MIX_SPLIT[:q])

        def h_and_norm(t):
            return h_all[:, t // TILES, t % TILES, :]

        def ring_at(j):
            return ring[:].rearrange("p j h c -> p (j h) c")[:, bass.ds((j % 2) * 2, 2), :]

        def z_src(q):
            return ps[:, Z_BANK + (q + 1) % 2, :].rearrange("p (h b t) -> p h b t", h=2, b=IPG)

        def z_dst(q):
            return zs[:, :, 2 * q:2 * q + 2, :].rearrange("p b h t -> p h b t")

        block = ctx.enter_context(nc.Block())

        @block.sync
        def _(sp):
            def load_patches(n, a, b):
                sp.dma_start(xT[:, :, a:b], patches[:, :, a:b]).then_inc(s[f"x_in{n}"], 16)

            sp.dma_start(sm[:, T_EI:T_W3], small[:, T_EI:T_W3]).then_inc(s["vec_in"], 16)
            sp.dma_start(sm[:, T_W:T_EI], small[:, T_W:T_EI]).then_inc(s["small_in"], 16)
            load_patches(0, 0, GROUP)
            sp.dma_start(cst[:], consts).then_inc(s["cst_in"], 16)
            load_patches(1, GROUP, 4 * GROUP)
            sp.dma_start(sm[:, T_W3:T_END], small[:, T_W3:T_END]).then_inc(s["w3_in"], 16)
            sp.dma_start(at[:].rearrange("p a b c -> p (a b c)"), attn).then_inc(s["attn_in"], 16)
            sp.dma_start(row[:, R_B3:R_END], rows[R_B3:R_END].partition_broadcast(P)).then_inc(s["rows_in"], 16)
            load_patches(2, 4 * GROUP, NTOK)
            sp.wait_ge(s["x_in2"], 16)
            sp.dma_start(ew1[:].rearrange("p e f -> p (e f)"), E_W1).then_inc(s["ew_in"], 16)
            sp.dma_start(ew2[:].rearrange("p e c d -> p (e c d)"), E_W2).then_inc(s["ew_in"], 16)

            sp.wait_ge(s["tail_ready"], 2)
            sp.dma_start(rows_dram[IDLE_ROWS:IDLE_ROWS + EXPERT_TILE, :].rearrange("(p r) c -> p r c", p=P),
                         tail[:, 0, 0:EXPERT_TILE // P, :]).then_inc(s["idle_out"], 16)
            sp.wait_ge(s["fill_step"], 2)
            for e in range(EXPERTS):
                n = sp.value_load(fill[0:1, e:e + 1], min_val=0, max_val=NTOK)
                dst = rows_dram[bass.ds(n + e * REGION, TAIL), :]
                sp.dma_start(dst.rearrange("(p r) c -> p r c", r=TAIL_R), tail[:, e, :, :])\
                    .then_inc(s["tail_out"], 16)

            def load_step(j, at_row, load_entries):
                sp.wait_ge(s["ring_free"], j + 1)
                apart(sp)
                sp.dma_start(ring_at(j), rows_dram[bass.ds(at_row, EXPERT_TILE), :].rearrange("(h p) c -> p h c", p=P))\
                    .then_inc(s["xe_in"], 16)
                load_entries()
                sp.wait_ge(s["xe_in"], (j + 1) * 16)
                apart(sp)

            sp.wait_ge(s["idle_out"], 16)
            sp.wait_ge(s["rows_ready"], 1)
            sp.wait_ge(s["scattered"], 16 * (GROUPS - 2) * 2 * TILES)
            apart(sp)
            firsts = [sp.value_load(first_rows[0:1, e:e + 1], min_val=0, max_val=IDLE_ROWS) for e in range(2)]
            for e in range(EXPERTS):
                def load_next(e=e):
                    if e + 2 < EXPERTS:
                        firsts.append(sp.value_load(first_rows[0:1, e + 2:e + 3], min_val=0, max_val=IDLE_ROWS))

                load_step(e, firsts[e], load_next)

            def entries(e):
                return entry(sp, e, 2, 0, IDLE_ROWS), entry(sp, e, 1, 1, EXPERTS), \
                    entry(sp, e, 0, EXPERTS, 6 * EXPERTS)

            sp.wait_ge(s["work_ready"], 1)
            total, (first_row, c, end) = EXPERTS, entries(0)
            sp.wait_ge(s["scattered"], 16 * GROUPS * 2 * TILES)
            for e in range(EXPERTS):
                after = []

                def load_entries(e=e, after=after):
                    if e + 1 < EXPERTS:
                        after.extend(entries(e + 1))

                with sp.Fori(0, c) as i:
                    load_step(i + total, i * EXPERT_TILE + first_row, load_entries)
                total = end
                if after:
                    first_row, c, end = after
            load_step(total, 0, lambda: None)
            load_step(total + 1, 0, lambda: None)

            for h in range(2):
                sp.wait_ge(s[f"y_out{h}"], (total + 1) * 16)
            mv_ = mixed_dram[0:2 * NTOK, :].rearrange("(k t p) d -> k p t d", k=2, p=P)
            for q in range(CHUNKS):
                cols = chunk(q)
                sp.dma_start(first[:, cols, :], mv_[0][:, cols, :]).then_inc(s[f"fin_in{q}"], 16)
                sp.dma_start(second[:, cols, :], mv_[1][:, cols, :]).then_inc(s[f"fin_in{q}"], 16)
            ov = out.rearrange("a l d -> (a l) d").rearrange("(t p) d -> p t d", p=P)
            for q in range(CHUNKS):
                cols = chunk(q)
                sp.wait_ge(s["mix_step"], 2 * mixed_before(q + 1, 0))
                sp.wait_ge(s["mix_step_p"], 2 * mixed_before(q + 1, 1))
                sp.dma_start(ov[:, cols, :], first[:, cols, :]).then_inc(s["out_done"], 16)
            sp.wait_ge(s["out_done"], 16 * CHUNKS)

        @block.gpsimd
        def _(pool):
            pool.memset(ones[:], 1.0).then_inc(s["bf_ready"], 1)
            pool.memset(run[:], 0.0).then_inc(s["run0"], 1)
            pool.memset(tail[:], 0.0).then_inc(s["tail_ready"], 1)
            pool.wait_ge(s["cst_in"], 16)
            pool.wait_ge(s["tail_ready"], 1)
            pool.tensor_copy(tail[:, :, :, D], cst[:, C_TAIL:C_END].rearrange("p (e r) -> p e r", e=EXPERTS))\
                .then_inc(s["tail_ready"], 1)
            pool.tensor_copy(dest[:].rearrange("p k i -> p (k i)"), cst[:, C_DEST:C_STEP])\
                .then_inc(s["send_step"], 1)
            pool.wait_ge(s["tail_ready"], 2)
            for h in range(2):
                pool.dma_start(mixed_dram[2 * NTOK + h * P:2 * NTOK + (h + 1) * P, :], tail[:, 0, 0, 0:D])\
                    .then_inc(s[f"y_out{h}"], 16)

            def probabilities(g, i):
                wait(pool, "e_ready", g, TILES, i)
                wait(pool, "soft_rec", g, TILES, i)
                wait(pool, "pt_p", g - 1, TILES, i)
                pool.tensor_tensor(prob[:, i, :, :], sx[:, i, :, :],
                                   srec[:, i, :].unsqueeze(2).broadcast_to([P, HEADS, L]), ALU.mult)\
                    .then_inc(s["prob_ready"], 1)

            def rows_to_send(g):
                if g_is(g, 0):
                    pool.wait_ge(s["rows_in"], 16)
                wait(pool, "hh_ready", g, TILES, 1)
                pool.tensor_tensor(hg[:], hh[:], g_row.unsqueeze(1).broadcast_to([P, TILES, D]), ALU.mult)\
                    .then_inc(s["send_step"], 1)
                if not (isinstance(g, int) and g == 0):
                    pool.wait_ge(s["scattered"], g * (32 * TILES))
                wait(pool, "hft_p", g - 1)
                pool.wait_ge(s["send_step"], g * 4 + 1)
                apart(pool)
                for k in range(2):
                    pool.tensor_copy(send[k][:, :, D], dest[:, k, :]).then_inc(s["send_step"], 1)
                pool.wait_ge(s["send_step"], g * 4 + 2)
                pool.tensor_tensor(send[0][:, :, 0:D], hg[:], b_row.unsqueeze(1).broadcast_to([P, TILES, D]),
                                   ALU.add).then_inc(s["send_ready"], 1)
                pool.wait_ge(s["send_step"], g * 4 + 4)
                apart(pool)
                pool.tensor_scalar(dest[:], dest[:], float(GROUP), None, ALU.add).then_inc(s["send_step"], 1)

            def scatter(g):
                wait(pool, "slot_ready", g)
                wait(pool, "send_ready", g, 2, 1)
                pool.wait_ge(s["send_step"], g * 4 + 5)
                apart(pool)
                if isinstance(g, int) and g == GROUPS - 2:
                    pool.wait_ge(s["tail_out"], 16 * EXPERTS)
                for n in range(2 * TILES - 1):
                    scatter_tile(n)

            def scatter_tile(n):
                k, i = n // TILES, n % TILES
                pool.indirect_dma_start(rows_dram, bass.IndirectOffsetOnAxis(ap=slot[:, n:n + 1], axis=0),
                                        send[k][:, i, :], None).then_inc(s["scattered"], 16)

            def gate_times_up(g):
                wait(pool, "up_ready", g)
                wait(pool, "gnu_ready", g - 1)
                pool.tensor_tensor(gu[:], gpre[:], up[:], ALU.mult).then_inc(s["gu_ready"], 1)

            def times_numerator(g):
                wait(pool, "num_ready", g)
                wait(pool, "gu_ready", g)
                pool.tensor_tensor(gnu[:], gnum[:], gu[:], ALU.mult).then_inc(s["gnu_ready"], 1)

            def step(g):
                if has(g):
                    probabilities(g, 0)
                if has(g - 2):
                    scatter_tile(2 * TILES - 1)
                if has(g + 3):
                    gate_times_up(g + 3)
                if has(g):
                    probabilities(g, 1)
                if has(g - 1):
                    rows_to_send(g - 1)
                if has(g + 3):
                    times_numerator(g + 3)
                if has(g - 1):
                    scatter(g - 1)

            all_steps(pool, step)
            scatter_tile(2 * TILES - 1)

            def results(e, j, load_end):
                for h in range(2):
                    pool.wait_ge(s["ye_ready"], j * 2 + h + 3)
                    apart(pool)
                    pool.indirect_dma_start(
                        mixed_dram, bass.IndirectOffsetOnAxis(ap=idx_now[h][:, 0:1], axis=0),
                        ye[h][:], None).then_inc(s[f"y_out{h}"], 16)
                load_end()

            def last_rows(n):
                if n == 1:
                    rows_to_send(GROUPS - 1)
                if n == 3:
                    wait(pool, "slot_ready", GROUPS - 1)
                    wait(pool, "send_ready", GROUPS - 1, 2, 1)
                if n in (3, 4):
                    for tile in range(TILES):
                        scatter_tile((n - 3) * TILES + tile)

            expert_steps(pool, results, last_rows)
            pool.wait_ge(s["hy_ready"], GROUPS * TILES)
            for q in range(CHUNKS):
                for n, t in enumerate(other_tiles(q), mixed_before(q, 1)):
                    pool.wait_ge(s["scaled"], 2 * n + 2)
                    pool.tensor_tensor(first[:, t, :], first[:, t, :], h_and_norm(t), ALU.add)\
                        .then_inc(s["mix_step_p"], 1)
                    pool.wait_ge(s["mix_step_p"], 2 * n + 1)
                    pool.tensor_tensor(first[:, t, :], first[:, t, :], second[:, t, :], ALU.add)\
                        .then_inc(s["mix_step_p"], 1)

        @block.scalar
        def _(act):
            act.dma_start(row[:, R_EO:R_B3], rows[R_EO:R_B3].partition_broadcast(P)).then_inc(s["eo_in"], 16)

            act.preload_act_table(ACT.Sqrt)
            act.wait_ge(s["vec_in"], 16)
            ei_in = sm[:, T_EI:T_VEC]
            ec_in = sm[:, T_VEC + 4:T_VEC + 6]
            act.activation(ei_abs[:], ei_in, ACT.Abs).then_inc(s["noise_a"], 1)
            act.activation(ei_sgn[:], ei_in, ACT.Sign).then_inc(s["noise_a"], 1)
            act.activation(ec_abs[:], ec_in, ACT.Abs).then_inc(s["noise_a"], 1)
            act.activation(ec_sgn[:], ec_in, ACT.Sign).then_inc(s["noise_a"], 1)
            act.wait_ge(s["noise_a"], 4)
            act.activation(ei_abs[:], ei_abs[:], ACT.Sqrt).then_inc(s["noise_a"], 1)
            act.activation(ec_abs[:], ec_abs[:], ACT.Sqrt).then_inc(s["noise_a"], 1)
            act.wait_ge(s["eo_in"], 16)
            eo_in = row[:, R_EO:R_B3].rearrange("p (n h) -> p n h", n=2)
            act.activation(eo_abs[:], eo_in, ACT.Abs).then_inc(s["noise_a"], 1)
            act.activation(eo_sgn[:], eo_in, ACT.Sign).then_inc(s["noise_a"], 1)
            act.wait_ge(s["noise_a"], 8)
            act.activation(eo_abs[:], eo_abs[:], ACT.Sqrt).then_inc(s["noise_a"], 1)
            act.preload_act_table_set("natural_log_exp_and_others")

            def qk_products_out():
                act.wait_ge(s["qkT_p"], 1)
                for par in range(2):
                    act.activation(qkT[:, par::2, :], ps[:, 2 + par, :].rearrange("p (a d) -> p a d", d=D), ACT.Copy,
                                   scale=HD ** -0.5).then_inc(s["qkTs"], 1)

            def linears_out(g):
                wait(act, "embed_p", g)
                wait(act, "gu_ready", g - 1)
                act.activation(gpre[:], ps[:, Z_BANK, 0:GROUP], ACT.Identity, bias=bias_tok[:, 0:1])\
                    .then_inc(s["gpre_ready"], 1)
                act.activation(up[:], ps[:, Z_BANK, GROUP:2 * GROUP], ACT.Identity, bias=bias_tok[:, 1:2])\
                    .then_inc(s["up_ready"], 1)

            def gate_exp(g):
                wait(act, "clip_ready", g)
                act.activation(gexp[:], gclip[:], ACT.Exp).then_inc(s["exp_ready"], 1)

            def gate_guess(g):
                wait(act, "den_ready", g)
                act.activation(glog[:], gden[:], ACT.Ln).then_inc(s["log_ready"], 1)
                wait(act, "log_ready", g)
                act.activation(grec[:], glog[:], ACT.Exp, scale=-1.0).then_inc(s["rec_ready"], 1)

            def norm1(g):
                wait(act, "ln1_step", g, LN1, 5)
                act.activation(ln1[:], ve1[:], ACT.Ln).then_inc(s["ln1_ln"], 1)
                wait(act, "ln1_ln", g)
                act.activation(r1[:], ln1[:], ACT.Exp, scale=-0.5).then_inc(s["ln1_guess"], 1)

            def norm1_out(g):
                wait(act, "xnT_p", g)
                wait(act, "v_p", g - 1, TILES, 1)
                act.activation(xnT[:], ps[:, N_BANK, GROUP:2 * GROUP], ACT.Copy).then_inc(s["xnT_ready"], 1)

            def z_out(g, q):
                wait(act, "z_p", g, 4, q)
                act.activation(z_dst(q), z_src(q), ACT.Copy).then_inc(s["z_out"], 1)

            def values(g, i):
                wait(act, "v_p", g, TILES, i)
                wait(act, "pv_p", g - 1, TILES, i)
                act.activation(vs[:, i].rearrange("p b a k -> p (b a k)"), ps[:, VALUES_BANKS[i], :], ACT.Copy)\
                    .then_inc(s["vs_ready"], 1)

            def expo(g, i):
                wait(act, "soft_sub", g, TILES, i)
                act.activation(sx[:, i].rearrange("p h t -> p (h t)"), sx[:, i].rearrange("p h t -> p (h t)"),
                               ACT.Exp).then_inc(s["e_ready"], 1)

            def probs_out(g, i):
                wait(act, "pt_p", g, TILES, i)
                wait(act, "pv_p", g - 1, TILES, i)
                act.activation(probT[:, i].rearrange("p a b -> p (a b)"), ps[:, PT_BANK, :], ACT.Copy)\
                    .then_inc(s["probT_ready"], 1)

            def o_out(g, i):
                wait(act, "pv_p", g, TILES, i)
                wait(act, "wo_p", g - 1)
                act.activation(oT[:, i].rearrange("p a b -> p (a b)"), ps[:, O_BANK, :], ACT.Copy)\
                    .then_inc(s["o_ready"], 1)

            def norm2(g):
                wait(act, "ln2_step", g, LN2, 5)
                act.activation(ln2[:], ve2[:], ACT.Ln).then_inc(s["ln2_ln"], 1)
                wait(act, "ln2_ln", g)
                act.activation(r2[:], ln2[:], ACT.Exp, scale=-0.5).then_inc(s["ln2_guess"], 1)

            def norm2_out(g):
                wait(act, "ln2_step", g, LN2, 10)
                wait(act, "send_step", g - 1, 4, 1)
                apart(act)
                for i in range(TILES):
                    act.activation(hh[:, i, :], h_tile(g, i), ACT.Identity, scale=rstd2[:, 1, i:i + 1],
                                   bias=shift2[:, 1, i:i + 1]).then_inc(s["hh_ready"], 1)

            def add_norm2(g):
                wait(act, "hh_ready", g, TILES, 1)
                apart(act)
                for i in range(TILES):
                    act.activation(h_tile(g, i), h_tile(g, i), ACT.Identity, scale=grow2[:, i:i + 1],
                                   bias=shift2[:, 0, i:i + 1]).then_inc(s["hy_ready"], 1)

            def send_copy(g):
                wait(act, "send_ready", g, 2, 0)
                act.activation(send[1][:, :, 0:D], send[0][:, :, 0:D], ACT.Copy).then_inc(s["send_ready"], 1)

            def hfT_out(g):
                wait(act, "hft_p", g)
                act.activation(hfT[:].rearrange("p i t -> p (i t)"), ps[:, rows_at(g), 0:GROUP], ACT.Copy)\
                    .then_inc(s["hfT_ready"], 1)

            def step(g):
                if has(g):
                    expo(g, 0)
                    values(g, 0)
                if has(g + 1):
                    norm1_out(g + 1)
                if has(g):
                    expo(g, 1)
                    values(g, 1)
                if has(g + 3):
                    linears_out(g + 3)
                if has(g - 1):
                    norm2(g - 1)
                if has(g):
                    probs_out(g, 0)
                if has(g + 3):
                    gate_exp(g + 3)
                if has(g + 1):
                    z_out(g + 1, 0)
                    z_out(g + 1, 1)
                if has(g - 1):
                    norm2_out(g - 1)
                if has(g + 2):
                    norm1(g + 2)
                if has(g):
                    o_out(g, 0)
                if has(g + 1):
                    z_out(g + 1, 2)
                if has(g):
                    probs_out(g, 1)
                if has(g + 3):
                    gate_guess(g + 3)
                if g_is(g, FIRST_STEP + 1):
                    qk_products_out()
                if has(g - 1):
                    send_copy(g - 1)
                if has(g + 1):
                    z_out(g + 1, 3)
                if has(g - 1):
                    hfT_out(g - 1)
                    add_norm2(g - 1)
                if has(g):
                    o_out(g, 1)

            act.wait_ge(s["bias_ready"], 1)
            all_steps(act, step)

            act.preload_act_table(ACT.Gelu)
            act.wait_ge(s["w3_in"], 16)

            def hidden(e, j, load_end):
                for f in range(FC):
                    act.wait_ge(s["hid_p"], j * FC + f + 1)
                    act.activation(hid[:, f, :], ps[:, HID_BANKS[f], 0:EXPERT_TILE], ACT.Gelu,
                                   bias=sm[:, T_B1 + e * FC + f:T_B1 + e * FC + f + 1])\
                        .then_inc(s["hid_ready"], 1)
                load_end()

            def last_rows(n):
                if n == 0:
                    act.preload_act_table_set("natural_log_exp_and_others")
                    norm2(GROUPS - 1)
                    act.preload_act_table(ACT.Gelu)
                if n == 1:
                    norm2_out(GROUPS - 1)
                    add_norm2(GROUPS - 1)
                if n == 2:
                    send_copy(GROUPS - 1)
                    hfT_out(GROUPS - 1)

            expert_steps(act, hidden, last_rows)

            wait(act, "route_step", GROUPS - 1, ROUTE, 3)
            act.activation(ediff[:], diff[:], ACT.Exp).then_inc(s["gate_exp"], 1)
            act.wait_ge(s["gate_step"], 3)
            for q in range(CHUNKS):
                for t in other_tiles(q):
                    act.wait_ge(s[f"fin_in{q}"], 32)
                    for k, chosen in enumerate((first, second)):
                        act.activation(chosen[:, t, :], chosen[:, t, :], ACT.Copy, scale=gates[:, k, t:t + 1])\
                            .then_inc(s["scaled"], 1)

        @block.vector
        def _(dve):
            dve.wait_ge(s["noise_a"], 6)
            dve.tensor_tensor(ei[:], ei_abs[:], ei_sgn[:], ALU.mult).then_inc(s["noise_step"], 1)
            dve.tensor_tensor(ec[:], ec_abs[:], ec_sgn[:], ALU.mult).then_inc(s["noise_step"], 1)
            dve.wait_ge(s["noise_step"], 2)
            dve.tensor_tensor(bias_t[:], sm[:, T_VEC + 2:T_VEC + 4], ec[:], ALU.mult).then_inc(s["noise_step"], 1)
            dve.wait_ge(s["noise_step"], 3)
            dve.tensor_tensor(bias_tok[:], bias_t[:], sm[:, T_VEC:T_VEC + 2], ALU.add).then_inc(s["bias_ready"], 1)
            dve.wait_ge(s["noise_a"], 9)
            dve.tensor_tensor(eo[:], eo_abs[:], eo_sgn[:], ALU.mult).then_inc(s["noise_step"], 1)
            dve.wait_ge(s["noise_step"], 4)
            dve.wait_ge(s["small_in"], 16)
            for n in range(2):
                for k in range(2):
                    dve.scalar_tensor_tensor(noise[:, n, k, :], eo[:, n, :], ei[:, 2 * n + k:2 * n + k + 1],
                                             sw_tokT[:, n, k, :], ALU.mult, ALU.mult).then_inc(s["noise_step"], 1)
            dve.wait_ge(s["noise_step"], 8)
            dve.tensor_tensor(w_tokT, w_tokT, noise[:], ALU.add).then_inc(s["w_noise"], 1)
            dve.wait_ge(s["cst_in"], 16)
            dve.tensor_copy(upper[:], cst[:, C_UPPER:C_UPPER + P]).then_inc(s["bf_ready"], 1)
            dve.wait_ge(s["run0"], 1)

            def newton(name, g, per, k, ve, r, n, to):
                dve.scalar_tensor_tensor(n, r, -0.5, r, ALU.mult, ALU.mult).then_inc(s[name], 1)
                wait(dve, name, g, per, k)
                dve.tensor_tensor(n, n, ve, ALU.mult).then_inc(s[name], 1)
                wait(dve, name, g, per, k + 1)
                dve.scalar_tensor_tensor(to, n, 1.5, r, ALU.add, ALU.mult).then_inc(s[name], 1)
                wait(dve, name, g, per, k + 2)

            def gate_clip(g):
                wait(dve, "gpre_ready", g)
                dve.tensor_scalar(gclip[:], gpre[:], 20.0, None, ALU.min).then_inc(s["clip_ready"], 1)

            def gate_fraction(g):
                wait(dve, "exp_ready", g)
                dve.scalar_tensor_tensor(gnum[:], gexp[:], 2.0, gexp[:], ALU.add, ALU.mult).then_inc(s["num_ready"], 1)
                wait(dve, "num_ready", g)
                dve.tensor_scalar(gden[:], gnum[:], 2.0, None, ALU.add).then_inc(s["den_ready"], 1)

            def gated(g):
                wait(dve, "rec_ready", g)
                dve.scalar_tensor_tensor(gleft[:], gden[:], -1.0, grec[:], ALU.mult, ALU.mult)\
                    .then_inc(s["fac_step"], 1)
                wait(dve, "fac_step", g, 2, 0)
                dve.scalar_tensor_tensor(gfac[:], gleft[:], 2.0, grec[:], ALU.add, ALU.mult)\
                    .then_inc(s["fac_step"], 1)
                wait(dve, "fac_step", g, 2, 1)
                wait(dve, "gnu_ready", g)
                wait(dve, "w3_p", g - 1)
                dve.tensor_tensor(mT[:], gfac[:], gnu[:], ALU.mult).then_inc(s["mT_ready"], 1)

            def token_norm(g):
                if g_is(g, 0):
                    dve.wait_ge(s["rows_in"], 16)
                    dve.tensor_tensor(pos_b3[:], cst[:, C_POS:C_POS + D], row[:, R_B3:R_G], ALU.add)\
                        .then_inc(s["posb"], 1)
                    dve.wait_ge(s["posb"], 1)
                wait(dve, "w3_p", g)
                h0 = h_at(g)
                dve.tensor_tensor(h0, ps[:, N_BANK, 0:GROUP].rearrange("p (i d) -> p i d", i=TILES),
                                  pos_b3[:].unsqueeze(1).broadcast_to([P, TILES, D]), ALU.add)\
                    .then_inc(s["ln1_step"], 1)
                wait(dve, "ln1_step", g, LN1, 0)
                for i in range(TILES):
                    dve.bn_stats(st1[:, i, :], h_tile(g, i)).then_inc(s["ln1_step"], 1)
                for i in range(TILES):
                    wait(dve, "ln1_step", g, LN1, 1 + i)
                    apart(dve)
                    dve.bn_aggr(mv1[:, i, :], st1[:, i, :]).then_inc(s["ln1_step"], 1)
                wait(dve, "ln1_step", g, LN1, 4)
                dve.tensor_scalar(ve1[:], mv1[:, :, 1], EPS, None, ALU.add).then_inc(s["ln1_step"], 1)

            def token_norm_out(g):
                wait(dve, "ln1_guess", g)
                newton("ln1_step", g, LN1, 6, ve1[:], r1[:], n1[:], rstd1[:])
                wait(dve, "xnT_p", g - 1)
                for i in range(TILES):
                    ins = dve.tensor_scalar(xn[:, i, :], h_tile(g, i), mv1[:, i, 0:1], rstd1[:, i:i + 1],
                                            ALU.subtract, ALU.mult)
                    ins.then_inc(s["xn_ready"], 1)

            def soft_a(g, i):
                wait(dve, "s_p", g, TILES, i)
                sc = ps[:, S_BANK + i, :].rearrange("p (h t) -> p h t", h=HEADS)
                dve.tensor_reduce(smax[:, i, :], sc, AX_X, ALU.max).then_inc(s["soft_max"], 1)
                wait(dve, "soft_max", g, TILES, i)
                wait(dve, "prob_ready", g - 1, TILES, i)
                dve.tensor_tensor(sx[:, i], sc, smax[:, i, :].unsqueeze(2).broadcast_to([P, HEADS, L]),
                                  ALU.subtract).then_inc(s["soft_sub"], 1)

            def soft_b(g, i):
                wait(dve, "e_ready", g, TILES, i)
                dve.tensor_reduce(ssum[:, i, :], sx[:, i], AX_X, ALU.add).then_inc(s["soft_sum"], 1)
                wait(dve, "soft_sum", g, TILES, i)
                dve.reciprocal(srec[:, i, :], ssum[:, i, :]).then_inc(s["soft_rec"], 1)

            def residual(g):
                wait(dve, "wo_p", g)
                h = h_at(g)
                dve.tensor_tensor(h, ps[:, V_BANK, 0:GROUP].rearrange("p (i d) -> p i d", i=TILES), h, ALU.add)\
                    .then_inc(s["h1_ready"], 1)

            def norm2_a(g):
                wait(dve, "h1_ready", g)
                for i in range(TILES):
                    dve.bn_stats(st2[:, i, :], h_tile(g, i)).then_inc(s["ln2_step"], 1)
                for i in range(TILES):
                    wait(dve, "ln2_step", g, LN2, i)
                    apart(dve)
                    dve.bn_aggr(mv2[:, i, :], st2[:, i, :]).then_inc(s["ln2_step"], 1)
                wait(dve, "ln2_step", g, LN2, 3)
                dve.tensor_scalar(ve2[:, 0, :], mv2[:, :, 1], EPS, None, ALU.add).then_inc(s["ln2_step"], 1)
                wait(dve, "ln2_step", g, LN2, 4)
                dve.scalar_tensor_tensor(ve2[:, 1, :], ve2[:, 0, :], EPS, mv2[:, :, 1], ALU.mult, ALU.add)\
                    .then_inc(s["ln2_step"], 1)

            def norm2_b(g):
                wait(dve, "ln2_guess", g)
                wait(dve, "hy_ready", g - 1, TILES, 1)
                newton("ln2_step", g, LN2, 6, ve2[:], r2[:], n2[:], rstd2[:])
                dve.scalar_tensor_tensor(shift2[:], rstd2[:], -1.0, mv2[:, :, 0].unsqueeze(1).broadcast_to([P, 2, TILES]),
                                         ALU.mult, ALU.mult).then_inc(s["ln2_step"], 1)
                dve.tensor_scalar(grow2[:], rstd2[:, 0, :], 1.0, None, ALU.add).then_inc(s["ln2_step"], 1)

            def route_a(g):
                def done(k):
                    wait(dve, "route_step", g, ROUTE, k)

                wait(dve, "lg_p", g)
                dve.tensor_tensor(lg[:], router_at(g, 0, TILES * EXPERTS).rearrange("p (i e) -> p i e", i=TILES),
                                  br_row.unsqueeze(1).broadcast_to([P, TILES, EXPERTS]), ALU.add)\
                    .then_inc(s["route_step"], 1)
                done(0)
                apart(dve)
                for i in range(TILES):
                    dve.max(top[:, i, :], lg[:, i, :]).then_inc(s["route_step"], 1)
                done(2)
                dve.tensor_tensor(diff_at(g), top[:, :, 1], top[:, :, 0], ALU.subtract).then_inc(s["route_step"], 1)
                for i in range(TILES):
                    dve.max_index(topi[:, i, :], top[:, i, :], lg[:, i, :]).then_inc(s["route_step"], 1)
                done(5)
                dve.tensor_copy(topf[:], topi[:, :, 0:2]).then_inc(s["route_step"], 1)
                done(6)
                iota = cst[:, C_IOTA:C_EBASE].rearrange("p (i e) -> p i e", i=TILES)
                for k in range(2):
                    dve.tensor_tensor(onehot[:, k], iota, topf[:, :, k].unsqueeze(2).broadcast_to([P, TILES, EXPERTS]),
                                      ALU.is_equal).then_inc(s["route_step"], 1)
                wait(dve, "rank_p", g - 1)
                dve.tensor_copy(run[:, 0, :], run[:, TILES, :]).then_inc(s["route_step"], 1)
                done(8)
                dve.tensor_tensor(picks[:], onehot[:, 0], onehot[:, 1], ALU.add).then_inc(s["route_step"], 1)
                for i in range(TILES):
                    done(10 + i)
                    dve.tensor_tensor(run[:, i + 1, :], run[:, i, :], picks[:, i, :], ALU.add)\
                        .then_inc(s["route_step"], 1)

            def route_b(g):
                def done(k):
                    wait(dve, "route_step", g, ROUTE, k)

                wait(dve, "rank_p", g)
                dve.tensor_tensor(slot8[:], router_at(g, 32, TILES * EXPERTS).rearrange("p (i e) -> p i e", i=TILES),
                                  cst[:, C_EBASE:C_DEST].rearrange("p (i e) -> p i e", i=TILES), ALU.add)\
                    .then_inc(s["route_step"], 1)
                done(13)
                dve.tensor_tensor(slotk[:], onehot[:], slot8[:].unsqueeze(1).broadcast_to([P, 2, TILES, EXPERTS]),
                                  ALU.mult).then_inc(s["route_step"], 1)
                done(14)
                dve.tensor_reduce(slotf[:], slotk[:], AX_X, ALU.add).then_inc(s["route_step"], 1)
                done(15)
                if not (isinstance(g, int) and g == 0):
                    dve.wait_ge(s["scattered"], g * (32 * TILES))
                dve.tensor_copy(slot[:], slotf[:].rearrange("p k i -> p (k i)")).then_inc(s["slot_ready"], 1)

            def diff_at(g):
                return diff[:, g * TILES:(g + 1) * TILES] if isinstance(g, int) else \
                    diff[:, bass.ds(g * TILES, TILES)]

            def step(g):
                if has(g):
                    soft_a(g, 0)
                    soft_a(g, 1)
                    soft_b(g, 0)
                if has(g - 1):
                    norm2_a(g - 1)
                if has(g):
                    soft_b(g, 1)
                if has(g + 3):
                    gate_clip(g + 3)
                if has(g - 1):
                    norm2_b(g - 1)
                if has(g + 2):
                    token_norm(g + 2)
                if has(g + 3):
                    gate_fraction(g + 3)
                if has(g + 2):
                    token_norm_out(g + 2)
                if has(g + 3):
                    gated(g + 3)
                if g_is_last(g):
                    return
                if has(g - 1):
                    route_a(g - 1)
                if has(g):
                    residual(g)
                if has(g - 1):
                    route_b(g - 1)
                if isinstance(g, int) and g == GROUPS - 2:
                    dve.wait_ge(s["fill_p"], 1)
                    dve.tensor_copy(cnt[:, 0], router_at(g - 1, 64, EXPERTS)).then_inc(s["fill_step"], 1)
                    dve.wait_ge(s["fill_step"], 1)
                    dve.tensor_copy(fill[:], cnt[:, 0]).then_inc(s["fill_step"], 1)


            lower = cst[:, C_LOWER:C_TAIL].rearrange("p (a b) -> p a b", a=EXPERTS)

            def by_expert(v):
                return v.unsqueeze(1).broadcast_to([P, EXPERTS, EXPERTS])

            def full_steps():
                def done(k):
                    dve.wait_ge(s["full_step"], k)

                dve.wait_ge(s["fill_step"], 1)
                dve.tensor_scalar(steps[:, 0], cnt[:, 0], float(EXPERT_TILE), None, ALU.is_ge)\
                    .then_inc(s["full_step"], 1)
                done(1)
                dve.tensor_tensor(rel[:], steps[:, 0], cst[:, C_BASE:C_LOWER], ALU.mult).then_inc(s["full_step"], 1)
                done(2)
                dve.tensor_scalar(first_rows_f[:], rel[:], float(IDLE_ROWS), None, ALU.add)\
                    .then_inc(s["full_step"], 1)
                done(3)
                dve.tensor_copy(first_rows[:], first_rows_f[:]).then_inc(s["rows_ready"], 1)

            def rest_steps():
                def done(k):
                    dve.wait_ge(s["rest_step"], k)

                dve.wait_ge(s["rest_p"], 1)
                dve.tensor_copy(cnt[:, 1], router_at(GROUPS - 1, 64, EXPERTS)).then_inc(s["rest_step"], 1)
                done(1)
                dve.tensor_tensor(over[:], cnt[:, 1].unsqueeze(2).broadcast_to([P, EXPERTS, EXPERTS]),
                                  by_expert(cst[:, C_STEP:C_BASE]), ALU.is_gt).then_inc(s["rest_step"], 1)
                done(2)
                dve.tensor_reduce(rel[:], over[:], AX_X, ALU.add).then_inc(s["rest_step"], 1)
                done(3)
                dve.tensor_tensor(steps[:, 1], rel[:], steps[:, 0], ALU.subtract).then_inc(s["rest_step"], 1)
                done(4)
                dve.scalar_tensor_tensor(before[:], by_expert(steps[:, 1]), 1.0, lower, ALU.max, ALU.mult)\
                    .then_inc(s["rest_step"], 1)
                dve.tensor_scalar(work_f[:, 1, :], steps[:, 1], 1.0, None, ALU.max).then_inc(s["rest_step"], 1)
                dve.scalar_tensor_tensor(work_f[:, 2, :], steps[:, 0], float(EXPERT_TILE),
                                         cst[:, C_EBASE:C_EBASE + EXPERTS], ALU.mult, ALU.add)\
                    .then_inc(s["rest_step"], 1)
                done(5)
                dve.tensor_reduce(ends[:], before[:], AX_X, ALU.add).then_inc(s["rest_step"], 1)
                done(8)
                dve.tensor_scalar(work_f[:, 0, :], ends[:], float(EXPERTS), None, ALU.add)\
                    .then_inc(s["rest_step"], 1)
                done(9)
                dve.tensor_copy(work[:], work_f[:]).then_inc(s["work_ready"], 1)

            dve.nop().then_inc(s["ring_free"], 2)
            dve.nop().then_inc(s["ye_ready"], 2)

            def fetch(j):
                dve.wait_ge(s["xe_in"], (j + 1) * 16)
                src = ring_at(j)
                dve.tensor_copy(xe[0][:], src[:, 0, :]).then_inc(s["xe_ready"], 1)
                dve.tensor_copy(xe[1][:], src[:, 1, :]).then_inc(s["ring_free"], 1)

            def turned(j):
                dve.wait_ge(s["xet_p"], j + 1)
                dve.tensor_copy(xeT[:], ps[:, XET_BANK, 0:EXPERT_TILE]).then_inc(s["xeT_ready"], 1)

            def next_places(j):
                dve.wait_ge(s["xe_ready"], j + 1)
                dve.tensor_copy(idx_next[:, 0:1], xe[0][:, D:D + 1]).then_inc(s["idx_step"], 1)
                dve.wait_ge(s["ring_free"], j + 3)
                dve.tensor_copy(idx_next[:, 1:2], xe[1][:, D:D + 1]).then_inc(s["idx_step"], 1)
                dve.wait_ge(s["idx_step"], j * 2 + 2)

            all_steps(dve, step)
            full_steps()
            fetch(0)
            route_a(GROUPS - 2)
            turned(0)
            next_places(0)
            fetch(1)
            residual(GROUPS - 1)
            route_b(GROUPS - 2)
            norm2_a(GROUPS - 1)

            def results(e, j, load_end):
                dve.wait_ge(s["hid_p"], j * FC + FC)
                turned(j + 1)
                load_end()
                for h in range(2):
                    dve.wait_ge(s[f"y_out{h}"], j * 16 + 16)
                    dve.tensor_copy(idx_now[h][:], idx_next[:, h:h + 1]).then_inc(s[f"idx_ready{h}"], 1)
                    dve.wait_ge(s["y_p"], j * 2 + h + 1)
                    dve.tensor_tensor(ye[h][:], ps[:, Y_BANKS[h], 0:D], b2_row[:, e, :], ALU.add)\
                        .then_inc(s["ye_ready"], 1)
                for h in range(2):
                    dve.wait_ge(s[f"idx_ready{h}"], j + 1)
                next_places(j + 1)
                fetch(j + 2)

            def last_rows(n):
                if n == 0:
                    norm2_b(GROUPS - 1)
                if n == 2:
                    route_a(GROUPS - 1)
                if n == 3:
                    route_b(GROUPS - 1)
                if n == 4:
                    rest_steps()

            expert_steps(dve, results, last_rows)

            dve.wait_ge(s["hy_ready"], GROUPS * TILES)
            dve.wait_ge(s["gate_exp"], 1)
            dve.tensor_scalar(eone[:], ediff[:], 1.0, None, ALU.add).then_inc(s["gate_step"], 1)
            dve.wait_ge(s["gate_step"], 1)
            dve.reciprocal(gates[:, 0], eone[:]).then_inc(s["gate_step"], 1)
            dve.wait_ge(s["gate_step"], 2)
            dve.tensor_tensor(gates[:, 1], gates[:, 0], ediff[:], ALU.mult).then_inc(s["gate_step"], 1)
            dve.wait_ge(s["gate_step"], 3)
            for q in range(CHUNKS):
                tiles = vector_tiles(q)
                dve.wait_ge(s[f"fin_in{q}"], 32)
                for t in tiles:
                    dve.scalar_tensor_tensor(first[:, t, :], first[:, t, :], gates[:, 0, t:t + 1], h_and_norm(t),
                                             ALU.mult, ALU.add).then_inc(s["mix_step"], 1)
                for n, t in enumerate(tiles):
                    dve.wait_ge(s["mix_step"], 2 * mixed_before(q, 0) + n + 1)
                    dve.scalar_tensor_tensor(first[:, t, :], second[:, t, :], gates[:, 1, t:t + 1],
                                             first[:, t, :], ALU.mult, ALU.add).then_inc(s["mix_step"], 1)

        @block.tensor
        def _(pe):
            def qk_products():
                pe.wait_ge(s["attn_in"], 16)
                for h in range(HEADS):
                    a, par = h // 2, h % 2
                    r = slice(par * HD, par * HD + HD)
                    last = pe.matmul(ps[:, 2 + par, a * D:(a + 1) * D], wkT[r, a, :], wqT[r, a, :],
                                     start=True, stop=True)
                last.then_inc(s["qkT_p"], 1)

            def embed(g):
                if isinstance(g, int) and g <= 1:
                    pe.wait_ge(s[f"x_in{g}"], 16)
                    pe.wait_ge(s["w_noise"], 1)
                if isinstance(g, int) and g == 4:
                    pe.wait_ge(s["x_in2"], 16)
                if isinstance(g, int) and g <= 2:
                    wait(pe, "up_ready", g - 1)
                else:
                    wait(pe, "z_out", g - 3, 4, 3)
                for n in range(2):
                    for k in range(2):
                        last = pe.matmul(ps[:, Z_BANK, n * GROUP:(n + 1) * GROUP], w_tokT[:, n, k, :], xT_at(g, k),
                                         start=(k == 0), stop=(k == 1))
                last.then_inc(s["embed_p"], 1)

            def xT_at(g, k):
                return xT[:, k, g * GROUP:(g + 1) * GROUP] if isinstance(g, int) else \
                    xT[:].rearrange("p k t -> p (k t)")[:, bass.ds(g * GROUP + k * NTOK, GROUP)]

            def project(g):
                if g_is(g, 0):
                    pe.wait_ge(s["cst_in"], 16)
                    pe.wait_ge(s["w3_in"], 16)
                wait(pe, "mT_ready", g)
                wait(pe, "xnT_ready", g - 1)
                for i in range(TILES):
                    last = pe.matmul(ps[:, N_BANK, i * D:(i + 1) * D], mT[:, i * P:(i + 1) * P], w3T,
                                     start=True, stop=True)
                last.then_inc(s["w3_p"], 1)

            def turn_norm(g):
                for i in range(TILES):
                    wait(pe, "xn_ready", g, TILES, i)
                    last = pe.transpose(ps[:, N_BANK, GROUP + i * P:GROUP + (i + 1) * P], xn[:, i, :], ident)
                last.then_inc(s["xnT_p"], 1)

            def z(g, q):
                wait(pe, "xnT_ready", g)
                if isinstance(g, int) and g == 0:
                    pe.wait_ge(s["qkTs"], 2)
                if q == 0:
                    wait(pe, "z_out", g - 1, 4, 2)
                elif q == 1 and has(g + 2):
                    wait(pe, "up_ready", g + 2)
                elif q == 1:
                    wait(pe, "z_out", g - 1, 4, 3)
                else:
                    wait(pe, "z_out", g, 4, q - 2)
                for k in range(2):
                    last = pe.matmul(ps[:, Z_BANK + (q + 1) % 2, k * GROUP:(k + 1) * GROUP], qkT[:, 2 * q + k, :],
                                     xnT[:], start=True, stop=True)
                last.then_inc(s["z_p"], 1)

            def scores(g, i):
                wait(pe, "z_out", g, 4, 3)
                wait(pe, "soft_sub", g - 1, TILES, i)
                if i == 1:
                    wait(pe, "hfT_ready", g - 2)
                for b in range(IPT):
                    n = i * IPT + b
                    last = pe.matmul(ps[b * L:(b + 1) * L, S_BANK + i, :], xnT[:, n * L:(n + 1) * L],
                                     zs[:, n].rearrange("p h t -> p (h t)"), start=True, stop=True)
                last.then_inc(s["s_p"], 1)

            def values(g, i):
                if i == 0:
                    wait(pe, "h1_ready", g - 1)
                else:
                    wait(pe, "o_ready", g - 1, TILES, 1)
                for b in range(IPT):
                    n = i * IPT + b
                    for par in range(2):
                        last = pe.matmul(ps[par * HD:(par + 1) * HD, VALUES_BANKS[i], b * GROUP:(b + 1) * GROUP],
                                         xnT[:, n * L:(n + 1) * L], wv[:, par, :], start=True, stop=True)
                last.then_inc(s["v_p"], 1)

            def turn_probs(g, i):
                wait(pe, "prob_ready", g, TILES, i)
                if i == 0:
                    wait(pe, "probT_ready", g - 1, TILES, 1)
                    wait(pe, "route_step", g - 2, ROUTE, 13)
                    if g_is_last(g):
                        pe.wait_ge(s["fill_step"], 1)
                else:
                    wait(pe, "probT_ready", g, TILES, 0)
                for a in range(PAIRS):
                    last = pe.transpose(ps[:, PT_BANK, a * P:(a + 1) * P],
                                        prob[:, i, 2 * a:2 * a + 2, :].rearrange("p h t -> p (h t)"), ident)
                last.then_inc(s["pt_p"], 1)

            def attend(g, i):
                wait(pe, "probT_ready", g, TILES, i)
                wait(pe, "vs_ready", g, TILES, 1)
                if i == 1:
                    wait(pe, "o_ready", g, TILES, 0)
                apart(pe)
                for a in range(PAIRS):
                    for b in range(IPT):
                        for par in range(2):
                            r = slice(par * HD, par * HD + HD)
                            last = pe.matmul(ps[r, O_BANK, a * P + b * L:a * P + (b + 1) * L], vs[r, i, b, a, :],
                                             probT[r, i, a, b * L:(b + 1) * L], start=True, stop=True)
                last.then_inc(s["pv_p"], 1)

            def out_project(g):
                for i in range(TILES):
                    wait(pe, "o_ready", g, TILES, i)
                    for a in range(PAIRS):
                        last = pe.matmul(ps[:, V_BANK, i * D:(i + 1) * D], oT[:, i, a, :], wo[:, a, :],
                                         start=(a == 0), stop=(a == PAIRS - 1))
                last.then_inc(s["wo_p"], 1)

            def turn_rows(g):
                wait(pe, "send_ready", g, 2, 0)
                if g_is_last(g):
                    wait(pe, "h1_ready", g)
                else:
                    wait(pe, "soft_sub", g + 1, TILES, 1)
                for i in range(TILES):
                    last = pe.transpose(ps[:, rows_at(g), i * P:(i + 1) * P], send[0][:, i, 0:D], ident)
                last.then_inc(s["hft_p"], 1)

            def logits(g):
                wait(pe, "hfT_ready", g)
                if not g_is_last(g):
                    wait(pe, "probT_ready", g + 1, TILES, 1)
                for i in range(TILES):
                    last = pe.matmul(router_at(g, i * EXPERTS, EXPERTS), hfT[:, i, :],
                                     wrT, start=True, stop=True)
                last.then_inc(s["lg_p"], 1)

            def ranks(g):
                wait(pe, "route_step", g, ROUTE, 12)
                if isinstance(g, int) and g == 0:
                    pe.wait_ge(s["bf_ready"], 2)
                o = router_at(g, 32, TILES * EXPERTS)
                pe.matmul(o, upper[:], picks[:].rearrange("p i e -> p (i e)"), start=True, stop=False)
                pe.matmul(o, ones[:], run[:, 0:TILES, :].rearrange("p i e -> p (i e)"), start=False, stop=True)\
                    .then_inc(s["rank_p"], 1)

            def count(g, signal):
                wait(pe, "route_step", g, ROUTE, 13)
                pe.matmul(router_at(g, 64, EXPERTS), ones[:], run[:, TILES, :], start=True, stop=True)\
                    .then_inc(s[signal], 1)

            def step(g):
                if has(g):
                    scores(g, 0)
                    scores(g, 1)
                    values(g, 0)
                    values(g, 1)
                if has(g + 3):
                    embed(g + 3)
                if has(g + 2):
                    project(g + 2)
                if g_is(g, FIRST_STEP + 1):
                    qk_products()
                if has(g):
                    turn_probs(g, 0)
                if has(g + 1):
                    z(g + 1, 0)
                    z(g + 1, 1)
                if has(g):
                    attend(g, 0)
                if has(g + 1):
                    z(g + 1, 2)
                if has(g):
                    turn_probs(g, 1)
                if has(g + 1):
                    z(g + 1, 3)
                if has(g - 1):
                    turn_rows(g - 1)
                if has(g):
                    attend(g, 1)
                if has(g - 1):
                    logits(g - 1)
                if has(g + 2):
                    turn_norm(g + 2)
                if g_is_last(g):
                    return
                if has(g):
                    out_project(g)
                if has(g - 1):
                    ranks(g - 1)
                if isinstance(g, int) and g == GROUPS - 2:
                    count(g - 1, "fill_p")

            all_steps(pe, step)

            def turn(j):
                pe.wait_ge(s["xe_ready"], j + 1)
                pe.transpose(ps[:, XET_BANK, 0:P], xe[0][:, 0:D], ident)
                pe.wait_ge(s["ring_free"], j + 3)
                pe.transpose(ps[:, XET_BANK, P:2 * P], xe[1][:, 0:D], ident).then_inc(s["xet_p"], 1)

            turn(0)
            out_project(GROUPS - 1)
            ranks(GROUPS - 2)
            pe.wait_ge(s["ew_in"], 32)

            def expert(e, j, load_end):
                load_end()
                pe.wait_ge(s["xeT_ready"], j + 1)
                for f in range(FC):
                    pe.matmul(ps[:, HID_BANKS[f], 0:EXPERT_TILE],
                              ew1[:, e, f * P:(f + 1) * P], xeT[:], start=True, stop=True)\
                        .then_inc(s["hid_p"], 1)
                turn(j + 1)
                for f in range(FC):
                    pe.wait_ge(s["hid_ready"], j * FC + f + 1)
                    if f == 0:
                        pe.wait_ge(s["ye_ready"], j * 2 + 2)
                    if f == 0 and g_is(j, 0):
                        wait(pe, "route_step", GROUPS - 2, ROUTE, 13)
                    for h in range(2):
                        last = pe.matmul(ps[:, Y_BANKS[h], 0:D], hid[:, f, h * P:(h + 1) * P], ew2[:, e, f, :],
                                         start=(f == 0), stop=(f == FC - 1))
                        if f == FC - 1:
                            last.then_inc(s["y_p"], 1)

            def last_rows(n):
                if n == 2:
                    turn_rows(GROUPS - 1)
                    logits(GROUPS - 1)
                if n == 3:
                    ranks(GROUPS - 1)
                if n == 4:
                    count(GROUPS - 1, "rest_p")

            expert_steps(pe, expert, last_rows)


def _laid_out(i):
    import numpy as np

    def t(name):
        return np.asarray(i[name])

    def cols(v, n):
        return v.reshape(n, P).T

    tok, ffn = "L0_tok_", "L0_ffn_"
    patches = t("x").reshape(IMAGES, SIDE // PATCH, PATCH, SIDE // PATCH, PATCH).transpose(2, 4, 0, 1, 3)
    patches = patches.reshape(2, P, NTOK).transpose(1, 0, 2)

    def linear(w):
        return t(tok + w).T.reshape(2, P, P).transpose(1, 0, 2).reshape(P, 2 * P)

    small = np.concatenate(
        [linear("W1_w"), linear("W2_w"), linear("W1_sw"), linear("W2_sw"),
         cols(t(tok + "eps_in1"), 2), cols(t(tok + "eps_in2"), 2)]
        + [cols(t(tok + n), 1) for n in ("W1_b", "W2_b", "W1_sb", "W2_sb", "eps_out1", "eps_out2")]
        + [t(tok + "W3_w").T, t(ffn + "w_r").T, cols(t(ffn + "b1").reshape(-1), EXPERTS * FC)], axis=1)
    rows = np.concatenate([t(tok + "eps_out1"), t(tok + "eps_out2"), t(tok + "W3_b"), t(ffn + "ln_g"),
                           t(ffn + "ln_b"), t(ffn + "b_r"), t(ffn + "b2").reshape(-1)])
    k = t("L0_attn_kernel").reshape(PAIRS, 2, 3, D, HD)
    q_and_k = [k[:, :, n].transpose(1, 3, 0, 2).reshape(P, PAIRS * D) for n in range(2)]
    v = k[:, :, 2].transpose(2, 1, 0, 3).reshape(D, HEADS * HD)
    wo = t("L0_attn_head_kernel").reshape(PAIRS, P, D).transpose(1, 0, 2).reshape(P, PAIRS * D)
    attn = np.concatenate(q_and_k + [v, wo], axis=1)
    w1 = t(ffn + "W1").transpose(1, 0, 2).reshape(D, EXPERTS * HID)
    w2 = t(ffn + "W2").reshape(EXPERTS, FC, P, D).transpose(2, 0, 1, 3).reshape(P, EXPERTS * FC * D)
    return {"patches": patches, "small": small, "rows": rows, "attn": attn, "w1": w1, "w2": w2,
            "constants": constants()}


def kernel(**inputs):
    import numpy as _np
    import concourse.bacc as _bacc
    from concourse import mybir as _mybir
    from concourse.bass_utils import run_bass_kernel_spmd as _run

    nc = _bacc.Bacc("TRN2", target_bir_lowering=False, num_devices=1)
    arrays, args = {}, []
    for name, a in _laid_out(inputs).items():
        a = _np.ascontiguousarray(a)
        arrays[f"in_{name}_dram"] = a
        args.append(nc.dram_tensor(f"in_{name}_dram", a.shape, _mybir.dt.from_np(a.dtype), kind="ExternalInput").ap())
    args.append(nc.dram_tensor("out_0_dram", (IMAGES, L, D), F32, kind="ExternalOutput").ap())
    vit_tower(nc, *args)
    r = _run(nc, [arrays], core_ids=[0])
    return r.results[0]["out_0_dram"]
```
